# Optimizing a Trainium2 kernel written in Bass

```python
import numpy as np
import jax
import jax.numpy as jnp

def _softmax(x, axis=-1):
    return jax.nn.softmax(x, axis=axis)

def _gelu(x):
    return jax.nn.gelu(x, approximate=True)

def _silu(x):
    return jax.nn.silu(x)

def _sigmoid(x):
    return jax.nn.sigmoid(x)

def _layernorm(x, axis=-1, eps=1e-05):
    m = jnp.mean(x, axis=axis, keepdims=True)
    v = jnp.var(x, axis=axis, keepdims=True)
    return (x - m) / jnp.sqrt(v + eps)

def _scatter_add(tgt, idx, src, axis=0):
    return tgt.at[idx].add(src)

def _segment_sum(src, seg, n):
    return jax.ops.segment_sum(src, seg, n)
kernel_name = 'mk_gnn_ffn_d4_gnn_r16_3dbe13'

def setup_inputs(seed: int=0):
    np.random.seed(seed)
    _w = jnp.asarray

    def _rec_inputs():
        import jax
        import jax.numpy as jnp
        _gk = jax.random.key(seed)
        x = -0.0003713 + 1 * jax.random.normal(jax.random.fold_in(_gk, 1), (3125, 256), jnp.float32)
        src = jax.random.randint(jax.random.fold_in(_gk, 2), (50000,), 0, 3125, jnp.int32)
        dst = jax.random.randint(jax.random.fold_in(_gk, 3), (50000,), 0, 3125, jnp.int32)
        _o = jnp.argsort(dst, stable=True)
        src = src[_o]
        dst = dst[_o]
        edge_attr_3 = -1.09012e-05 + 0.99985 * jax.random.normal(jax.random.fold_in(_gk, 12), (50000, 3), jnp.float32)
        return (x, src, dst, edge_attr_3)
    x, src, dst, edge_attr_3 = _rec_inputs()

    def _L0_gnn_setup():
        import jax, jax.numpy as jnp
        import numpy as np
        N = 3125
        E = 100000
        D = 256
        H = 256
        EPS = 1e-05

        def _gnn_layer(x, row, col, W, b, g, beta):
            n = x.shape[0]
            neigh = x[col]
            agg = jax.ops.segment_sum(neigh, row, num_segments=n)
            deg = jax.ops.segment_sum(jnp.ones((row.shape[0],), x.dtype), row, num_segments=n)
            deg = jnp.maximum(deg, 1.0)[:, None]
            h = (x + agg / deg) @ W.T + b
            mu = jnp.mean(h, axis=-1, keepdims=True)
            var = jnp.mean(jnp.square(h - mu), axis=-1, keepdims=True)
            hn = (h - mu) * jax.lax.rsqrt(var + EPS) * g + beta
            return jax.nn.silu(hn)
        key = jax.random.key(seed)
        ks = jax.random.split(key, 12)
        x = jax.random.normal(ks[0], (N, D), dtype=jnp.float32)
        edge_index = jax.random.randint(ks[1], (2, E), 0, N, dtype=jnp.int32)
        s0 = 1.0 / np.sqrt(D)
        s1 = 1.0 / np.sqrt(H)
        W0 = jax.random.uniform(ks[2], (H, D), jnp.float32, -s0, s0)
        b0 = jax.random.uniform(ks[3], (H,), jnp.float32, -s0, s0)
        g0 = jnp.ones((H,), jnp.float32)
        beta0 = jnp.zeros((H,), jnp.float32)
        W1 = jax.random.uniform(ks[4], (H, H), jnp.float32, -s1, s1)
        b1 = jax.random.uniform(ks[5], (H,), jnp.float32, -s1, s1)
        g1 = jnp.ones((H,), jnp.float32)
        beta1 = jnp.zeros((H,), jnp.float32)
        return {'x': x, 'edge_index': edge_index, 'W0': W0, 'b0': b0, 'g0': g0, 'beta0': beta0, 'W1': W1, 'b1': b1, 'g1': g1, 'beta1': beta1}
    _L0_gnn_all = _L0_gnn_setup()
    _L0_gnn_in = {k: v for k, v in _L0_gnn_all.items() if k in ('W0', 'b0', 'g0', 'beta0', 'W1', 'b1', 'g1', 'beta1')}
    del _L0_gnn_all

    def _L0_ffn_setup():
        import math
        import jax, jax.numpy as jnp
        import numpy as np
        CAPACITY_FACTOR = 1.25
        key = jax.random.key(seed)
        ks = jax.random.split(key, 5)
        B, L, D, F, E = (8, 512, 256, 1024, 8)
        h = jax.random.normal(ks[0], (B, L, D), dtype=jnp.float32)
        gate_w = jax.random.normal(ks[1], (D, E), dtype=jnp.float32) * 0.02
        gate_b = jnp.zeros((E,), dtype=jnp.float32)
        w1 = jax.random.normal(ks[2], (E, D, F), dtype=jnp.float32) * (1.0 / math.sqrt(D))
        b1 = jnp.zeros((E, F), dtype=jnp.float32)
        w2 = jax.random.normal(ks[3], (E, F, D), dtype=jnp.float32) * (1.0 / math.sqrt(F))
        b2 = jnp.zeros((E, D), dtype=jnp.float32)
        return {'h': h, 'gate_w': gate_w, 'gate_b': gate_b, 'w1': w1, 'b1': b1, 'w2': w2, 'b2': b2}
    _L0_ffn_all = _L0_ffn_setup()
    _L0_ffn_in = {k: v for k, v in _L0_ffn_all.items() if k in ('gate_w', 'gate_b', 'w1', 'b1', 'w2', 'b2')}
    del _L0_ffn_all

    def _L1_gnn_setup():
        import jax, jax.numpy as jnp
        import numpy as np
        N_NODES = 3125
        N_EDGES = 50000
        IN_C, EMB, OUT_C = (256, 512, 256)
        BN_EPS = 1e-05

        def _gcn_norm(src, dst, n):
            loop = jnp.arange(n, dtype=src.dtype)
            s = jnp.concatenate([src, loop])
            d = jnp.concatenate([dst, loop])
            deg = jax.ops.segment_sum(jnp.ones_like(d, dtype=jnp.float32), d, num_segments=n)
            dinv = jnp.where(deg > 0, jax.lax.rsqrt(deg), 0.0)
            return (s, d, dinv[s] * dinv[d])

        def _gcn_conv(x, W, b, s, d, norm, n):
            h = x @ W
            msg = h[s] * norm[:, None]
            agg = jax.ops.segment_sum(msg, d, num_segments=n)
            return agg + b

        def _bn_relu(x, g, be):
            mu = jnp.mean(x, axis=0)
            var = jnp.mean(jnp.square(x - mu), axis=0)
            y = (x - mu) * jax.lax.rsqrt(var + BN_EPS) * g + be
            return jax.nn.relu(y)
        key = jax.random.key(seed)
        ks = jax.random.split(key, 8)
        node_feat = jax.random.normal(ks[0], (N_NODES, IN_C), dtype=jnp.float32)
        src = jax.random.randint(ks[1], (N_EDGES,), 0, N_NODES, dtype=jnp.int64 if jax.config.jax_enable_x64 else jnp.int32)
        dst = jax.random.randint(ks[2], (N_EDGES,), 0, N_NODES, dtype=jnp.int64 if jax.config.jax_enable_x64 else jnp.int32)
        W1 = jax.random.normal(ks[3], (IN_C, EMB), dtype=jnp.float32) * (1.0 / np.sqrt(IN_C))
        b1 = jnp.zeros((EMB,), dtype=jnp.float32)
        W2 = jax.random.normal(ks[4], (EMB, EMB), dtype=jnp.float32) * (1.0 / np.sqrt(EMB))
        b2 = jnp.zeros((EMB,), dtype=jnp.float32)
        W3 = jax.random.normal(ks[5], (EMB, OUT_C), dtype=jnp.float32) * (1.0 / np.sqrt(EMB))
        b3 = jnp.zeros((OUT_C,), dtype=jnp.float32)
        g1 = jnp.ones((EMB,), dtype=jnp.float32)
        be1 = jnp.zeros((EMB,), dtype=jnp.float32)
        g2 = jnp.ones((EMB,), dtype=jnp.float32)
        be2 = jnp.zeros((EMB,), dtype=jnp.float32)
        return {'node_feat': node_feat, 'W1': W1, 'b1': b1, 'g1': g1, 'be1': be1, 'W2': W2, 'b2': b2, 'g2': g2, 'be2': be2, 'W3': W3, 'b3': b3, 'src': src, 'dst': dst}
    _L1_gnn_all = _L1_gnn_setup()
    _L1_gnn_in = {k: v for k, v in _L1_gnn_all.items() if k in ('W1', 'b1', 'g1', 'be1', 'W2', 'b2', 'g2', 'be2', 'W3', 'b3')}
    del _L1_gnn_all

    def _L1_ffn_setup():
        import jax, jax.numpy as jnp
        import numpy as np
        D_MODEL = 256
        EXPERT_DIM = 512
        NUM_EXPERTS = 8
        TOP_K = 2
        SEQ_LEN = 128
        BATCH = 2
        key = jax.random.key(seed)
        ks = jax.random.split(key, 8)
        s = 0.02
        x = jax.random.normal(ks[0], (SEQ_LEN, BATCH, D_MODEL), dtype=jnp.float32)
        Wg = jax.random.normal(ks[1], (D_MODEL, NUM_EXPERTS), dtype=jnp.float32) * s
        bg = jax.random.normal(ks[2], (NUM_EXPERTS,), dtype=jnp.float32) * s
        bias = jnp.zeros((NUM_EXPERTS,), dtype=jnp.float32)
        W1 = jax.random.normal(ks[3], (NUM_EXPERTS, D_MODEL, EXPERT_DIM), dtype=jnp.float32) * s
        b1 = jax.random.normal(ks[4], (NUM_EXPERTS, EXPERT_DIM), dtype=jnp.float32) * s
        W2 = jax.random.normal(ks[5], (NUM_EXPERTS, EXPERT_DIM, D_MODEL), dtype=jnp.float32) * s
        b2 = jax.random.normal(ks[6], (NUM_EXPERTS, D_MODEL), dtype=jnp.float32) * s
        return {'x': x, 'Wg': Wg, 'bg': bg, 'bias': bias, 'W1': W1, 'b1': b1, 'W2': W2, 'b2': b2}
    _L1_ffn_all = _L1_ffn_setup()
    _L1_ffn_in = {k: v for k, v in _L1_ffn_all.items() if k in ('Wg', 'bg', 'bias', 'W1', 'b1', 'W2', 'b2')}
    del _L1_ffn_all

    def _L2_gnn_setup():
        import jax, jax.numpy as jnp
        import numpy as np
        N = 3125
        E = 25000
        IN = 256
        H = 8
        D = 32
        EF = 3
        key = jax.random.key(seed)
        ks = jax.random.split(key, 8)
        x = jax.random.normal(ks[0], (N, IN), dtype=jnp.float32)
        edge_index = jax.random.randint(ks[1], (2, E), 0, N, dtype=jnp.int64)
        edge_attr = jax.random.normal(ks[2], (E, EF), dtype=jnp.float32)
        W = jax.random.normal(ks[3], (H * D, IN), dtype=jnp.float32) * np.float32(np.sqrt(2.0 / (IN + H * D)))
        a_src = jax.random.normal(ks[4], (H, D), dtype=jnp.float32) * np.float32(np.sqrt(2.0 / (H + D)))
        a_dst = jax.random.normal(ks[5], (H, D), dtype=jnp.float32) * np.float32(np.sqrt(2.0 / (H + D)))
        edge_W = jax.random.normal(ks[6], (H * D, EF), dtype=jnp.float32) * np.float32(np.sqrt(2.0 / (EF + H * D)))
        edge_b = jnp.zeros((H * D,), dtype=jnp.float32)
        bias = jnp.zeros((H * D,), dtype=jnp.float32)
        return {'x': x, 'W': W, 'a_src': a_src, 'a_dst': a_dst, 'edge_W': edge_W, 'edge_b': edge_b, 'bias': bias, 'edge_attr': edge_attr, 'edge_index': edge_index}
    _L2_gnn_all = _L2_gnn_setup()
    _L2_gnn_in = {k: v for k, v in _L2_gnn_all.items() if k in ('W', 'a_src', 'a_dst', 'edge_W', 'edge_b', 'bias')}
    del _L2_gnn_all

    def _L2_ffn_setup():
        import jax, jax.numpy as jnp
        import numpy as np
        BN_EPS = 0.001

        def _bn(h, g, b, m, v):
            return g * (h - m) * jax.lax.rsqrt(v + BN_EPS) + b
        key = jax.random.key(seed)
        ks = jax.random.split(key, 8)
        B, F, Df = (256, 64, 256)
        E, H, D = (8, 256, 256)
        s1 = 1.0 / np.sqrt(Df)
        s2 = 1.0 / np.sqrt(H)
        return {'x': jax.random.normal(ks[0], (B, F, Df), jnp.float32), 'Wr': jax.random.normal(ks[1], (Df, E), jnp.float32) * s1, 'br': jnp.zeros((E,), jnp.float32), 'W1': jax.random.normal(ks[2], (E, Df, H), jnp.float32) * s1, 'b1': jnp.zeros((E, H), jnp.float32), 'g1': jnp.ones((E, H), jnp.float32), 'be1': jnp.zeros((E, H), jnp.float32), 'm1': jnp.zeros((E, H), jnp.float32), 'v1': jnp.ones((E, H), jnp.float32), 'W2': jax.random.normal(ks[3], (E, H, H), jnp.float32) * s2, 'b2': jnp.zeros((E, H), jnp.float32), 'g2': jnp.ones((E, H), jnp.float32), 'be2': jnp.zeros((E, H), jnp.float32), 'm2': jnp.zeros((E, H), jnp.float32), 'v2': jnp.ones((E, H), jnp.float32), 'Wo': jax.random.normal(ks[4], (E, H, D), jnp.float32) * s2, 'bo': jnp.zeros((E, D), jnp.float32)}
    _L2_ffn_all = _L2_ffn_setup()
    _L2_ffn_in = {k: v for k, v in _L2_ffn_all.items() if k in ('Wr', 'br', 'W1', 'b1', 'g1', 'be1', 'm1', 'v1', 'W2', 'b2', 'g2', 'be2', 'm2', 'v2', 'Wo', 'bo')}
    del _L2_ffn_all

    def _L3_gnn_setup():
        import jax, jax.numpy as jnp
        import numpy as np
        HEADS = 4
        OUT_CH = 64
        NEG_SLOPE = 0.2
        key = jax.random.key(seed)
        k1, k2, k3, k4, k5 = jax.random.split(key, 5)
        N, E, IN = (3125, 100000, 256)
        x = jax.random.normal(k1, (N, IN), dtype=jnp.float32)
        edge_index = jax.random.randint(k2, (2, E), 0, N, dtype=jnp.int32)
        W = jax.random.normal(k3, (IN, HEADS * OUT_CH), dtype=jnp.float32) * (1.0 / np.sqrt(IN))
        att_src = jax.random.normal(k4, (HEADS, OUT_CH), dtype=jnp.float32) * 0.1
        att_dst = jax.random.normal(k5, (HEADS, OUT_CH), dtype=jnp.float32) * 0.1
        bias = jnp.zeros((HEADS * OUT_CH,), dtype=jnp.float32)
        return {'x': x, 'edge_index': edge_index, 'W': W, 'att_src': att_src, 'att_dst': att_dst, 'bias': bias}
    _L3_gnn_all = _L3_gnn_setup()
    _L3_gnn_in = {k: v for k, v in _L3_gnn_all.items() if k in ('W', 'att_src', 'att_dst', 'bias')}
    del _L3_gnn_all

    def _L3_ffn_setup():
        import jax, jax.numpy as jnp
        import numpy as np
        B, S, D, E, H, K = (4, 256, 256, 8, 512, 2)
        key = jax.random.key(seed)
        ks = jax.random.split(key, 6)
        x = jax.random.normal(ks[0], (B, S, D), jnp.float32)
        Wg = jax.random.normal(ks[1], (D, E), jnp.float32) * 0.02
        bg = jnp.zeros((E,), jnp.float32)
        W1 = jax.random.normal(ks[2], (E, D, H), jnp.float32) * 0.02
        b1 = jnp.zeros((E, H), jnp.float32)
        W2 = jax.random.normal(ks[3], (E, H, D), jnp.float32) * 0.02
        b2 = jnp.zeros((E, D), jnp.float32)
        return {'x': x, 'Wg': Wg, 'bg': bg, 'W1': W1, 'b1': b1, 'W2': W2, 'b2': b2}
    _L3_ffn_all = _L3_ffn_setup()
    _L3_ffn_in = {k: v for k, v in _L3_ffn_all.items() if k in ('Wg', 'bg', 'W1', 'b1', 'W2', 'b2')}
    del _L3_ffn_all
    return {'x': x, 'src': src, 'dst': dst, 'edge_attr_3': edge_attr_3, 'L0_gnn_W0': _L0_gnn_in['W0'], 'L0_gnn_b0': _L0_gnn_in['b0'], 'L0_gnn_g0': _L0_gnn_in['g0'], 'L0_gnn_beta0': _L0_gnn_in['beta0'], 'L0_gnn_W1': _L0_gnn_in['W1'], 'L0_gnn_b1': _L0_gnn_in['b1'], 'L0_gnn_g1': _L0_gnn_in['g1'], 'L0_gnn_beta1': _L0_gnn_in['beta1'], 'L0_ffn_gate_w': _L0_ffn_in['gate_w'], 'L0_ffn_gate_b': _L0_ffn_in['gate_b'], 'L0_ffn_w1': _L0_ffn_in['w1'], 'L0_ffn_b1': _L0_ffn_in['b1'], 'L0_ffn_w2': _L0_ffn_in['w2'], 'L0_ffn_b2': _L0_ffn_in['b2'], 'L1_gnn_W1': _L1_gnn_in['W1'], 'L1_gnn_b1': _L1_gnn_in['b1'], 'L1_gnn_g1': _L1_gnn_in['g1'], 'L1_gnn_be1': _L1_gnn_in['be1'], 'L1_gnn_W2': _L1_gnn_in['W2'], 'L1_gnn_b2': _L1_gnn_in['b2'], 'L1_gnn_g2': _L1_gnn_in['g2'], 'L1_gnn_be2': _L1_gnn_in['be2'], 'L1_gnn_W3': _L1_gnn_in['W3'], 'L1_gnn_b3': _L1_gnn_in['b3'], 'L1_ffn_Wg': _L1_ffn_in['Wg'], 'L1_ffn_bg': _L1_ffn_in['bg'], 'L1_ffn_bias': _L1_ffn_in['bias'], 'L1_ffn_W1': _L1_ffn_in['W1'], 'L1_ffn_b1': _L1_ffn_in['b1'], 'L1_ffn_W2': _L1_ffn_in['W2'], 'L1_ffn_b2': _L1_ffn_in['b2'], 'L2_gnn_W': _L2_gnn_in['W'], 'L2_gnn_a_src': _L2_gnn_in['a_src'], 'L2_gnn_a_dst': _L2_gnn_in['a_dst'], 'L2_gnn_edge_W': _L2_gnn_in['edge_W'], 'L2_gnn_edge_b': _L2_gnn_in['edge_b'], 'L2_gnn_bias': _L2_gnn_in['bias'], 'L2_ffn_Wr': _L2_ffn_in['Wr'], 'L2_ffn_br': _L2_ffn_in['br'], 'L2_ffn_W1': _L2_ffn_in['W1'], 'L2_ffn_b1': _L2_ffn_in['b1'], 'L2_ffn_g1': _L2_ffn_in['g1'], 'L2_ffn_be1': _L2_ffn_in['be1'], 'L2_ffn_m1': _L2_ffn_in['m1'], 'L2_ffn_v1': _L2_ffn_in['v1'], 'L2_ffn_W2': _L2_ffn_in['W2'], 'L2_ffn_b2': _L2_ffn_in['b2'], 'L2_ffn_g2': _L2_ffn_in['g2'], 'L2_ffn_be2': _L2_ffn_in['be2'], 'L2_ffn_m2': _L2_ffn_in['m2'], 'L2_ffn_v2': _L2_ffn_in['v2'], 'L2_ffn_Wo': _L2_ffn_in['Wo'], 'L2_ffn_bo': _L2_ffn_in['bo'], 'L3_gnn_W': _L3_gnn_in['W'], 'L3_gnn_att_src': _L3_gnn_in['att_src'], 'L3_gnn_att_dst': _L3_gnn_in['att_dst'], 'L3_gnn_bias': _L3_gnn_in['bias'], 'L3_ffn_Wg': _L3_ffn_in['Wg'], 'L3_ffn_bg': _L3_ffn_in['bg'], 'L3_ffn_W1': _L3_ffn_in['W1'], 'L3_ffn_b1': _L3_ffn_in['b1'], 'L3_ffn_W2': _L3_ffn_in['W2'], 'L3_ffn_b2': _L3_ffn_in['b2']}

def reference(x, src, dst, edge_attr_3, L0_gnn_W0, L0_gnn_b0, L0_gnn_g0, L0_gnn_beta0, L0_gnn_W1, L0_gnn_b1, L0_gnn_g1, L0_gnn_beta1, L0_ffn_gate_w, L0_ffn_gate_b, L0_ffn_w1, L0_ffn_b1, L0_ffn_w2, L0_ffn_b2, L1_gnn_W1, L1_gnn_b1, L1_gnn_g1, L1_gnn_be1, L1_gnn_W2, L1_gnn_b2, L1_gnn_g2, L1_gnn_be2, L1_gnn_W3, L1_gnn_b3, L1_ffn_Wg, L1_ffn_bg, L1_ffn_bias, L1_ffn_W1, L1_ffn_b1, L1_ffn_W2, L1_ffn_b2, L2_gnn_W, L2_gnn_a_src, L2_gnn_a_dst, L2_gnn_edge_W, L2_gnn_edge_b, L2_gnn_bias, L2_ffn_Wr, L2_ffn_br, L2_ffn_W1, L2_ffn_b1, L2_ffn_g1, L2_ffn_be1, L2_ffn_m1, L2_ffn_v1, L2_ffn_W2, L2_ffn_b2, L2_ffn_g2, L2_ffn_be2, L2_ffn_m2, L2_ffn_v2, L2_ffn_Wo, L2_ffn_bo, L3_gnn_W, L3_gnn_att_src, L3_gnn_att_dst, L3_gnn_bias, L3_ffn_Wg, L3_ffn_bg, L3_ffn_W1, L3_ffn_b1, L3_ffn_W2, L3_ffn_b2):
    import jax
    import jax.numpy as jnp

    def _L0_gnn_ref(x, edge_index, W0, b0, g0, beta0, W1, b1, g1, beta1):
        import jax, jax.numpy as jnp
        import numpy as np
        N = 3125
        E = 100000
        D = 256
        H = 256
        EPS = 1e-05

        def _gnn_layer(x, row, col, W, b, g, beta):
            n = x.shape[0]
            neigh = x[col]
            agg = jax.ops.segment_sum(neigh, row, num_segments=n)
            deg = jax.ops.segment_sum(jnp.ones((row.shape[0],), x.dtype), row, num_segments=n)
            deg = jnp.maximum(deg, 1.0)[:, None]
            h = (x + agg / deg) @ W.T + b
            mu = jnp.mean(h, axis=-1, keepdims=True)
            var = jnp.mean(jnp.square(h - mu), axis=-1, keepdims=True)
            hn = (h - mu) * jax.lax.rsqrt(var + EPS) * g + beta
            return jax.nn.silu(hn)
        row, col = (edge_index[0], edge_index[1])
        x = _gnn_layer(x, row, col, W0, b0, g0, beta0)
        x = _gnn_layer(x, row, col, W1, b1, g1, beta1)
        return x

    def _L0_ffn_ref(h, gate_w, gate_b, w1, b1, w2, b2):
        import math
        import jax, jax.numpy as jnp
        import numpy as np
        CAPACITY_FACTOR = 1.25
        B, L, D = h.shape
        E = gate_w.shape[1]
        T = B * L
        C = max(1, math.ceil(CAPACITY_FACTOR * T / E))
        x = h.reshape(T, D)
        logits = x @ gate_w + gate_b
        probs = jax.nn.softmax(logits, axis=-1)
        idx = jnp.argmax(probs, axis=-1)
        prb = jnp.take_along_axis(probs, idx[:, None], axis=1)[:, 0]
        one_hot = jax.nn.one_hot(idx, E, dtype=jnp.float32)
        pos = (jnp.cumsum(one_hot, axis=0) * one_hot).sum(-1).astype(jnp.int32) - 1
        kept = pos < C
        pos_safe = jnp.where(kept, pos, C)
        buf = jnp.zeros((E, C, D), dtype=h.dtype).at[idx, pos_safe].set(x, mode='drop')
        hmid = jax.nn.relu(jnp.einsum('ecd,edf->ecf', buf, w1) + b1[:, None, :])
        ybuf = jnp.einsum('ecf,efd->ecd', hmid, w2) + b2[:, None, :]
        pos_g = jnp.minimum(pos, C - 1)
        y_tok = ybuf[idx, pos_g] * (prb * kept)[:, None]
        y = y_tok.reshape(B, L, D)
        y = jnp.nan_to_num(y, nan=0.0, posinf=10000.0, neginf=-10000.0)
        return y

    def _L1_gnn_ref(node_feat, W1, b1, g1, be1, W2, b2, g2, be2, W3, b3, src, dst):
        import jax, jax.numpy as jnp
        import numpy as np
        N_NODES = 3125
        N_EDGES = 50000
        IN_C, EMB, OUT_C = (256, 512, 256)
        BN_EPS = 1e-05

        def _gcn_norm(src, dst, n):
            loop = jnp.arange(n, dtype=src.dtype)
            s = jnp.concatenate([src, loop])
            d = jnp.concatenate([dst, loop])
            deg = jax.ops.segment_sum(jnp.ones_like(d, dtype=jnp.float32), d, num_segments=n)
            dinv = jnp.where(deg > 0, jax.lax.rsqrt(deg), 0.0)
            return (s, d, dinv[s] * dinv[d])

        def _gcn_conv(x, W, b, s, d, norm, n):
            h = x @ W
            msg = h[s] * norm[:, None]
            agg = jax.ops.segment_sum(msg, d, num_segments=n)
            return agg + b

        def _bn_relu(x, g, be):
            mu = jnp.mean(x, axis=0)
            var = jnp.mean(jnp.square(x - mu), axis=0)
            y = (x - mu) * jax.lax.rsqrt(var + BN_EPS) * g + be
            return jax.nn.relu(y)
        n = node_feat.shape[0]
        s, d, norm = _gcn_norm(src, dst, n)
        x = _bn_relu(_gcn_conv(node_feat, W1, b1, s, d, norm, n), g1, be1)
        x = _bn_relu(_gcn_conv(x, W2, b2, s, d, norm, n), g2, be2)
        x = _gcn_conv(x, W3, b3, s, d, norm, n)
        return x

    def _L1_ffn_ref(x, Wg, bg, bias, W1, b1, W2, b2):
        import jax, jax.numpy as jnp
        import numpy as np
        D_MODEL = 256
        EXPERT_DIM = 512
        NUM_EXPERTS = 8
        TOP_K = 2
        SEQ_LEN = 128
        BATCH = 2
        x_flat = x.reshape(-1, D_MODEL)
        gate_logits = x_flat @ Wg + bg + bias
        topk_vals, topk_idx = jax.lax.top_k(gate_logits, TOP_K)
        topk_w = jax.nn.softmax(topk_vals, axis=-1)
        combine = (jax.nn.one_hot(topk_idx, NUM_EXPERTS, dtype=x.dtype) * topk_w[..., None]).sum(axis=1)
        h = jax.nn.relu(jnp.einsum('td,edh->teh', x_flat, W1) + b1)
        y = jnp.einsum('teh,ehd->ted', h, W2) + b2
        out = jnp.einsum('ted,te->td', y, combine)
        return out.reshape(x.shape)

    def _L2_gnn_ref(x, W, a_src, a_dst, edge_W, edge_b, bias, edge_attr, edge_index):
        import jax, jax.numpy as jnp
        import numpy as np
        N = 3125
        E = 25000
        IN = 256
        H = 8
        D = 32
        EF = 3
        n = x.shape[0]
        h = (x @ W.T).reshape(n, H, D)
        src, dst = (edge_index[0], edge_index[1])
        h_src = h[src]
        h_dst = h[dst]
        alpha = jnp.einsum('ehd,hd->eh', h_src, a_src) + jnp.einsum('ehd,hd->eh', h_dst, a_dst)
        enc = jax.nn.relu(edge_attr @ edge_W.T + edge_b).reshape(-1, H, D)
        alpha = alpha + jnp.sum(enc * h_dst, axis=-1)
        alpha = jnp.where(alpha >= 0, alpha, 0.2 * alpha)
        amax = jax.ops.segment_max(alpha, dst, num_segments=n)
        ex = jnp.exp(alpha - amax[dst])
        denom = jax.ops.segment_sum(ex, dst, num_segments=n)
        attn = ex / jnp.maximum(denom[dst], 1e-10)
        out = jax.ops.segment_sum(h_src * attn[..., None], dst, num_segments=n)
        return out.reshape(n, H * D) + bias

    def _L2_ffn_ref(x, Wr, br, W1, b1, g1, be1, m1, v1, W2, b2, g2, be2, m2, v2, Wo, bo):
        import jax, jax.numpy as jnp
        import numpy as np
        BN_EPS = 0.001

        def _bn(h, g, b, m, v):
            return g * (h - m) * jax.lax.rsqrt(v + BN_EPS) + b
        feat = jnp.mean(x, axis=0)
        w = jax.nn.softmax(feat @ Wr + br, axis=-1)
        h = jnp.einsum('bfd,edh->bfeh', x, W1) + b1
        h = jax.nn.relu(_bn(h, g1, be1, m1, v1))
        h = jnp.einsum('bfeh,ehk->bfek', h, W2) + b2
        h = jax.nn.relu(_bn(h, g2, be2, m2, v2))
        y = jnp.einsum('bfeh,ehd->bfed', h, Wo) + bo
        return jnp.einsum('bfed,fe->bfd', y, w)

    def _L3_gnn_ref(x, edge_index, W, att_src, att_dst, bias):
        import jax, jax.numpy as jnp
        import numpy as np
        HEADS = 4
        OUT_CH = 64
        NEG_SLOPE = 0.2
        N = x.shape[0]
        loop = jnp.arange(N, dtype=edge_index.dtype)
        src = jnp.concatenate([edge_index[0], loop])
        dst = jnp.concatenate([edge_index[1], loop])
        h = (x @ W).reshape(N, HEADS, OUT_CH)
        a_src = jnp.einsum('nhc,hc->nh', h, att_src)
        a_dst = jnp.einsum('nhc,hc->nh', h, att_dst)
        e = a_src[src] + a_dst[dst]
        e = jnp.where(e >= 0, e, NEG_SLOPE * e)
        e_max = jax.ops.segment_max(e, dst, num_segments=N)
        e_exp = jnp.exp(e - e_max[dst])
        denom = jax.ops.segment_sum(e_exp, dst, num_segments=N)
        alpha = e_exp / denom[dst]
        msgs = h[src] * alpha[:, :, None]
        out = jax.ops.segment_sum(msgs, dst, num_segments=N)
        out = out.reshape(N, HEADS * OUT_CH) + bias
        out = jax.nn.relu(out)
        norm = jnp.sqrt(jnp.sum(out * out, axis=-1, keepdims=True))
        out = out / jnp.maximum(norm, 1e-12)
        return out

    def _L3_ffn_ref(x, Wg, bg, W1, b1, W2, b2):
        import jax, jax.numpy as jnp
        import numpy as np
        B, S, D, E, H, K = (4, 256, 256, 8, 512, 2)
        Bv, Sv, Dv = x.shape
        gate_scores = x @ Wg + bg
        _, idx = jax.lax.top_k(gate_scores, K)
        mask = jax.nn.one_hot(idx, E, dtype=x.dtype).sum(axis=-2)
        xf = x.reshape(-1, Dv)
        mf = mask.reshape(-1, E)
        h = jax.nn.gelu(jnp.einsum('td,edh->teh', xf, W1) + b1[None], approximate=False)
        y = jnp.einsum('teh,ehd->ted', h, W2) + b2[None]
        out = jnp.einsum('ted,te->td', y, mf)
        return out.reshape(Bv, Sv, Dv)
    edge_index = jnp.stack([src, dst])
    x = x + _L0_gnn_ref(_layernorm(x, axis=-1), edge_index, L0_gnn_W0, L0_gnn_b0, L0_gnn_g0, L0_gnn_beta0, L0_gnn_W1, L0_gnn_b1, L0_gnn_g1, L0_gnn_beta1)
    x = x + _L0_ffn_ref(_layernorm(x, axis=-1)[None], L0_ffn_gate_w, L0_ffn_gate_b, L0_ffn_w1, L0_ffn_b1, L0_ffn_w2, L0_ffn_b2)[0]
    x = x + _L1_gnn_ref(_layernorm(x, axis=-1), L1_gnn_W1, L1_gnn_b1, L1_gnn_g1, L1_gnn_be1, L1_gnn_W2, L1_gnn_b2, L1_gnn_g2, L1_gnn_be2, L1_gnn_W3, L1_gnn_b3, src, dst)
    x = x + _L1_ffn_ref(_layernorm(x, axis=-1)[None], L1_ffn_Wg, L1_ffn_bg, L1_ffn_bias, L1_ffn_W1, L1_ffn_b1, L1_ffn_W2, L1_ffn_b2)[0]
    x = x + _L2_gnn_ref(_layernorm(x, axis=-1), L2_gnn_W, L2_gnn_a_src, L2_gnn_a_dst, L2_gnn_edge_W, L2_gnn_edge_b, L2_gnn_bias, edge_attr_3, edge_index)
    x = x + _L2_ffn_ref(_layernorm(x, axis=-1)[None], L2_ffn_Wr, L2_ffn_br, L2_ffn_W1, L2_ffn_b1, L2_ffn_g1, L2_ffn_be1, L2_ffn_m1, L2_ffn_v1, L2_ffn_W2, L2_ffn_b2, L2_ffn_g2, L2_ffn_be2, L2_ffn_m2, L2_ffn_v2, L2_ffn_Wo, L2_ffn_bo)[0]
    x = x + _L3_gnn_ref(_layernorm(x, axis=-1), edge_index, L3_gnn_W, L3_gnn_att_src, L3_gnn_att_dst, L3_gnn_bias)
    x = x + _L3_ffn_ref(_layernorm(x, axis=-1)[None], L3_ffn_Wg, L3_ffn_bg, L3_ffn_W1, L3_ffn_b1, L3_ffn_W2, L3_ffn_b2)[0]
    return x

_drawn_inputs = setup_inputs


def setup_inputs(seed=0):
    import zlib

    import numpy as np

    out = dict(_drawn_inputs(seed))
    spreads = {'L0_gnn_g0': (1.0, 0.2),
     'L0_gnn_beta0': (0.0, 0.1),
     'L0_gnn_g1': (1.0, 0.2),
     'L0_gnn_beta1': (0.0, 0.1),
     'L0_ffn_gate_b': (0.0, 0.1),
     'L0_ffn_b1': (0.0, 0.483),
     'L0_ffn_b2': (0.0, 0.351),
     'L1_gnn_b1': (0.0, 0.8),
     'L1_gnn_g1': (1.0, 0.2),
     'L1_gnn_be1': (0.0, 0.42),
     'L1_gnn_b2': (0.0, 0.8),
     'L1_gnn_g2': (1.0, 0.2),
     'L1_gnn_be2': (0.0, 0.1),
     'L1_gnn_b3': (0.0, 0.1),
     'L1_ffn_bias': (0.0, 0.268),
     'L2_gnn_edge_b': (0.0, 0.1),
     'L2_gnn_bias': (0.0, 0.1),
     'L2_ffn_br': (0.0, 0.431),
     'L2_ffn_b1': (0.0, 0.317),
     'L2_ffn_g1': (1.0, 0.2),
     'L2_ffn_be1': (0.0, 0.35),
     'L2_ffn_m1': (0.0, 0.335),
     'L2_ffn_v1': (1.0, 0.6),
     'L2_ffn_b2': (0.0, 0.1),
     'L2_ffn_g2': (1.0, 0.2),
     'L2_ffn_be2': (0.0, 0.1),
     'L2_ffn_m2': (0.0, 0.1),
     'L2_ffn_v2': (1.0, 0.6),
     'L2_ffn_bo': (0.0, 0.1),
     'L3_gnn_bias': (0.0, 0.536),
     'L3_ffn_bg': (0.0, 0.1),
     'L3_ffn_b1': (0.0, 0.324),
     'L3_ffn_b2': (0.0, 0.1)}
    factors = {'L1_ffn_bg': 4.038,
     'L1_ffn_b1': 7.024,
     'L1_ffn_b2': 3.348,
     'L3_gnn_att_src': 4.808,
     'L3_gnn_att_dst': 8.0}
    for name, (base, spread) in spreads.items():
        noise = np.random.default_rng([zlib.crc32(name.encode()), seed]).standard_normal(out[name].shape)
        drawn = base * np.exp(spread * noise) if base else spread * noise
        out[name] = jnp.asarray(drawn.astype(out[name].dtype))
    for name, factor in factors.items():
        out[name] = (out[name] * factor).astype(out[name].dtype)
    return out
```

```python
import numpy as np
import concourse.bass as bass
from concourse import mybir

F32, I32, BF16 = mybir.dt.float32, mybir.dt.int32, mybir.dt.bfloat16
ALU, ACT, AX = mybir.AluOpType, mybir.ActivationFunctionType, mybir.AxisListType
ds = bass.ds

P = 128
NODES, D = 3125, 256
B = 125
NBLK = NODES // B
EDGES = 50000
EC = EDGES // B
EXP = 8
CAP = 489
TU = 5
NTMIN = EDGES // P + NBLK
NT = 420
assert NTMIN <= NT and NT % 10 == 0 and NT % 4 == 0
PF = 8
BIG = float(2.0 ** 100)
XW = NBLK * D
HID = 512
BUFW = NBLK * 514
LN_EPS, GBN_EPS, FBN_EPS = 1e-5, 1e-5, 1e-3

C_ID, C_IOTA, C_STRICT, C_UPTO, C_ONE, C_TILE, C_EPS = 0, 128, 256, 381, 506, 634, 1054
C_END = 1058
ROWS = ["L0_gnn_b0", "L0_gnn_g0", "L0_gnn_beta0", "L0_gnn_b1", "L0_gnn_g1", "L0_gnn_beta1", "L1_gnn_b3",
        "L2_gnn_bias", "L2_gnn_a_src", "L2_gnn_a_dst", "L3_gnn_bias", "L3_gnn_att_src", "L3_gnn_att_dst"]
GATEB = ["L0_ffn_gate_b", "L1_ffn_bg", "L1_ffn_bias", "L2_ffn_br", "L3_ffn_bg"]
ROWN = 256 * len(ROWS) + EXP * len(GATEB)
COLS = [("L0_ffn_b1", 64), ("L1_gnn_b1", 4), ("L1_gnn_g1", 4), ("L1_gnn_be1", 4), ("L1_gnn_b2", 4),
        ("L1_gnn_g2", 4), ("L1_gnn_be2", 4), ("L1_ffn_b1", 32), ("L2_ffn_b1", 16), ("L2_ffn_g1", 16),
        ("L2_ffn_be1", 16), ("L2_ffn_m1", 16), ("L2_ffn_v1", 16), ("L2_ffn_b2", 16), ("L2_ffn_g2", 16),
        ("L2_ffn_be2", 16), ("L2_ffn_m2", 16), ("L2_ffn_v2", 16), ("L3_ffn_b1", 32)]
COLN = sum(n for _, n in COLS)
GATES = ["L0_ffn_gate_w", "L1_ffn_Wg", "L2_ffn_Wr", "L3_ffn_Wg"]
B2S = ["L0_ffn_b2", "L1_ffn_b2", "L2_ffn_bo", "L3_ffn_b2"]


def row_at(name):
    if name in ROWS:
        return 256 * ROWS.index(name)
    return 256 * len(ROWS) + EXP * GATEB.index(name)


def col_at(name):
    at = 0
    for n, w in COLS:
        if n == name:
            return at
        at += w
    raise KeyError(name)


class Chain:

    def __init__(self, eng, sem):
        self.eng, self.sem, self.n, self.i, self.per, self.k = eng, sem, 0, None, 0, 0

    def enter(self, i, per):
        self.i, self.per, self.k = i, per, 0

    def leave(self, rounds):
        assert self.k == self.per, (self.k, self.per)
        self.n += rounds * self.per
        self.i, self.k = None, 0

    def value(self):
        return self.n + self.k if self.i is None else self.i * self.per + (self.n + self.k)

    def link(self, ins):
        if self.i is None:
            self.n += 1
        else:
            self.k += 1
        ins.then_inc(self.sem, 1)
        self.eng.wait_ge(self.sem, self.value())


def hold(eng, sem, value):
    eng.wait_ge(sem, value)
    eng.nop(nofuse=True)


class Mem:

    def __init__(self, nc):
        self.nc, self.made = nc, 0

    def name(self, name):
        self.made += 1
        return f"{name}_{self.made}"

    def sb(self, name, shape, dtype):
        return self.nc.alloc_sbuf_tensor(self.name(name), shape, dtype)

    def psum(self, name):
        return self.nc.alloc_psum_tensor(self.name(name), [P, 512], F32)

    def sem(self, name):
        return self.nc.alloc_semaphore(self.name(name))


def build(nc, a, out, upto=99):
    m = Mem(nc)
    sb = m.sb
    m.X = sb("x_res", [B, XW], F32)
    m.bufa = sb("bufa", [P, BUFW], F32)
    m.bufb = sb("bufb", [P, BUFW], F32)
    m.cst = sb("cst", [P, C_END], F32)
    m.rows = sb("rows", [P, ROWN], F32)
    m.cols = sb("cols", [P, COLN], F32)
    m.lists = {k: sb(f"list_{k}", [P, NT * PF], F32) for k in ("src", "dst")}
    m.blk = {k: sb(f"blk_{k}", [1, NT], I32) for k in ("src", "dst")}
    m.small = sb("small", [P, 1400], F32)
    m.deg = m.small[:B, 1300:1325]
    m.table = nc.dram_tensor("table", (NODES, D), F32, kind="Internal").ap()
    m.table2 = nc.dram_tensor("table2", (NODES, HID), F32, kind="Internal").ap()
    m.tablea = {h: nc.dram_tensor(f"tablea{h}", (NODES, h), F32, kind="Internal").ap() for h in (4, 8)}
    m.ldram = {k: nc.dram_tensor(f"edges_{k}", (P * NT, PF), F32, kind="Internal").ap() for k in ("src", "dst")}
    m.a = a

    load(nc, m)
    bin_edges(nc, m, "src")
    bin_edges(nc, m, "dst")
    X, XN, AGG = m.X, m.bufb[:B, 0:XW], m.bufa
    layernorm(nc, m, X[:], XN)
    for l in range(2):
        store_table(nc, m, XN, m.table, D)
        aggregate(nc, m, "src", m.table, D, True, True)
        sage_layer(nc, m, l, XN)
    residual(nc, m, XN)
    if upto >= 1:
        layernorm(nc, m, X[:], XN)
        ffn(nc, m, 0, XN)
    if upto >= 2:
        layernorm(nc, m, X[:], XN)
        gcn(nc, m, XN)
    if upto >= 3:
        layernorm(nc, m, X[:], XN)
        ffn(nc, m, 1, XN)
    if upto >= 4:
        layernorm(nc, m, X[:], XN)
        gat(nc, m, 2, XN)
    if upto >= 5:
        layernorm(nc, m, X[:], XN)
        ffn(nc, m, 2, XN)
    if upto >= 6:
        layernorm(nc, m, X[:], XN)
        gat(nc, m, 3, XN)
    if upto >= 7:
        layernorm(nc, m, X[:], XN)
        ffn(nc, m, 3, XN)
    with nc.cleanup_on_exit():
        stored = m.sem("stored")
        with nc.Block() as block:
            @block.sync
            def _(sp):
                sp.dma_start(out.rearrange("(t p) w -> p t w", p=B),
                             m.X[:, :].rearrange("p (t w) -> p t w", w=D)).then_inc(stored, 16)
                sp.wait_ge(stored, 16)


def load(nc, m):
    with nc.cleanup_on_exit():
        loaded = m.sem("loaded")
        with nc.Block() as block:
            @block.sync
            def _(sp):
                sp.dma_start(m.cst[:, :], m.a["consts"]).then_inc(loaded, 16)
                sp.dma_start(m.rows[:, :], m.a["rows"]).then_inc(loaded, 16)
                sp.dma_start(m.cols[:, :], m.a["cols"]).then_inc(loaded, 16)
                sp.dma_start(m.X[:, :].rearrange("p (t w) -> p t w", w=D),
                             m.a["x"].rearrange("(t p) w -> p t w", p=B)).then_inc(loaded, 16)
                sp.wait_ge(loaded, 64)


def bin_edges(nc, m, key):
    other = "dst" if key == "src" else "src"
    count_degree = key == "dst"
    NS = 10
    with nc.cleanup_on_exit():
        sb, sem = m.sb, m.sem
        wa = m.bufa[:B, :]
        names = ["key", "hi", "lo", "onehot", "scan", "tmp", "rank", "zero", "slot"]
        W = {n: wa[:, i * EC:(i + 1) * EC] for i, n in enumerate(names)}
        keyi = wa[:, 9 * EC:10 * EC].bitcast(I32)
        othi = wa[:, 10 * EC:11 * EC].bitcast(I32)
        iq = wa[:, 11 * EC:12 * EC].bitcast(I32)
        iq2 = wa[:, 12 * EC:13 * EC].bitcast(I32)
        attr = wa[:, 13 * EC:16 * EC]
        slot_i = wa[:, 16 * EC:17 * EC].bitcast(I32)
        pay = m.bufb[:B, 0:EC * PF]
        payv = pay.rearrange("p (c f) -> p c f", f=PF)
        fill = m.bufb[:, 3400:3400 + NT * PF]
        small = m.small
        cnt, tot, tiles, tstart, base, ti = [small[:B, 32 * i:32 * i + NBLK] for i in range(6)]
        tii = small[:B, 192:192 + NBLK].bitcast(I32)
        paystage = sb("paystage", [B, NS, PF], F32)
        slotstage = sb("slotstage", [B, NS], I32)
        ohl = sb("ohl", [B, 2, 5, B], BF16)
        ohh = sb("ohh", [B, 2, 5, NBLK], BF16)
        blkf = sb("blkf", [1, NT], F32)
        ps = m.psum("ps")
        pd = m.psum("pd")
        iota = m.cst[:B, C_IOTA:C_IOTA + NBLK]
        edges_in, filled, steps, counted = sem("edges_in"), sem("filled"), sem("steps"), sem("counted")
        prefixed, prefilled = sem("prefixed"), sem("prefilled")
        hot, hot_used, degree_done = sem("hot"), sem("hot_used"), sem("degree_done")
        staged, slots_ready = sem("staged"), sem("slots_ready")
        sent = [sem(f"sent{k}") for k in range(NS)]
        listed = sem("listed")
        with nc.Block() as block:
            @block.sync
            def _(sp):
                sp.dma_start(keyi, m.a[key]).then_inc(edges_in, 16)
                sp.dma_start(othi, m.a[other]).then_inc(edges_in, 16)
                sp.dma_start(attr, m.a["attr"]).then_inc(edges_in, 16)
                sp.wait_ge(filled, 1)
                sp.dma_start(m.ldram[key].rearrange("(p c) f -> p (c f)", p=P), fill).then_inc(prefilled, 16)
                for k in range(NS):
                    sp.wait_ge(sent[k], 16 * (EC // NS))
                sp.dma_start(m.lists[key][:, :],
                             m.ldram[key].rearrange("(p c) f -> p (c f)", p=P)).then_inc(listed, 16)
                sp.wait_ge(listed, 16)

            @block.tensor
            def _(pe):
                pe.wait_ge(counted, 1)
                pe.matmul(ps[:B, 0:NBLK], m.cst[:B, C_STRICT:C_STRICT + B], cnt, start=True, stop=True)
                pe.matmul(ps[:B, 32:32 + NBLK], m.cst[:B, C_ONE:C_ONE + B], cnt, start=True,
                          stop=True).then_inc(prefixed, 1)
                if count_degree:
                    pe.matmul(pd[:B, 0:NBLK], m.cst[:B, C_ONE:C_ONE + B], W["zero"][:, 0:NBLK], start=True,
                              stop=True, skip_group_check=True)
                    with pe.Fori(0, EC // 10) as i:
                        for g in range(2):
                            pe.wait_ge(hot, i * 2 + (g + 1))
                            for c in range(5):
                                mm = pe.matmul(pd[:B, 0:NBLK], ohl[:, g, c, :], ohh[:, g, c, :], start=False,
                                               stop=False, skip_group_check=True)
                            mm.then_inc(hot_used, 1)

            @block.gpsimd
            def _(pool):
                pool.wait_ge(prefilled, 16)
                with pool.Fori(0, EC // NS) as i:
                    hold(pool, staged, i * 2 + 2)
                    for k in range(NS):
                        pool.indirect_dma_start(
                            out=m.ldram[key], out_offset=bass.IndirectOffsetOnAxis(ap=slotstage[:, k:k + 1], axis=0),
                            in_=paystage[:, k, :], in_offset=None).then_inc(sent[k], 16)

            @block.vector
            def _(v):
                c = Chain(v, steps)
                link = c.link
                fv = fill.rearrange("p (c f) -> p c f", f=PF)
                link(v.memset(fill, 0.0))
                v.memset(fv[:, :, 1:2], -1.0).then_inc(filled, 1)
                v.memset(W["rank"], 0.0)
                v.memset(W["zero"], 0.0)
                v.memset(W["slot"], 0.0)
                link(v.memset(pay, 0.0))
                v.wait_ge(edges_in, 48)
                link(v.tensor_copy(W["key"], keyi))
                link(v.tensor_scalar(W["hi"], W["key"], float(B), None, ALU.is_ge))
                for b in range(2, NBLK):
                    link(v.scalar_tensor_tensor(W["hi"], W["key"], float(B * b), W["hi"], ALU.is_ge, ALU.add))
                link(v.scalar_tensor_tensor(W["lo"], W["hi"], -float(B), W["key"], ALU.mult, ALU.add))
                with v.Fori(0, NBLK) as b:
                    c.enter(b, 4)
                    link(v.tensor_scalar(W["onehot"], W["hi"], iota[:, ds(b, 1)], None, ALU.is_equal))
                    link(v.tensor_tensor_scan(W["scan"], W["onehot"], W["zero"], 0.0, ALU.add, ALU.add))
                    v.tensor_scalar(cnt[:, ds(b, 1)], W["scan"][:, EC - 1:EC], 1.0, None, ALU.mult)
                    link(v.tensor_tensor(W["tmp"], W["onehot"], W["scan"], ALU.mult))
                    link(v.tensor_tensor(W["rank"], W["rank"], W["tmp"], ALU.add))
                c.leave(NBLK)
                v.tensor_scalar(tiles, cnt, 1.0, None, ALU.mult).then_inc(counted, 1)
                v.wait_ge(prefixed, 1)
                link(v.tensor_scalar(tot, ps[:B, 32:32 + NBLK], float(P - 1), None, ALU.add))
                link(v.tensor_copy(tii, tot))
                link(v.tensor_scalar(tii, tii, 7, None, ALU.arith_shift_right))
                link(v.tensor_copy(tiles, tii))
                link(v.tensor_tensor_scan(tstart, tiles, W["zero"][:, 0:NBLK], 0.0, ALU.add, ALU.add))
                link(v.tensor_tensor(tstart, tstart, tiles, ALU.subtract))
                link(v.tensor_scalar(ti, tstart, float(P), -1.0, ALU.mult, ALU.add))
                link(v.tensor_tensor(base, ti, ps[:B, 0:NBLK], ALU.add))
                with v.Fori(0, NBLK) as b:
                    c.enter(b, 2)
                    link(v.tensor_scalar(W["tmp"], W["hi"], iota[:, ds(b, 1)], base[:, ds(b, 1)], ALU.is_equal,
                                         ALU.mult))
                    link(v.tensor_tensor(W["slot"], W["slot"], W["tmp"], ALU.add))
                c.leave(NBLK)
                link(v.tensor_tensor(W["slot"], W["slot"], W["rank"], ALU.add))
                link(v.tensor_copy(iq, W["slot"]))
                v.tensor_scalar(iq2, iq, 7, None, ALU.arith_shift_right)
                link(v.tensor_scalar(iq, iq, P - 1, None, ALU.bitwise_and))
                link(v.tensor_copy(W["tmp"], iq))
                link(v.tensor_copy(W["scan"], iq2))
                link(v.scalar_tensor_tensor(W["slot"], W["tmp"], float(NT), W["scan"], ALU.mult, ALU.add))
                link(v.tensor_copy(slot_i, W["slot"]))
                link(v.tensor_scalar(blkf[:, :], m.cst[0:1, C_TILE:C_TILE + NT], tstart[0:1, 1:2], None, ALU.is_ge))
                with v.Fori(2, NBLK) as b:
                    c.enter(b - 2, 1)
                    link(v.scalar_tensor_tensor(blkf[:, :], m.cst[0:1, C_TILE:C_TILE + NT], tstart[0:1, ds(b, 1)],
                                                blkf[:, :], ALU.is_ge, ALU.add))
                c.leave(NBLK - 2)
                v.tensor_copy(m.blk[key][:, :], blkf[:, :])
                v.tensor_copy(payv[:, :, 0].bitcast(I32), othi)
                v.tensor_copy(payv[:, :, 1], W["lo"])
                v.tensor_copy(payv[:, :, 2:5], attr.rearrange("p (c f) -> p c f", f=3))
                link(v.memset(payv[:, :, 5:6], 1.0))
                v.sem_inc(hot_used, 2)
                with v.Fori(0, EC // NS) as i:
                    for k in range(NS):
                        v.wait_ge(sent[k], i * 16)
                    v.tensor_scalar(paystage[:, :, :].rearrange("p a f -> p (a f)").bitcast(I32),
                                    pay[:, ds(i * (NS * PF), NS * PF)].bitcast(I32), 0, None,
                                    ALU.bitwise_or).then_inc(staged, 1)
                    v.tensor_scalar(slotstage[:, :], slot_i[:, ds(i * NS, NS)], 0, None,
                                    ALU.bitwise_or).then_inc(staged, 1)
                    if count_degree:
                        for g in range(2):
                            v.wait_ge(hot_used, i * 2 + (g + 1))
                            for q in range(5):
                                col = i * NS + (g * 5 + q)
                                v.tensor_scalar(ohl[:, g, q, :], m.cst[:B, C_IOTA:C_IOTA + B],
                                                W["lo"][:, ds(col, 1)], None, ALU.is_equal)
                                last = v.tensor_scalar(ohh[:, g, q, :], iota, W["hi"][:, ds(col, 1)], None,
                                                       ALU.is_equal)
                            last.then_inc(hot, 1)
                if count_degree:
                    v.wait_ge(hot_used, 2 + EC // 5)
                    v.tensor_copy(m.deg, pd[:B, 0:NBLK])


def layernorm(nc, m, src, dst):
    with nc.cleanup_on_exit():
        sem = m.sem
        st = m.small[:B, 0:6 * NBLK]
        f = st.rearrange("p (t s) -> p s t", s=6)
        mean, var, dif, std, inv, nb = [m.small[:B, 200 + 32 * i:200 + 32 * i + NBLK] for i in range(6)]
        steps, var_ready, std_ready = sem("steps"), sem("var_ready"), sem("std_ready")
        with nc.Block() as block:
            @block.vector
            def _(v):
                c = Chain(v, steps)
                link = c.link
                with v.Fori(0, NBLK // TU) as i:
                    c.enter(i, 1)
                    for k in range(TU):
                        ins = v.bn_stats(st[:, ds((i * TU + k) * 6, 6)], src[:, ds((i * TU + k) * D, D)])
                    link(ins)
                c.leave(NBLK // TU)
                link(v.tensor_tensor(mean, f[:, 1], f[:, 4], ALU.add))
                link(v.tensor_scalar(mean, mean, 0.5, None, ALU.mult))
                link(v.tensor_tensor(dif, f[:, 1], f[:, 4], ALU.subtract))
                link(v.tensor_tensor(dif, dif, dif, ALU.mult))
                link(v.tensor_scalar(dif, dif, 0.25, None, ALU.mult))
                link(v.tensor_tensor(var, f[:, 2], f[:, 5], ALU.add))
                v.scalar_tensor_tensor(var, var, 1.0 / D, dif, ALU.mult, ALU.add).then_inc(var_ready, 1)
                v.wait_ge(std_ready, 1)
                link(v.reciprocal(inv, std))
                link(v.scalar_tensor_tensor(nb, mean, -1.0, inv, ALU.mult, ALU.mult))
                with v.Fori(0, NBLK // TU) as i:
                    for k in range(TU):
                        t = i * TU + k
                        v.tensor_scalar(dst[:, ds(t * D, D)], src[:, ds(t * D, D)], inv[:, ds(t, 1)],
                                        nb[:, ds(t, 1)], ALU.mult, ALU.add)

            @block.scalar
            def _(act):
                act.wait_ge(var_ready, 1)
                act.activation(std, var, ACT.Sqrt, bias=m.cst[:B, C_EPS:C_EPS + 1]).then_inc(std_ready, 1)


def store_table(nc, m, src, table, width):
    with nc.cleanup_on_exit():
        stored = m.sem("stored")
        with nc.Block() as block:
            @block.sync
            def _(sp):
                sp.dma_start(table.rearrange("(t p) w -> p t w", p=B),
                             src.rearrange("p (t w) -> p t w", w=width)).then_inc(stored, 16)
                sp.wait_ge(stored, 16)


def aggregate(nc, m, key, table, width, count, clear):
    W = width + (1 if count else 0)
    NB = 10
    acc = m.bufa[:B, 0:NBLK * W]
    lst = m.lists[key][:, :].rearrange("p (c f) -> p c f", f=PF)
    with nc.cleanup_on_exit():
        sb, sem = m.sb, m.sem
        rows = sb("gathered", [P, NB, W], F32)
        idx = sb("idx", [P, NB], I32)
        onehot = sb("onehot", [P, NB, B], F32)
        ps = [m.psum(f"ps{i}") for i in range(5)]
        cleared, idx_ready, onehot_ready = sem("cleared"), sem("idx_ready"), sem("onehot_ready")
        summed, added = sem("summed"), sem("added")
        gathered = [sem(f"gathered{k}") for k in range(NB)]
        with nc.Block() as block:
            @block.vector
            def _(v):
                if count:
                    v.memset(rows[:, :, width:W], 1.0).then_inc(cleared, 1)
                else:
                    v.sem_inc(cleared, 1)
                if clear:
                    v.memset(acc, 0.0).then_inc(cleared, 1)
                    v.wait_ge(cleared, 2)
                v.sem_inc(added, 5)
                with v.Fori(0, NT // NB) as i:
                    v.wait_ge(summed, i * NB)
                    v.tensor_scalar(idx[:, :], lst[:, ds(i * NB, NB), 0].bitcast(I32), 0, None,
                                    ALU.bitwise_or).then_inc(idx_ready, 1)
                    for k in range(NB):
                        v.tensor_scalar(onehot[:, k, :], m.cst[:, C_IOTA:C_IOTA + B], lst[:, ds(i * NB + k, 1), 1],
                                        None, ALU.is_equal).then_inc(onehot_ready, 1)
                    for k in range(NB):
                        b = v.value_load(m.blk[key][0:1, ds(i * NB + k, 1)], min_val=0, max_val=NBLK - 1)
                        part = acc[:, ds(b * W, W)]
                        v.wait_ge(summed, i * NB + (k + 1))
                        v.tensor_tensor(part, part, ps[k % 5][:B, 0:W], ALU.add).then_inc(added, 1)
                        v.wait_ge(added, i * NB + (k + 6))

            @block.gpsimd
            def _(pool):
                pool.wait_ge(cleared, 1)
                with pool.Fori(0, NT // NB) as i:
                    hold(pool, idx_ready, i + 1)
                    for k in range(NB):
                        pool.indirect_dma_start(
                            out=rows[:, k, 0:width], out_offset=None, in_=table,
                            in_offset=bass.IndirectOffsetOnAxis(ap=idx[:, k:k + 1], axis=0)).then_inc(gathered[k], 16)

            @block.tensor
            def _(pe):
                with pe.Fori(0, NT // NB) as i:
                    for k in range(NB):
                        pe.wait_ge(gathered[k], i * 16 + 16)
                        pe.wait_ge(onehot_ready, i * NB + (k + 1))
                        pe.wait_ge(added, i * NB + (k + 1))
                        pe.matmul(ps[k % 5][:B, 0:W], onehot[:, k, :], rows[:, k, :], start=True,
                                  stop=True).then_inc(summed, 1)


def token_linear(nc, m, src, wdram, wide, evac, stage_add=None, keep=None):
    with nc.cleanup_on_exit():
        sb, sem = m.sb, m.sem
        w = sb("w", [P, 2, wide], F32)
        st = sb("st", [B, TU, D], F32)
        stT = sb("stT", [P, TU, 2 * B], F32)
        ps = [m.psum(f"ps{i}") for i in range(TU)]
        w_in, staged, turned, lifted = sem("w_in"), sem("staged"), sem("turned"), sem("lifted")
        product, out_done, kept = sem("product"), sem("out_done"), sem("kept")
        with nc.Block() as block:
            @block.sync
            def _(sp):
                sp.dma_start(w[:, :, :], wdram).then_inc(w_in, 16)
                sp.wait_ge(w_in, 16)

            @block.vector
            def _(v):
                v.sem_inc(out_done, TU)
                with v.Fori(0, NBLK // TU) as i:
                    for k in range(TU):
                        t = i * TU + k
                        v.wait_ge(turned, i * TU)
                        if stage_add:
                            scale, other, ow = stage_add
                            v.scalar_tensor_tensor(st[:, k, :], other[:, ds(t * ow, D)], scale[:, ds(t, 1)],
                                                   src[:, ds(t * D, D)], ALU.mult, ALU.add).then_inc(staged, 1)
                        else:
                            v.tensor_scalar(st[:, k, :], src[:, ds(t * D, D)], 1.0, None,
                                            ALU.mult).then_inc(staged, 1)
                    for k in range(TU):
                        t = i * TU + k
                        if keep is not None:
                            v.wait_ge(lifted, t + 1)
                            for h in range(2):
                                kp = v.tensor_scalar(keep[:, ds(t * B + h * NODES, B)], stT[:, k, h * B:(h + 1) * B],
                                                     1.0, None, ALU.mult)
                            kp.then_inc(kept, 1)
                        v.wait_ge(product, t + 1)
                        evac(v, t, ps[k][:B, 2 * B:2 * B + wide]).then_inc(out_done, 1)
                if keep is not None:
                    v.wait_ge(kept, NBLK)

            @block.scalar
            def _(act):
                with act.Fori(0, NBLK // TU) as i:
                    for k in range(TU):
                        act.wait_ge(turned, i * TU + (k + 1))
                        act.wait_ge(product, i * TU)
                        if keep is not None:
                            act.wait_ge(kept, i * TU)
                        act.activation(stT[:, k, :], ps[k][:, 0:2 * B], ACT.Copy).then_inc(lifted, 1)

            @block.tensor
            def _(pe):
                pe.wait_ge(w_in, 16)
                with pe.Fori(0, NBLK // TU) as i:
                    for k in range(TU):
                        pe.wait_ge(staged, i * TU + (k + 1))
                        pe.wait_ge(out_done, i * TU + (k + 1))
                        for h in range(2):
                            tr = pe.transpose(ps[k][:, h * B:(h + 1) * B], st[:, k, h * P:(h + 1) * P],
                                              m.cst[:B, C_ID:C_ID + B])
                        tr.then_inc(turned, 1)
                    for k in range(TU):
                        pe.wait_ge(lifted, i * TU + (k + 1))
                        for h in range(2):
                            mm = pe.matmul(ps[k][:B, 2 * B:2 * B + wide], stT[:, k, h * B:(h + 1) * B], w[:, h, :],
                                           start=(h == 0), stop=(h == 1))
                        mm.then_inc(product, 1)


def sage_layer(nc, m, l, XN):
    W = D + 1
    acc = m.bufa[:B, 0:NBLK * W]
    deg = acc.rearrange("p (t w) -> p t w", w=W)[:, :, D]
    rdeg = m.small[:B, 400:400 + NBLK]
    H = m.bufb[:B, XW:2 * XW]
    with nc.cleanup_on_exit():
        steps = m.sem("steps")
        with nc.Block() as block:
            @block.vector
            def _(v):
                c = Chain(v, steps)
                c.link(v.tensor_scalar(rdeg, deg, 1.0, None, ALU.max))
                c.link(v.reciprocal(rdeg, rdeg))
    at = row_at(f"L0_gnn_b{l}")
    bias = m.rows[:B, at:at + D]
    token_linear(nc, m, XN, m.a[f"L0_gnn_W{l}"], D,
                 lambda v, t, ps: v.tensor_tensor(H[:, ds(t * D, D)], ps, bias, ALU.add),
                 stage_add=(rdeg, acc, W))
    layernorm(nc, m, H, H)
    with nc.cleanup_on_exit():
        steps, affine, gate = (m.sem(n) for n in ("steps", "affine", "gate"))
        g = m.rows[:B, row_at(f"L0_gnn_g{l}"):][:, 0:D]
        be = m.rows[:B, row_at(f"L0_gnn_beta{l}"):][:, 0:D]
        with nc.Block() as block:
            @block.vector
            def _(v):
                c = Chain(v, steps)
                hv = H.rearrange("p (t w) -> p t w", w=D)
                c.link(v.tensor_tensor(hv, hv, g.unsqueeze(1).broadcast_to([B, NBLK, D]), ALU.mult))
                v.tensor_tensor(hv, hv, be.unsqueeze(1).broadcast_to([B, NBLK, D]), ALU.add).then_inc(affine, 1)
                v.wait_ge(gate, 1)
                v.tensor_tensor(XN, H, m.bufa[:B, 0:XW], ALU.mult)

            @block.scalar
            def _(act):
                act.wait_ge(affine, 1)
                act.activation(m.bufa[:B, 0:XW], H, ACT.Sigmoid).then_inc(gate, 1)


def residual(nc, m, src):
    with nc.cleanup_on_exit():
        with nc.Block() as block:
            @block.vector
            def _(v):
                v.tensor_tensor(m.X[:, :], m.X[:, :], src, ALU.add)


def spread(ap, n):
    return ap.unsqueeze(2).broadcast_to([ap.shape[0], ap.shape[1], n])


FFN = {0: dict(F=1024, act=ACT.Relu), 1: dict(F=512, act=ACT.Relu), 2: dict(F=256, act=ACT.Relu),
       3: dict(F=512, act=ACT.Gelu)}


def gates(nc, m, l, LG, coef):
    G = NBLK * EXP
    with nc.cleanup_on_exit():
        sem = m.sem
        mx, sm, ix, t1 = [m.small[:B, 600 + 32 * i:600 + 32 * i + NBLK] for i in range(4)]
        w1 = m.small[:B, 730:730 + NBLK]
        E = m.small[:B, 760:760 + G]
        OH = m.small[:B, 960:960 + G]
        v3 = lambda ap: ap.rearrange("p (t e) -> p t e", e=EXP)
        lg, ev, oh, cf = v3(LG), v3(E), v3(OH), v3(coef)
        io8 = m.cst[:B, C_IOTA:C_IOTA + EXP].unsqueeze(1).broadcast_to([B, NBLK, EXP])
        T = m.sb("gt", [B, 3, G], F32)
        a1, a2, a3 = v3(T[:, 0, :]), v3(T[:, 1, :]), v3(T[:, 2, :])
        ps = m.psum("ps")
        steps, shifted, exped, picked, counted = (sem(n) for n in ("steps", "shifted", "exped", "picked", "counted"))
        with nc.Block() as block:
            @block.vector
            def _(v):
                c = Chain(v, steps)
                link = c.link

                def first_max(values, largest, onehot):
                    link(v.tensor_tensor(a1, values, spread(largest, EXP), ALU.is_equal))
                    link(v.tensor_scalar(a1, a1, -float(EXP), float(EXP), ALU.mult, ALU.add))
                    link(v.tensor_tensor(a1, a1, io8, ALU.add))
                    link(v.tensor_reduce(ix, a1, AX.X, ALU.min))
                    link(v.tensor_tensor(onehot, io8, spread(ix, EXP), ALU.is_equal))

                link(v.tensor_reduce(mx, lg, AX.X, ALU.max))
                if l in (0, 2):
                    v.tensor_tensor(ev, lg, spread(mx, EXP), ALU.subtract).then_inc(shifted, 1)
                    v.wait_ge(exped, 1)
                    link(v.tensor_reduce(sm, ev, AX.X, ALU.add))
                    link(v.reciprocal(sm, sm))
                    if l == 2:
                        v.tensor_tensor(cf, ev, spread(sm, EXP), ALU.mult)
                        return
                    link(v.tensor_reduce(mx, ev, AX.X, ALU.max))
                    first_max(ev, mx, oh)
                    v.sem_inc(picked, 1)
                    v.wait_ge(counted, 1)
                    link(v.memset(T[:, 2, 0:NBLK], 0.0))
                    tot = v3(ps[:B, 256:256 + G])
                    for e in range(EXP):
                        link(v.tensor_tensor_scan(a2[:, :, e], tot[:, :, e], T[:, 2, 0:NBLK], 0.0, ALU.add, ALU.add))
                    link(v.tensor_tensor(a2, a2, tot, ALU.subtract))
                    link(v.tensor_tensor(a2, a2, v3(ps[:B, 0:G]), ALU.add))
                    link(v.tensor_scalar(a2, a2, float(CAP), None, ALU.is_le))
                    link(v.tensor_tensor(a2, a2, oh, ALU.mult))
                    link(v.tensor_tensor(t1, mx, sm, ALU.mult))
                    v.tensor_tensor(cf, a2, spread(t1, EXP), ALU.mult)
                    return
                first_max(lg, mx, oh)
                link(v.scalar_tensor_tensor(a3, oh, -BIG, lg, ALU.mult, ALU.add))
                link(v.tensor_reduce(sm, a3, AX.X, ALU.max))
                first_max(a3, sm, a2)
                if l == 3:
                    v.tensor_tensor(cf, oh, a2, ALU.add)
                    return
                v.tensor_tensor(t1, sm, mx, ALU.subtract).then_inc(shifted, 1)
                v.wait_ge(exped, 1)
                link(v.tensor_scalar(sm, t1, 1.0, None, ALU.add))
                link(v.reciprocal(w1, sm))
                link(v.tensor_tensor(t1, t1, w1, ALU.mult))
                link(v.tensor_tensor(a1, oh, spread(w1, EXP), ALU.mult))
                link(v.tensor_tensor(a2, a2, spread(t1, EXP), ALU.mult))
                v.tensor_tensor(cf, a1, a2, ALU.add)

            @block.scalar
            def _(act):
                if l in (0, 2):
                    act.wait_ge(shifted, 1)
                    act.activation(E, E, ACT.Exp).then_inc(exped, 1)
                if l == 1:
                    act.wait_ge(shifted, 1)
                    act.activation(t1, t1, ACT.Exp).then_inc(exped, 1)

            @block.tensor
            def _(pe):
                if l == 0:
                    pe.wait_ge(picked, 1)
                    pe.matmul(ps[:B, 0:G], m.cst[:B, C_UPTO:C_UPTO + B], OH, start=True, stop=True)
                    pe.matmul(ps[:B, 256:256 + G], m.cst[:B, C_ONE:C_ONE + B], OH, start=True,
                              stop=True).then_inc(counted, 1)


def ffn(nc, m, l, XN):
    F, func = FFN[l]["F"], FFN[l]["act"]
    FC = F // P
    LG = m.small[:B, 0:NBLK * EXP]
    coef = m.small[:B, 200:200 + NBLK * EXP]
    XT = m.bufa[:, 0:2 * NODES]
    gb = m.rows[:B, row_at({0: "L0_ffn_gate_b", 1: "L1_ffn_bg", 2: "L2_ffn_br", 3: "L3_ffn_bg"}[l]):][:, 0:EXP]
    token_linear(nc, m, XN, m.a[GATES[l]], EXP,
                 lambda v, t, ps: v.tensor_tensor(LG[:, ds(t * EXP, EXP)], ps, gb, ALU.add), keep=XT)
    if l == 1:
        with nc.cleanup_on_exit():
            with nc.Block() as block:
                @block.vector
                def _(v):
                    lg = LG.rearrange("p (t e) -> p t e", e=EXP)
                    b = m.rows[:B, row_at("L1_ffn_bias"):][:, 0:EXP].unsqueeze(1).broadcast_to([B, NBLK, EXP])
                    v.tensor_tensor(lg, lg, b, ALU.add)
    gates(nc, m, l, LG, coef)
    Y = m.bufb[:B, XW:2 * XW] if l == 0 else m.X[:, :]
    bias_out(nc, m, l, coef, Y, l == 0)
    experts(nc, m, l, XT, coef, Y)
    if l == 0:
        finite_residual(nc, m, Y)


def bias_out(nc, m, l, coef, Y, fresh):
    with nc.cleanup_on_exit():
        sb, sem = m.sb, m.sem
        b2 = sb("b2", [EXP, D], F32)
        st = sb("st", [B, TU, EXP], F32)
        cT = sb("cT", [EXP, TU, B], F32)
        ps = [m.psum(f"ps{i}") for i in range(TU)]
        w_in, staged, turned, lifted, product, added = (
            sem(n) for n in ("w_in", "staged", "turned", "lifted", "product", "added"))
        with nc.Block() as block:
            @block.sync
            def _(sp):
                sp.dma_start(b2[:, :], m.a[B2S[l]]).then_inc(w_in, 16)
                sp.wait_ge(w_in, 16)

            @block.vector
            def _(v):
                v.sem_inc(added, TU)
                with v.Fori(0, NBLK // TU) as i:
                    v.wait_ge(turned, i * TU)
                    for k in range(TU):
                        v.tensor_scalar(st[:, k, :], coef[:, ds((i * TU + k) * EXP, EXP)], 1.0, None,
                                        ALU.mult).then_inc(staged, 1)
                    for k in range(TU):
                        v.wait_ge(product, i * TU + (k + 1))
                        y = Y[:, ds((i * TU + k) * D, D)]
                        if fresh:
                            v.tensor_scalar(y, ps[k][:B, P:P + D], 1.0, None, ALU.mult).then_inc(added, 1)
                        else:
                            v.tensor_tensor(y, y, ps[k][:B, P:P + D], ALU.add).then_inc(added, 1)

            @block.scalar
            def _(act):
                with act.Fori(0, NBLK // TU) as i:
                    for k in range(TU):
                        act.wait_ge(turned, i * TU + (k + 1))
                        act.wait_ge(product, i * TU)
                        act.activation(cT[:, k, :], ps[k][:EXP, 0:B], ACT.Copy).then_inc(lifted, 1)

            @block.tensor
            def _(pe):
                pe.wait_ge(w_in, 16)
                with pe.Fori(0, NBLK // TU) as i:
                    for k in range(TU):
                        pe.wait_ge(staged, i * TU + (k + 1))
                        pe.wait_ge(added, i * TU + (k + 1))
                        pe.transpose(ps[k][:EXP, 0:B], st[:, k, :], m.cst[:B, C_ID:C_ID + B]).then_inc(turned, 1)
                    for k in range(TU):
                        pe.wait_ge(lifted, i * TU + (k + 1))
                        pe.matmul(ps[k][:B, P:P + D], cT[:, k, :], b2[:, :], start=True,
                                  stop=True).then_inc(product, 1)


HALVES = [(0, 3), (3, 2)]
CH = NBLK // TU


def experts(nc, m, l, XT, coef, Y):
    F, func = FFN[l]["F"], FFN[l]["act"]
    FC = F // P
    deep = l == 2
    layers = 2 if deep else 1
    with nc.cleanup_on_exit():
        sb, sem = m.sb, m.sem
        w1 = [m.bufb[:, k * 2 * F:(k + 1) * 2 * F].rearrange("p (c f) -> p c f", c=2) for k in range(2)]
        wm = [sb(f"wm_{k}", [P, 2, F], F32) for k in range(2)] if deep else None
        w2 = [sb(f"w2_{k}", [P, FC, D], F32) for k in range(2)]
        ht = [m.bufa[:, 2 * NODES + k * FC * 375:2 * NODES + (k + 1) * FC * 375] for k in range(2)]
        ht2 = [m.bufa[:, 2 * NODES + (2 + k) * FC * 375:2 * NODES + (3 + k) * FC * 375] for k in range(2)] if deep else None
        sc = sb("sc", [P, 4, EXP * FC], F32) if deep else None
        psh = [m.psum(f"psh{i}") for i in range(4)]
        psy = [m.psum(f"psy{i}") for i in range(4)]
        w_in = [sem(f"w_in{k}") for k in range(2)]
        h_ready, h_done, y_ready, y_done = (sem(n) for n in ("h_ready", "h_done", "y_ready", "y_done"))
        scaled, steps, variances, stds = sem("scaled"), sem("steps"), sem("variances"), sem("stds")
        ndma = 3 if deep else 2
        b1 = m.cols[:, col_at(f"L{l}_ffn_b1"):][:, 0:EXP * FC]
        HB = FC * layers
        with nc.Block() as block:
            @block.sync
            def _(sp):
                def load_expert(e, k):
                    sp.dma_start(w1[k], m.a[f"L{l}_ffn_W1"][ds(e, 1)].rearrange(
                        "a p c f -> (a p) c f")).then_inc(w_in[k], 16)
                    if deep:
                        sp.dma_start(wm[k][:, :, :], m.a["L2_ffn_Wm"][ds(e, 1)].rearrange(
                            "a p c f -> (a p) c f")).then_inc(w_in[k], 16)
                    sp.dma_start(w2[k][:, :, :], m.a[f"L{l}_ffn_W2"][ds(e, 1)].rearrange(
                        "a p c f -> (a p) c f")).then_inc(w_in[k], 16)

                for k in range(2):
                    load_expert(k, k)
                with sp.Fori(1, EXP // 2) as e2:
                    for k in range(2):
                        sp.wait_ge(y_ready, (e2 * 2 + k) * NBLK - NBLK + YR)
                        load_expert(e2 * 2 + k, k)
                for k in range(2):
                    sp.wait_ge(w_in[k], 16 * ndma * (EXP // 2))

            @block.tensor
            def _(pe):
                pe.sem_inc(y_ready, YR)
                with pe.Fori(0, EXP // 2) as e2:
                    for k in range(2):
                        hold(pe, w_in[k], e2 * (16 * ndma) + 16 * ndma)
                        with pe.Fori(0, CH) as c:
                            for half, (t0, tn) in enumerate(HALVES):
                                u = ((e2 * 2 + k) * CH + c) * 2 + half
                                n = tn * B
                                for f in range(FC):
                                    pe.wait_ge(h_done, u * HB + (f + 1))
                                    for h in range(2):
                                        mm = pe.matmul(psh[f % 4][:, 0:n], w1[k][:, h, f * P:(f + 1) * P],
                                                       XT[:, ds(c * (TU * B) + (h * NODES + t0 * B), n)],
                                                       start=(h == 0), stop=(h == 1))
                                    mm.then_inc(h_ready, 1)
                                src = ht[half]
                                if deep:
                                    for f in range(FC):
                                        pe.wait_ge(h_done, u * HB + (FC + 4))
                                        for h in range(FC):
                                            mm = pe.matmul(psh[(FC + f) % 4][:, 0:n], wm[k][:, h, f * P:(f + 1) * P],
                                                           src[:, h * 375:h * 375 + n], start=(h == 0),
                                                           stop=(h == FC - 1))
                                        mm.then_inc(h_ready, 1)
                                    src = ht2[half]
                                pe.wait_ge(h_done, u * HB + (HB + 4))
                                for t in range(tn):
                                    pe.wait_ge(y_done, ((e2 * 2 + k) * CH + c) * TU + (t0 + t + 1 if t0 + t else YB))
                                    for f in range(FC):
                                        mm = pe.matmul(psy[(t0 + t) % 4][:B, 0:D],
                                                       src[:, f * 375 + t * B:f * 375 + (t + 1) * B],
                                                       w2[k][:, f, :], start=(f == 0), stop=(f == FC - 1))
                                    mm.then_inc(y_ready, 1)

            @block.scalar
            def _(act):
                act.sem_inc(h_done, 4)
                if deep:
                    act.wait_ge(variances, 1)
                    act.activation(sc[:, 0:1, :], sc[:, 0:1, :], ACT.Sqrt, bias=m.cst[:, C_EPS + 1:C_EPS + 2])
                    act.activation(sc[:, 2:3, :], sc[:, 2:3, :], ACT.Sqrt,
                                   bias=m.cst[:, C_EPS + 1:C_EPS + 2]).then_inc(stds, 1)
                    act.wait_ge(scaled, 1)
                with act.Fori(0, EXP * CH) as ec:
                    for half, (t0, tn) in enumerate(HALVES):
                        u = ec * 2 + half
                        n = tn * B
                        hold(act, y_ready, ec * TU + (t0 + tn) - TU + YR)
                        for lay in range(layers):
                            dst = (ht, ht2)[lay][half]
                            for f in range(FC):
                                at = (ec // CH) * FC + f
                                hold(act, h_ready, u * HB + (lay * FC + f + 1))
                                if deep:
                                    act.activation(dst[:, f * 375:f * 375 + n], psh[(lay * FC + f) % 4][:, 0:n], func,
                                                   bias=sc[:, 2 * lay + 1, ds(at, 1)],
                                                   scale=sc[:, 2 * lay, ds(at, 1)]).then_inc(h_done, 1)
                                else:
                                    act.activation(dst[:, f * 375:f * 375 + n], psh[f % 4][:, 0:n], func,
                                                   bias=b1[:, ds(at, 1)]).then_inc(h_done, 1)

            @block.vector
            def _(v):
                ch = Chain(v, steps)
                link = ch.link
                if deep:
                    col = lambda n: m.cols[:, col_at(f"L2_ffn_{n}"):][:, 0:EXP * FC]
                    link(v.tensor_copy(sc[:, 0, :], col("v1")))
                    link(v.tensor_copy(sc[:, 2, :], col("v2")))
                    v.sem_inc(variances, 1)
                    v.wait_ge(stds, 1)
                    for i in range(2):
                        s, t = sc[:, 2 * i, :], sc[:, 2 * i + 1, :]
                        link(v.reciprocal(s, s))
                        link(v.tensor_tensor(s, s, col(f"g{i + 1}"), ALU.mult))
                        link(v.tensor_tensor(t, col(f"b{i + 1}"), col(f"m{i + 1}"), ALU.subtract))
                        link(v.tensor_tensor(t, t, s, ALU.mult))
                        link(v.tensor_tensor(t, t, col(f"be{i + 1}"), ALU.add))
                    v.sem_inc(scaled, 1)
                v.sem_inc(y_done, YB)
                with v.Fori(0, EXP * CH) as ec:
                    for t in range(TU):
                        tile = (ec % CH) * TU + t
                        y = Y[:, ds(tile * D, D)]
                        v.wait_ge(y_ready, ec * TU + (t + 1 + YR))
                        v.scalar_tensor_tensor(y, psy[t % 4][:B, 0:D], coef[:, ds(tile * EXP + ec // CH, 1)], y,
                                               ALU.mult, ALU.add).then_inc(y_done, 1)


YB = 4
YR = TU


def finite_residual(nc, m, Y):
    T = m.bufa[:B, 0:XW]
    big = 3.4028234663852886e38
    with nc.cleanup_on_exit():
        steps = m.sem("steps")
        mask = m.bufa[:B, XW:2 * XW].bitcast(I32)
        with nc.Block() as block:
            @block.vector
            def _(v):
                c = Chain(v, steps)
                c.link(v.memset(T, 0.0))
                c.link(v.tensor_tensor(mask, Y, Y, ALU.is_equal))
                c.link(v.copy_predicated(T, mask, Y))
                c.link(v.tensor_scalar(mask, T, big, None, ALU.is_gt))
                c.link(v.memset(Y, 1e4))
                c.link(v.copy_predicated(T, mask, Y))
                c.link(v.tensor_scalar(mask, T, -big, None, ALU.is_lt))
                c.link(v.memset(Y, -1e4))
                c.link(v.copy_predicated(T, mask, Y))
                v.tensor_tensor(m.X[:, :], m.X[:, :], T, ALU.add)


def gcn(nc, m, XN):
    dinv = m.small[:B, 1330:1355]
    HT = m.bufb[:, 0:4 * NODES]
    bns = m.small[:, 400:416]
    with nc.cleanup_on_exit():
        rooted = m.sem("rooted")
        with nc.Block() as block:
            @block.scalar
            def _(act):
                act.activation(dinv, m.deg, ACT.Sqrt, bias=m.cst[:B, C_ONE:C_ONE + 1]).then_inc(rooted, 1)

            @block.vector
            def _(v):
                v.wait_ge(rooted, 1)
                v.reciprocal(dinv, dinv).then_inc(rooted, 1)
                v.wait_ge(rooted, 2)
                with v.Fori(0, NBLK // TU) as i:
                    for k in range(TU):
                        t = i * TU + k
                        v.tensor_scalar(m.bufa[:B, ds(t * D, D)], XN[:, ds(t * D, D)], dinv[:, ds(t, 1)], None,
                                        ALU.mult)
    agg = m.bufa[:B, 0:XW]
    store_table(nc, m, agg, m.table, D)
    aggregate(nc, m, "dst", m.table, D, False, False)
    vT = m.bufa[:, XW:XW + 2 * NODES]
    to_features(nc, m, agg, D, dinv, vT, None)
    feature_linear(nc, m, vT, "L1_gnn_W1", m.cols[:, col_at("L1_gnn_b1"):][:, 0:4], HT)
    batch_stats(nc, m, HT, 1, bns)
    wide_agg = m.bufa[:B, 0:NBLK * HID]
    bn_linear(nc, m, HT, bns, "L1_gnn_W2", HID, dinv, wide_agg)
    store_table(nc, m, wide_agg, m.table2, HID)
    aggregate(nc, m, "dst", m.table2, HID, False, False)
    to_features(nc, m, wide_agg, HID, dinv, HT, m.cols[:, col_at("L1_gnn_b2"):][:, 0:4])
    batch_stats(nc, m, HT, 2, bns)
    bn_linear(nc, m, HT, bns, "L1_gnn_W3", D, dinv, agg)
    store_table(nc, m, agg, m.table, D)
    aggregate(nc, m, "dst", m.table, D, False, False)
    with nc.cleanup_on_exit():
        steps = m.sem("steps")
        with nc.Block() as block:
            @block.vector
            def _(v):
                c = Chain(v, steps)
                b3 = m.rows[:B, row_at("L1_gnn_b3"):][:, 0:D].unsqueeze(1).broadcast_to([B, NBLK, D])
                xv = m.X[:, :].rearrange("p (t w) -> p t w", w=D)
                with v.Fori(0, NBLK // TU) as i:
                    c.enter(i, 1)
                    for k in range(TU):
                        t = i * TU + k
                        x = m.X[:, ds(t * D, D)]
                        last = v.scalar_tensor_tensor(x, agg[:, ds(t * D, D)], dinv[:, ds(t, 1)], x, ALU.mult, ALU.add)
                    c.link(last)
                c.leave(NBLK // TU)
                v.tensor_tensor(xv, xv, b3, ALU.add)


def to_features(nc, m, src, width, scale, dst, bias):
    KC = width // P
    with nc.cleanup_on_exit():
        st = m.sb("st", [B, TU, width], F32)
        ps = [m.psum(f"ps{i}") for i in range(TU)]
        staged, turned, lifted = m.sem("staged"), m.sem("turned"), m.sem("lifted")
        with nc.Block() as block:
            @block.vector
            def _(v):
                with v.Fori(0, NBLK // TU) as i:
                    v.wait_ge(turned, i * TU)
                    for k in range(TU):
                        t = i * TU + k
                        v.tensor_scalar(st[:, k, :], src[:, ds(t * width, width)], scale[:, ds(t, 1)], None,
                                        ALU.mult).then_inc(staged, 1)

            @block.tensor
            def _(pe):
                with pe.Fori(0, NBLK // TU) as i:
                    for k in range(TU):
                        pe.wait_ge(staged, i * TU + (k + 1))
                        pe.wait_ge(lifted, i * TU + (k + 1))
                        for h in range(KC):
                            tr = pe.transpose(ps[k][:, h * B:(h + 1) * B], st[:, k, h * P:(h + 1) * P],
                                              m.cst[:B, C_ID:C_ID + B])
                        tr.then_inc(turned, 1)

            @block.scalar
            def _(act):
                act.sem_inc(lifted, TU)
                with act.Fori(0, NBLK // TU) as i:
                    for k in range(TU):
                        t = i * TU + k
                        hold(act, turned, t + 1)
                        for h in range(KC):
                            o = dst[:, ds(t * B + h * NODES, B)]
                            pt = ps[k][:, h * B:(h + 1) * B]
                            if bias is None:
                                up = act.activation(o, pt, ACT.Copy)
                            else:
                                up = act.activation(o, pt, ACT.Identity, bias=bias[:, h:h + 1])
                        up.then_inc(lifted, 1)


def feature_linear(nc, m, src, wname, bias, dst):
    with nc.cleanup_on_exit():
        w = m.sb("w", [P, 2, HID], F32)
        ps = [m.psum(f"ps{i}") for i in range(8)]
        w_in, ready, lifted = m.sem("w_in"), m.sem("ready"), m.sem("lifted")
        with nc.Block() as block:
            @block.sync
            def _(sp):
                sp.dma_start(w[:, :, :], m.a[wname]).then_inc(w_in, 16)
                sp.wait_ge(w_in, 16)

            @block.tensor
            def _(pe):
                pe.wait_ge(w_in, 16)
                with pe.Fori(0, CH) as c:
                    for half, (t0, tn) in enumerate(HALVES):
                        for f in range(4):
                            pe.wait_ge(lifted, c * 8 + (half * 4 + f + 1))
                            for h in range(2):
                                mm = pe.matmul(ps[half * 4 + f][:, 0:tn * B], w[:, h, f * P:(f + 1) * P],
                                               src[:, ds(c * (TU * B) + (h * NODES + t0 * B), tn * B)],
                                               start=(h == 0), stop=(h == 1))
                            mm.then_inc(ready, 1)

            @block.scalar
            def _(act):
                act.sem_inc(lifted, 8)
                with act.Fori(0, CH) as c:
                    for half, (t0, tn) in enumerate(HALVES):
                        for f in range(4):
                            hold(act, ready, c * 8 + (half * 4 + f + 1))
                            act.activation(dst[:, ds(c * (TU * B) + (f * NODES + t0 * B), tn * B)],
                                           ps[half * 4 + f][:, 0:tn * B], ACT.Identity,
                                           bias=bias[:, f:f + 1]).then_inc(lifted, 1)


def batch_stats(nc, m, HT, n, bns):
    with nc.cleanup_on_exit():
        st = m.sb("st", [P, 4, 2 * CH, 6], F32)
        mv = m.sb("mv", [P, 4, 2], F32)
        std = m.sb("std", [P, 4], F32)
        steps, var_ready, std_ready = m.sem("steps"), m.sem("var_ready"), m.sem("std_ready")
        with nc.Block() as block:
            @block.vector
            def _(v):
                c = Chain(v, steps)
                for ch in range(2 * CH):
                    t0, tn = HALVES[ch % 2]
                    at = (ch // 2) * TU * B + t0 * B
                    for f in range(4):
                        last = v.bn_stats(st[:, f, ch, :], HT[:, f * NODES + at:f * NODES + at + tn * B])
                c.link(last)
                for f in range(4):
                    last = v.bn_aggr(mv[:, f, :], st[:, f, :, :].rearrange("p c s -> p (c s)"))
                last.then_inc(var_ready, 1)
                v.wait_ge(std_ready, 1)
                c.link(v.reciprocal(std[:, :], std[:, :]))
                g = m.cols[:, col_at(f"L1_gnn_g{n}"):][:, 0:4]
                be = m.cols[:, col_at(f"L1_gnn_be{n}"):][:, 0:4]
                c.link(v.tensor_tensor(bns[:, 0:4], std[:, :], g, ALU.mult))
                c.link(v.tensor_tensor(std[:, :], mv[:, :, 0], bns[:, 0:4], ALU.mult))
                v.tensor_tensor(bns[:, 4:8], be, std[:, :], ALU.subtract)

            @block.scalar
            def _(act):
                act.wait_ge(var_ready, 1)
                act.activation(std[:, :], mv[:, :, 1], ACT.Sqrt,
                               bias=m.cst[:, C_EPS:C_EPS + 1]).then_inc(std_ready, 1)


def bn_linear(nc, m, HT, bns, wname, wide, dinv, dst):
    with nc.cleanup_on_exit():
        w = m.sb("w", [P, 4, wide], F32)
        st = m.sb("st", [P, TU, 4 * B], F32)
        ps = [m.psum(f"ps{i}") for i in range(TU)]
        w_in, staged, product, taken = m.sem("w_in"), m.sem("staged"), m.sem("product"), m.sem("taken")
        with nc.Block() as block:
            @block.sync
            def _(sp):
                sp.dma_start(w[:, :, :], m.a[wname]).then_inc(w_in, 16)
                sp.wait_ge(w_in, 16)

            @block.scalar
            def _(act):
                with act.Fori(0, NBLK // TU) as i:
                    hold(act, product, i * TU + TU)
                    for k in range(TU):
                        for f in range(4):
                            up = act.activation(st[:, k, f * B:(f + 1) * B],
                                                HT[:, ds((i * TU + k) * B + f * NODES, B)], ACT.Relu,
                                                bias=bns[:, 4 + f:5 + f], scale=bns[:, f:f + 1])
                        up.then_inc(staged, 1)

            @block.tensor
            def _(pe):
                pe.sem_inc(product, TU)
                pe.wait_ge(w_in, 16)
                with pe.Fori(0, NBLK // TU) as i:
                    for k in range(TU):
                        pe.wait_ge(staged, i * TU + (k + 1))
                        pe.wait_ge(taken, i * TU + (k + 1))
                        for f in range(4):
                            mm = pe.matmul(ps[k][:B, 0:wide], st[:, k, f * B:(f + 1) * B], w[:, f, :],
                                           start=(f == 0), stop=(f == 3))
                        mm.then_inc(product, 1)

            @block.vector
            def _(v):
                v.sem_inc(taken, TU)
                with v.Fori(0, NBLK // TU) as i:
                    for k in range(TU):
                        t = i * TU + k
                        v.wait_ge(product, i * TU + (k + 1 + TU))
                        v.tensor_scalar(dst[:, ds(t * wide, wide)], ps[k][:B, 0:wide], dinv[:, ds(t, 1)], None,
                                        ALU.mult).then_inc(taken, 1)


GU = 4


def gat(nc, m, l, XN):
    H = 8 if l == 2 else 4
    C = D // H
    W = D + H
    HB = m.bufa[:B, 0:NBLK * W]
    hb3 = HB.rearrange("p (t w) -> p t w", w=W)
    acc = m.bufb[:B, NT * 8:NT * 8 + NBLK * W]
    acc3 = acc.rearrange("p (t w) -> p t w", w=W)
    alpha = m.bufb[:, 0:NT * H]
    M = m.small[:B, 0:NBLK * H]
    asrc = m.small[:B, 200:200 + NBLK * H]
    self_e = m.small[:B, 400:400 + NBLK * H]
    names = {2: ("L2_gnn_a_src", "L2_gnn_a_dst", "L2_gnn_bias"),
             3: ("L3_gnn_att_src", "L3_gnn_att_dst", "L3_gnn_bias")}[l]
    vec = [m.rows[:B, row_at(n):][:, 0:D].unsqueeze(1).broadcast_to([B, NBLK, D]) for n in names]
    t3 = lambda ap: ap.rearrange("p (t h) -> p t h", h=H)
    token_linear(nc, m, XN, m.a[f"L{l}_gnn_W"], D,
                 lambda v, t, ps: v.tensor_scalar(HB[:, ds(t * W, D)], ps, 1.0, None, ALU.mult))
    with nc.cleanup_on_exit():
        steps, tables = m.sem("steps"), m.sem("tables")
        ready = m.sem("ready")
        tmp = m.bufb[:B, 0:XW]
        with nc.Block() as block:
            @block.vector
            def _(v):
                c = Chain(v, steps)
                tv = tmp.rearrange("p (t w) -> p t w", w=D)
                c.link(v.tensor_tensor(tv, hb3[:, :, 0:D], vec[0], ALU.mult))
                v.tensor_reduce(asrc, tmp.rearrange("p (q c) -> p q c", c=C), AX.X, ALU.add).then_inc(ready, 1)
                v.wait_ge(ready, 1)
                c.link(v.tensor_tensor(tv, hb3[:, :, 0:D], vec[1], ALU.mult))
                c.link(v.tensor_reduce(self_e, tmp.rearrange("p (q c) -> p q c", c=C), AX.X, ALU.add))
                c.link(v.tensor_scalar(hb3[:, :, D:W], t3(self_e), 1.0, None, ALU.mult))
                if l == 2:
                    v.memset(M, -BIG)
                    v.memset(acc, 0.0)
                else:
                    c.link(v.tensor_tensor(self_e, self_e, asrc, ALU.add))
                    c.link(v.scalar_tensor_tensor(self_e, self_e, 0.2, self_e, ALU.mult, ALU.max))
                    v.tensor_copy(M, self_e)

            @block.sync
            def _(sp):
                sp.dma_start(m.table.rearrange("(t p) w -> p t w", p=B), hb3[:, :, 0:D]).then_inc(tables, 16)
                sp.wait_ge(ready, 1)
                sp.dma_start(m.tablea[H].rearrange("(t p) w -> p t w", p=B), t3(asrc)).then_inc(tables, 16)
                sp.wait_ge(tables, 32)
    edge_scores(nc, m, H, l == 2, HB, W, alpha)
    edge_maxima(nc, m, H, alpha, M)
    if l == 3:
        with nc.cleanup_on_exit():
            steps, shifted, exped = m.sem("steps"), m.sem("shifted"), m.sem("exped")
            with nc.Block() as block:
                @block.vector
                def _(v):
                    v.tensor_tensor(self_e, self_e, M, ALU.subtract).then_inc(shifted, 1)
                    v.wait_ge(exped, 1)
                    v.tensor_scalar(acc3[:, :, D:W], t3(self_e), 1.0, None, ALU.mult)
                    with v.Fori(0, NBLK) as t:
                        for h in range(H):
                            v.tensor_scalar(acc[:, ds(t * W + h * C, C)], HB[:, ds(t * W + h * C, C)],
                                            self_e[:, ds(t * H + h, 1)], None, ALU.mult)

                @block.scalar
                def _(act):
                    act.wait_ge(shifted, 1)
                    act.activation(self_e, self_e, ACT.Exp).then_inc(exped, 1)
    edge_messages(nc, m, H, alpha, M, acc, W)
    with nc.cleanup_on_exit():
        steps, squared, rooted = m.sem("steps"), m.sem("squared"), m.sem("rooted")
        inv = M
        o = m.bufa[:B, 0:XW]
        ov = o.rearrange("p (t w) -> p t w", w=D)
        ss = m.small[:B, 700:700 + NBLK]
        with nc.Block() as block:
            @block.vector
            def _(v):
                c = Chain(v, steps)
                c.link(v.tensor_scalar(t3(inv), acc3[:, :, D:W], 1e-10, None, ALU.max))
                c.link(v.reciprocal(inv, inv))
                with v.Fori(0, NBLK) as t:
                    c.enter(t, 1)
                    for h in range(H):
                        last = v.tensor_scalar(o[:, ds(t * D + h * C, C)], acc[:, ds(t * W + h * C, C)],
                                               inv[:, ds(t * H + h, 1)], None, ALU.mult)
                    c.link(last)
                c.leave(NBLK)
                c.link(v.tensor_tensor(ov, ov, vec[2], ALU.add))
                if l == 3:
                    sq = acc[:, 0:XW]
                    c.link(v.tensor_scalar(o, o, 0.0, None, ALU.max))
                    c.link(v.tensor_tensor(sq, o, o, ALU.mult))
                    v.tensor_reduce(ss, sq.rearrange("p (t w) -> p t w", w=D), AX.X, ALU.add).then_inc(squared, 1)
                    v.wait_ge(rooted, 1)
                    c.link(v.tensor_scalar(ss, ss, 1e-12, None, ALU.max))
                    c.link(v.reciprocal(ss, ss))
                    with v.Fori(0, NBLK) as t:
                        x = m.X[:, ds(t * D, D)]
                        v.scalar_tensor_tensor(x, o[:, ds(t * D, D)], ss[:, ds(t, 1)], x, ALU.mult, ALU.add)
                else:
                    v.tensor_tensor(m.X[:, :], m.X[:, :], o, ALU.add)

            @block.scalar
            def _(act):
                if l == 3:
                    act.wait_ge(squared, 1)
                    act.activation(ss, ss, ACT.Sqrt).then_inc(rooted, 1)


def edge_scores(nc, m, H, encoded, HB, W, alpha):
    lst = m.lists["dst"][:, :].rearrange("p (c f) -> p c f", f=PF)
    n0 = 0 if encoded else D
    NW = W - n0
    C = D // H
    with nc.cleanup_on_exit():
        sb, sem, psum = m.sb, m.sem, m.psum
        idx, sums = sb("idx", [P, GU], I32), sb("sums", [P, GU, H], F32)
        asg = sb("asg", [P, GU, H], F32)
        onehot, onehotT = sb("onehot", [P, GU, B], F32), sb("onehotT", [B, GU, P], F32)
        rec, recT = sb("rec", [P, GU, PF], F32), sb("recT", [PF, GU, P], F32)
        enc, prod = sb("enc", [P, GU, D], F32), sb("prod", [P, GU, D], F32)
        ew = sb("ew", [PF, D], F32)
        pt, pw, pe_ = ([psum(f"{n}{i}") for i in range(2)] for n in ("pt", "pw", "pe"))
        idx_ready, hot_ready, turned, lifted = sem("idx_ready"), sem("hot_ready"), sem("turned"), sem("lifted")
        spread_done, enc_done, combined, steps = sem("spread_done"), sem("enc_done"), sem("combined"), sem("steps")
        w_in = sem("w_in")
        gathered = [sem(f"gathered{k}") for k in range(GU)]
        rounds = NT // GU
        with nc.Block() as block:
            @block.sync
            def _(sp):
                sp.dma_start(ew[:, :], m.a["edge_w"]).then_inc(w_in, 16)
                sp.wait_ge(w_in, 16)

            @block.gpsimd
            def _(pool):
                with pool.Fori(0, rounds) as i:
                    hold(pool, idx_ready, i + 1)
                    for k in range(GU):
                        pool.indirect_dma_start(
                            out=asg[:, k, :], out_offset=None, in_=m.tablea[H],
                            in_offset=bass.IndirectOffsetOnAxis(ap=idx[:, k:k + 1], axis=0)).then_inc(gathered[k], 16)

            @block.vector
            def _(v):
                c = Chain(v, steps)
                v.sem_inc(combined, 2)
                per = (3 if encoded else 1) * GU
                with v.Fori(0, rounds) as i:
                    c.enter(i, per)
                    v.tensor_scalar(idx[:, :], lst[:, ds(i * GU, GU), 0].bitcast(I32), 0, None,
                                    ALU.bitwise_or).then_inc(idx_ready, 1)
                    for k in range(GU):
                        one = v.tensor_scalar(onehot[:, k, :], m.cst[:, C_IOTA:C_IOTA + B],
                                              lst[:, ds(i * GU + k, 1), 1], None, ALU.is_equal)
                        if encoded:
                            one = v.tensor_scalar(rec[:, k, :].bitcast(I32),
                                                  lst[:, ds(i * GU + k, 1), :].rearrange("p c f -> p (c f)").bitcast(I32),
                                                  0, None, ALU.bitwise_or)
                        one.then_inc(hot_ready, 1)
                    for k in range(GU):
                        j = i * GU + k
                        s = sums[:, k, :]
                        tgt = pw[k % 2]
                        if encoded:
                            v.wait_ge(enc_done, j + 1)
                            c.link(v.tensor_tensor(prod[:, k, :], enc[:, k, :], tgt[:, 0:D], ALU.mult))
                            c.link(v.tensor_reduce(s, prod[:, k, :].rearrange("p (h c) -> p h c", c=C), AX.X, ALU.add))
                            v.tensor_tensor(s, s, tgt[:, D:W], ALU.add).then_inc(combined, 1)
                        else:
                            v.wait_ge(spread_done, j + (1 + GU))
                            v.tensor_scalar(s, tgt[:, 0:H], 1.0, None, ALU.mult).then_inc(combined, 1)
                        v.wait_ge(combined, j + 3)
                        v.wait_ge(gathered[k], i * 16 + 16)
                        c.link(v.tensor_tensor(s, s, asg[:, k, :], ALU.add))
                        v.scalar_tensor_tensor(alpha[:, ds(j * H, H)], s, 0.2, s, ALU.mult, ALU.max)
                c.leave(rounds)

            @block.tensor
            def _(pe):
                pe.sem_inc(spread_done, GU)
                pe.wait_ge(w_in, 16)
                with pe.Fori(0, rounds) as i:
                    for k in range(GU):
                        pe.wait_ge(hot_ready, i * GU + (k + 1))
                        pe.wait_ge(lifted, i * GU + (k + 1))
                        tr = pe.transpose(pt[k % 2][:B, 0:P], onehot[:, k, :], m.cst[:, C_ID:C_ID + P])
                        if encoded:
                            tr = pe.transpose(pt[k % 2][:PF, P:2 * P], rec[:, k, :], m.cst[:, C_ID:C_ID + P])
                        tr.then_inc(turned, 1)
                    for k in range(GU):
                        b = pe.value_load(m.blk["dst"][0:1, ds(i * GU + k, 1)], min_val=0, max_val=NBLK - 1)
                        pe.wait_ge(lifted, i * GU + (k + 3))
                        hold(pe, combined, i * GU + (k + 1))
                        mm = pe.matmul(pw[k % 2][:, 0:NW], onehotT[:, k, :], HB[:, ds(b * W + n0, NW)], start=True,
                                       stop=True)
                        if encoded:
                            mm = pe.matmul(pe_[k % 2][:, 0:D], recT[:, k, :], ew[:, :], start=True, stop=True)
                        mm.then_inc(spread_done, 1)

            @block.scalar
            def _(act):
                act.sem_inc(lifted, 2)
                with act.Fori(0, rounds) as i:
                    act.wait_ge(spread_done, i * GU + GU)
                    for k in range(GU):
                        act.wait_ge(turned, i * GU + (k + 1))
                        up = act.activation(onehotT[:, k, :], pt[k % 2][:B, 0:P], ACT.Copy)
                        if encoded:
                            up = act.activation(recT[:, k, :], pt[k % 2][:PF, P:2 * P], ACT.Copy)
                        up.then_inc(lifted, 1)
                    if encoded:
                        for k in range(GU):
                            act.wait_ge(spread_done, i * GU + (k + 1 + GU))
                            act.activation(enc[:, k, :], pe_[k % 2][:, 0:D], ACT.Relu).then_inc(enc_done, 1)


def edge_maxima(nc, m, H, alpha, M):
    lst = m.lists["dst"][:, :].rearrange("p (c f) -> p c f", f=PF)
    G = H // 4
    with nc.cleanup_on_exit():
        sb, sem, psum = m.sb, m.sem, m.psum
        onehot = sb("onehot", [P, GU, B], BF16)
        al, alT = sb("al", [P, GU, H], F32), sb("alT", [H, GU, P], F32)
        bigi, minus, ones = sb("bigi", [P, 4, P], BF16), sb("minus", [1, 4 * P], BF16), sb("ones", [1, B], BF16)
        sel = sb("sel", [H, H, B], F32)
        top = sb("top", [B, GU, H], F32)
        pt = [psum(f"pt{i}") for i in range(2)]
        pm = [[psum(f"pm{i}{g}") for g in range(G)] for i in range(2)]
        made, hot_ready, turned, lifted = sem("made"), sem("hot_ready"), sem("turned"), sem("lifted")
        masked, reduced, steps = sem("masked"), sem("reduced"), sem("steps")
        rounds = NT // GU
        with nc.Block() as block:
            @block.vector
            def _(v):
                c = Chain(v, steps)
                v.tensor_scalar(bigi[:, :, :], m.cst[:, C_ID:C_ID + P].unsqueeze(1).broadcast_to([P, 4, P]), BIG,
                                None, ALU.mult)
                v.memset(minus[:, :], -BIG)
                v.memset(ones[:, :], 1.0)
                v.tensor_scalar(sel[:, :, :], m.cst[:H, C_ID:C_ID + H].unsqueeze(2).broadcast_to([H, H, B]), 1.0,
                                None, ALU.mult).then_inc(made, 1)
                v.sem_inc(reduced, 2)
                with v.Fori(0, rounds) as i:
                    c.enter(i, GU)
                    for k in range(GU):
                        j = i * GU + k
                        v.tensor_scalar(al[:, k, :], alpha[:, ds(j * H, H)], 1.0, None, ALU.mult)
                        v.tensor_scalar(onehot[:, k, :], m.cst[:, C_IOTA:C_IOTA + B], lst[:, ds(j, 1), 1], None,
                                        ALU.is_equal).then_inc(hot_ready, 1)
                    for k in range(GU):
                        j = i * GU + k
                        b = v.value_load(m.blk["dst"][0:1, ds(j, 1)], min_val=0, max_val=NBLK - 1)
                        v.wait_ge(masked, j + 1)
                        for g in range(G):
                            r = v.tensor_reduce(top[:, k, 4 * g:4 * g + 4],
                                                pm[k % 2][g][:B, :].rearrange("p (h e) -> p h e", e=P), AX.X, ALU.max)
                        r.then_inc(reduced, 1)
                        v.wait_ge(reduced, j + 3)
                        part = M[:, ds(b * H, H)]
                        c.link(v.tensor_tensor(part, part, top[:, k, :], ALU.max))
                c.leave(rounds)

            @block.tensor
            def _(pe):
                pe.wait_ge(made, 1)
                with pe.Fori(0, rounds) as i:
                    for k in range(GU):
                        pe.wait_ge(hot_ready, i * GU + (k + 1))
                        pe.wait_ge(lifted, i * GU + (k + 1))
                        pe.transpose(pt[k % 2][:H, 0:P], al[:, k, :], m.cst[:, C_ID:C_ID + P]).then_inc(turned, 1)
                    for k in range(GU):
                        pe.wait_ge(lifted, i * GU + (k + 3))
                        pe.wait_ge(reduced, i * GU + (k + 1))
                        for g in range(G):
                            o = pm[k % 2][g][:B, :]
                            pe.matmul(o, onehot[:, k, :], bigi[:, :, :].rearrange("p a b -> p (a b)"), start=True,
                                      stop=False, skip_group_check=True)
                            pe.matmul(o, ones[:, :], minus[:, :], start=False, stop=False, skip_group_check=True)
                            for q in range(4):
                                mm = pe.matmul(o[:, q * P:(q + 1) * P], sel[:, 4 * g + q, :], alT[:, k, :],
                                               start=False, stop=(q == 3), skip_group_check=True)
                        mm.then_inc(masked, 1)

            @block.scalar
            def _(act):
                act.sem_inc(lifted, 2)
                with act.Fori(0, rounds) as i:
                    for k in range(GU):
                        act.wait_ge(turned, i * GU + (k + 1))
                        act.wait_ge(masked, i * GU)
                        act.activation(alT[:, k, :], pt[k % 2][:H, 0:P], ACT.Copy).then_inc(lifted, 1)


def edge_messages(nc, m, H, alpha, M, acc, W):
    lst = m.lists["dst"][:, :].rearrange("p (c f) -> p c f", f=PF)
    C = D // H
    with nc.cleanup_on_exit():
        sb, sem, psum = m.sb, m.sem, m.psum
        idx, rows = sb("idx", [P, GU], I32), sb("rows", [P, GU, D], F32)
        onehot, onehotT = sb("onehot", [P, GU, B], F32), sb("onehotT", [B, GU, P], F32)
        sh = sb("sh", [P, GU, H], F32)
        msg = sb("msg", [P, GU, W], F32)
        pt, pm, pa = ([psum(f"{n}{i}") for i in range(2)] for n in ("pt", "pm", "pa"))
        idx_ready, hot_ready, turned, lifted = sem("idx_ready"), sem("hot_ready"), sem("turned"), sem("lifted")
        spread_done, shifted, clamped, exped = sem("spread_done"), sem("shifted"), sem("clamped"), sem("exped")
        msg_ready, summed, added = sem("msg_ready"), sem("summed"), sem("added")
        gathered = [sem(f"gathered{k}") for k in range(GU)]
        rounds = NT // GU
        with nc.Block() as block:
            @block.gpsimd
            def _(pool):
                with pool.Fori(0, rounds) as i:
                    hold(pool, idx_ready, i + 1)
                    for k in range(GU):
                        pool.indirect_dma_start(
                            out=rows[:, k, :], out_offset=None, in_=m.table,
                            in_offset=bass.IndirectOffsetOnAxis(ap=idx[:, k:k + 1], axis=0)).then_inc(gathered[k], 16)

            @block.vector
            def _(v):
                v.sem_inc(added, 2)
                v.sem_inc(shifted, 2)
                with v.Fori(0, rounds) as i:
                    v.tensor_scalar(idx[:, :], lst[:, ds(i * GU, GU), 0].bitcast(I32), 0, None,
                                    ALU.bitwise_or).then_inc(idx_ready, 1)
                    for k in range(GU):
                        v.tensor_scalar(onehot[:, k, :], m.cst[:, C_IOTA:C_IOTA + B], lst[:, ds(i * GU + k, 1), 1],
                                        None, ALU.is_equal).then_inc(hot_ready, 1)
                    for k in range(GU):
                        j = i * GU + k
                        v.wait_ge(spread_done, j + 1)
                        v.tensor_tensor(sh[:, k, :], alpha[:, ds(j * H, H)], pm[k % 2][:, 0:H],
                                        ALU.subtract).then_inc(shifted, 1)
                        v.wait_ge(shifted, j + 3)
                        v.tensor_scalar(sh[:, k, :], sh[:, k, :], 0.0, None, ALU.min).then_inc(clamped, 1)
                    for k in range(GU):
                        v.wait_ge(exped, i * GU + (k + 1))
                        v.wait_ge(gathered[k], i * 16 + 16)
                        v.tensor_tensor(msg[:, k, 0:D].rearrange("p (h c) -> p h c", c=C),
                                        rows[:, k, :].rearrange("p (h c) -> p h c", c=C),
                                        spread(msg[:, k, D:W], C), ALU.mult).then_inc(msg_ready, 1)
                    for k in range(GU):
                        j = i * GU + k
                        b = v.value_load(m.blk["dst"][0:1, ds(j, 1)], min_val=0, max_val=NBLK - 1)
                        part = acc[:, ds(b * W, W)]
                        v.wait_ge(summed, j + 1)
                        v.tensor_tensor(part, part, pa[k % 2][:B, 0:W], ALU.add).then_inc(added, 1)
                        v.wait_ge(added, j + 3)

            @block.tensor
            def _(pe):
                with pe.Fori(0, rounds) as i:
                    for k in range(GU):
                        pe.wait_ge(hot_ready, i * GU + (k + 1))
                        pe.wait_ge(lifted, i * GU + (k + 1))
                        pe.transpose(pt[k % 2][:B, 0:P], onehot[:, k, :], m.cst[:, C_ID:C_ID + P]).then_inc(turned, 1)
                    for k in range(GU):
                        b = pe.value_load(m.blk["dst"][0:1, ds(i * GU + k, 1)], min_val=0, max_val=NBLK - 1)
                        pe.wait_ge(lifted, i * GU + (k + 3))
                        hold(pe, shifted, i * GU + (k + 1))
                        pe.matmul(pm[k % 2][:, 0:H], onehotT[:, k, :], M[:, ds(b * H, H)], start=True,
                                  stop=True).then_inc(spread_done, 1)
                    for k in range(GU):
                        pe.wait_ge(msg_ready, i * GU + (k + 1))
                        pe.wait_ge(added, i * GU + (k + 1))
                        pe.matmul(pa[k % 2][:B, 0:W], onehot[:, k, :], msg[:, k, :], start=True,
                                  stop=True).then_inc(summed, 1)

            @block.scalar
            def _(act):
                act.sem_inc(lifted, 2)
                with act.Fori(0, rounds) as i:
                    for k in range(GU):
                        act.wait_ge(turned, i * GU + (k + 1))
                        act.wait_ge(spread_done, i * GU)
                        act.activation(onehotT[:, k, :], pt[k % 2][:B, 0:P], ACT.Copy).then_inc(lifted, 1)
                    for k in range(GU):
                        act.wait_ge(clamped, i * GU + (k + 1))
                        act.activation(msg[:, k, D:W], sh[:, k, :], ACT.Exp).then_inc(exped, 1)


def spread_cols(v, fc):
    v = np.asarray(v).reshape(-1, fc, P)
    return np.ascontiguousarray(v.transpose(2, 0, 1).reshape(P, -1))


def consts():
    c = np.zeros((P, C_END), np.float32)
    c[:, C_ID:C_ID + P] = np.eye(P)
    c[:, C_IOTA:C_IOTA + P] = np.arange(P)
    r = np.arange(B)
    c[:B, C_STRICT:C_STRICT + B] = r[:, None] < r[None]
    c[:B, C_UPTO:C_UPTO + B] = r[:, None] <= r[None]
    c[:, C_ONE:C_ONE + P] = 1
    c[:, C_TILE:C_TILE + NT] = np.arange(NT)
    c[:, C_EPS] = LN_EPS
    c[:, C_EPS + 1] = FBN_EPS
    return c


def kernel(**inp):
    import concourse.bacc as bacc
    from concourse.bass_utils import run_bass_kernel_spmd

    v = {k: np.asarray(x) for k, x in inp.items()}
    arr = {"consts": consts(), "x": v["x"]}
    arr["src"] = v["src"].reshape(B, EC)
    arr["dst"] = v["dst"].reshape(B, EC)
    arr["attr"] = v["edge_attr_3"].reshape(B, EC * 3)
    flat = np.concatenate([v[n].reshape(-1) for n in ROWS + GATEB])
    arr["rows"] = np.broadcast_to(flat, (P, ROWN))
    fc = {64: 8, 32: 4, 16: 2, 4: 4}
    arr["cols"] = np.concatenate([spread_cols(v[n], fc[w]) for n, w in COLS], axis=1)

    def kmajor(w):
        w = w.reshape(w.shape[:-2] + (w.shape[-2] // P, P, w.shape[-1]))
        return np.swapaxes(w, -3, -2)

    for l in range(2):
        arr[f"L0_gnn_W{l}"] = kmajor(v[f"L0_gnn_W{l}"].T)
    for n in ("L1_gnn_W1", "L1_gnn_W2", "L1_gnn_W3"):
        arr[n] = kmajor(v[n])
    arr["L2_gnn_W"] = kmajor(v["L2_gnn_W"].T)
    arr["L3_gnn_W"] = kmajor(v["L3_gnn_W"])
    ew = np.zeros((PF, D), np.float32)
    ew[2:5] = v["L2_gnn_edge_W"].T
    ew[5] = v["L2_gnn_edge_b"]
    arr["edge_w"] = ew
    for n in GATES:
        arr[n] = kmajor(v[n])
    for n in B2S:
        arr[n] = v[n]
    arr["L0_ffn_W1"], arr["L0_ffn_W2"] = kmajor(v["L0_ffn_w1"]), kmajor(v["L0_ffn_w2"])
    for l in (1, 3):
        arr[f"L{l}_ffn_W1"], arr[f"L{l}_ffn_W2"] = kmajor(v[f"L{l}_ffn_W1"]), kmajor(v[f"L{l}_ffn_W2"])
    arr["L2_ffn_W1"], arr["L2_ffn_Wm"], arr["L2_ffn_W2"] = (kmajor(v[f"L2_ffn_{n}"]) for n in ("W1", "W2", "Wo"))

    nc = bacc.Bacc("TRN2", target_bir_lowering=False, num_devices=1)
    arr = {k: np.ascontiguousarray(x) for k, x in arr.items()}
    a = {k: nc.dram_tensor(f"in_{k}", x.shape, mybir.dt.from_np(x.dtype), kind="ExternalInput").ap()
         for k, x in arr.items()}
    out = nc.dram_tensor("out", (NODES, D), F32, kind="ExternalOutput").ap()
    build(nc, a, out, UPTO)
    r = run_bass_kernel_spmd(nc, [{f"in_{k}": x for k, x in arr.items()}], core_ids=[0])
    return r.results[0]["out"]


UPTO = 7
```

```python
import numpy as np
import concourse.bass as bass
from concourse import mybir

F32, I32, BF16 = mybir.dt.float32, mybir.dt.int32, mybir.dt.bfloat16
ALU, ACT, AX = mybir.AluOpType, mybir.ActivationFunctionType, mybir.AxisListType
ds = bass.ds

P = 128
NODES, D = 3125, 256
B = 125
NBLK = NODES // B
EDGES = 50000
EC = EDGES // B
EXP = 8
UR = 4 * B
UNITS = {0: EXP, 1: (2 * NODES + EXP * (UR - 1)) // UR, 3: (2 * NODES + EXP * (UR - 1)) // UR}
SPARE = UNITS[1] * UR
CAP = 489
TU = 5
NTMIN = EDGES // P + NBLK
NT = 416
EU = 8
EG = EU // 2
assert NTMIN <= NT and NT % EU == 0 and EC % EU == 0
PF = 8
BIG = float(2.0 ** 100)
XW = NBLK * D
HID = 512
BUFW = NBLK * 514
LN_EPS, GBN_EPS, FBN_EPS = 1e-5, 1e-5, 1e-3

C_ID, C_IOTA, C_STRICT, C_UPTO, C_ONE, C_TILE, C_EPS = 0, 128, 256, 381, 506, 634, 1050
C_SPARE, C_STEP = 1054, 1079
C_END = C_STEP + 7
ROWS = ["L0_gnn_b0", "L0_gnn_g0", "L0_gnn_beta0", "L0_gnn_b1", "L0_gnn_g1", "L0_gnn_beta1", "L1_gnn_b3",
        "L2_gnn_bias", "L2_gnn_a_src", "L2_gnn_a_dst", "L3_gnn_bias", "L3_gnn_att_src", "L3_gnn_att_dst"]
GATEB = ["L0_ffn_gate_b", "L1_ffn_bg", "L1_ffn_bias", "L2_ffn_br", "L3_ffn_bg"]
ROWN = 256 * len(ROWS) + EXP * len(GATEB)
COLS = [("L0_ffn_b1", 64), ("L1_gnn_b1", 4), ("L1_gnn_g1", 4), ("L1_gnn_be1", 4), ("L1_gnn_b2", 4),
        ("L1_gnn_g2", 4), ("L1_gnn_be2", 4), ("L1_ffn_b1", 32), ("L2_ffn_b1", 16), ("L2_ffn_g1", 16),
        ("L2_ffn_be1", 16), ("L2_ffn_m1", 16), ("L2_ffn_v1", 16), ("L2_ffn_b2", 16), ("L2_ffn_g2", 16),
        ("L2_ffn_be2", 16), ("L2_ffn_m2", 16), ("L2_ffn_v2", 16), ("L3_ffn_b1", 32)]
COLN = sum(n for _, n in COLS)
GATES = ["L0_ffn_gate_w", "L1_ffn_Wg", "L2_ffn_Wr", "L3_ffn_Wg"]
B2S = ["L0_ffn_b2", "L1_ffn_b2", "L2_ffn_bo", "L3_ffn_b2"]


def row_at(name):
    if name in ROWS:
        return 256 * ROWS.index(name)
    return 256 * len(ROWS) + EXP * GATEB.index(name)


def col_at(name):
    at = 0
    for n, w in COLS:
        if n == name:
            return at
        at += w
    raise KeyError(name)


class Chain:

    def __init__(self, eng, sem):
        self.eng, self.sem, self.n, self.i, self.per, self.k = eng, sem, 0, None, 0, 0

    def enter(self, i, per):
        self.i, self.per, self.k = i, per, 0

    def leave(self, rounds):
        assert self.k == self.per, (self.k, self.per)
        self.n += rounds * self.per
        self.i, self.k = None, 0

    def value(self):
        return self.n + self.k if self.i is None else self.i * self.per + (self.n + self.k)

    def link(self, ins):
        if self.i is None:
            self.n += 1
        else:
            self.k += 1
        ins.then_inc(self.sem, 1)
        self.eng.wait_ge(self.sem, self.value())


def hold(eng, sem, value):
    eng.wait_ge(sem, value)
    eng.nop(nofuse=True)


class Mem:

    def __init__(self, nc):
        self.nc, self.made = nc, 0

    def name(self, name):
        self.made += 1
        return f"{name}_{self.made}"

    def sb(self, name, shape, dtype):
        return self.nc.alloc_sbuf_tensor(self.name(name), shape, dtype)

    def psum(self, name):
        return self.nc.alloc_psum_tensor(self.name(name), [P, 512], F32)

    def sem(self, name):
        return self.nc.alloc_semaphore(self.name(name))


def build(nc, a, out, upto=99):
    m = Mem(nc)
    sb = m.sb
    m.X = sb("x_res", [B, XW], F32)
    m.bufa = sb("bufa", [P, BUFW], F32)
    m.bufb = sb("bufb", [P, BUFW], F32)
    m.cst = sb("cst", [P, C_END], F32)
    m.rows = sb("rows", [P, ROWN], F32)
    m.cols = sb("cols", [P, COLN], F32)
    m.lists = {k: sb(f"list_{k}", [P, NT * PF], F32) for k in ("src", "dst")}
    m.blk = {k: sb(f"blk_{k}", [1, NT], I32) for k in ("src", "dst")}
    m.slots = sb("slots", [B, EC], I32)
    m.small = sb("small", [P, 1400], F32)
    m.weight = [m.small[:B, 200 + 32 * k:200 + 32 * k + NBLK] for k in range(2)]
    m.answer_row, m.token_row = ([m.small[:B, at + 32 * k:at + 32 * k + NBLK].bitcast(I32) for k in range(2)]
                                 for at in (264, 328))
    m.deg = m.small[:B, 1300:1325]
    m.table = nc.dram_tensor("table", (NODES, D), F32, kind="Internal").ap()
    m.table2 = nc.dram_tensor("table2", (NODES, HID), F32, kind="Internal").ap()
    m.tablea = {h: nc.dram_tensor(f"tablea{h}", (NODES, h), F32, kind="Internal").ap() for h in (4, 8)}
    m.tokens = nc.dram_tensor("tokens", (SPARE + NODES, D), F32, kind="Internal").ap()
    m.answers = nc.dram_tensor("answers", (SPARE, D), F32, kind="Internal").ap()
    m.units = sb("units", [1, UNITS[1]], I32)
    m.ldram = {k: nc.dram_tensor(f"edges_{k}", (P * NT, PF), F32, kind="Internal").ap() for k in ("src", "dst")}
    m.a = a

    load(nc, m)
    bin_slots(nc, m, "src", None)
    bin_slots(nc, m, "dst", "src")
    with nc.cleanup_on_exit():
        run = scatter_records(m, "dst")
        with nc.Block() as block:
            block.gpsimd(run.pool)
            block.sync(run.sync)
    X, XN, AGG = m.X, m.bufb[:B, 0:XW], m.bufa
    layernorm(nc, m, X[:], XN)
    for l in range(2):
        store_table(nc, m, XN, m.table, D)
        aggregate(nc, m, "src", m.table, D, True, True, Arena(m.bufb[:, XW:]))
        sage_layer(nc, m, l, XN)
    residual(nc, m, XN)
    if upto >= 1:
        layernorm(nc, m, X[:], XN)
        ffn(nc, m, 0, XN)
    if upto >= 2:
        layernorm(nc, m, X[:], XN)
        gcn(nc, m, XN)
    if upto >= 3:
        layernorm(nc, m, X[:], XN)
        ffn(nc, m, 1, XN)
    if upto >= 4:
        layernorm(nc, m, X[:], XN)
        gat(nc, m, 2, XN)
    if upto >= 5:
        layernorm(nc, m, X[:], XN)
        ffn(nc, m, 2, XN)
    if upto >= 6:
        layernorm(nc, m, X[:], XN)
        gat(nc, m, 3, XN)
    if upto >= 7:
        layernorm(nc, m, X[:], XN)
        ffn(nc, m, 3, XN)
    with nc.cleanup_on_exit():
        stored = m.sem("stored")
        with nc.Block() as block:
            @block.sync
            def _(sp):
                sp.dma_start(out.rearrange("(t p) w -> p t w", p=B),
                             m.X[:, :].rearrange("p (t w) -> p t w", w=D)).then_inc(stored, 16)
                sp.wait_ge(stored, 16)


def load(nc, m):
    with nc.cleanup_on_exit():
        loaded = m.sem("loaded")
        with nc.Block() as block:
            @block.sync
            def _(sp):
                sp.dma_start(m.cst[:, :], m.a["consts"]).then_inc(loaded, 16)
                sp.dma_start(m.rows[:, :], m.a["rows"]).then_inc(loaded, 16)
                sp.dma_start(m.cols[:, :], m.a["cols"]).then_inc(loaded, 16)
                sp.dma_start(m.X[:, :].rearrange("p (t w) -> p t w", w=D),
                             m.a["x"].rearrange("(t p) w -> p t w", p=B)).then_inc(loaded, 16)
                sp.wait_ge(loaded, 64)


class Scatter:
    pass


def records(m, key):
    return m.bufb[:B, 0:EC * PF] if key == "src" else m.lists["dst"][:B, 0:EC * PF]


def scatter_records(m, key):
    stage = m.sb("recordstage", [B, EU, PF], F32)
    slot = m.sb("slotstage", [B, EU], I32)
    copied = m.sem("copied")
    sent = [m.sem(f"sent{k}") for k in range(EU)]
    listed = m.sem("listed")
    pay = records(m, key)
    run = Scatter()

    def group(pool, i, g, value):
        pool.tensor_copy(stage[:, g * EG:(g + 1) * EG, :].rearrange("p c f -> p (c f)"),
                         pay[:, ds(i * (EU * PF) + g * EG * PF, EG * PF)]).then_inc(copied, 1)
        pool.tensor_copy(slot[:, g * EG:(g + 1) * EG], m.slots[:, ds(i * EU + g * EG, EG)]).then_inc(copied, 1)
        hold(pool, copied, value)
        for k in range(g * EG, (g + 1) * EG):
            pool.indirect_dma_start(
                out=m.ldram[key], out_offset=bass.IndirectOffsetOnAxis(ap=slot[:, k:k + 1], axis=0),
                in_=stage[:, k, :], in_offset=None).then_inc(sent[k], 16)

    def pool_program(pool):
        for g in range(2):
            group(pool, 0, g, 2 * g + 2)
        with pool.Fori(1, EC // EU) as i:
            for g in range(2):
                for k in range(g * EG, (g + 1) * EG):
                    hold(pool, sent[k], i * 16)
                group(pool, i, g, i * 4 + (2 * g + 2))

    def sync_program(sp):
        for k in range(EU):
            sp.wait_ge(sent[k], 16 * (EC // EU))
        sp.dma_start(m.lists[key][:, :], m.ldram[key].rearrange("(p c) f -> p (c f)", p=P)).then_inc(listed, 16)
        sp.wait_ge(listed, 16)

    run.pool, run.sync = pool_program, sync_program
    return run


def bin_slots(nc, m, key, other_list):
    other = "dst" if key == "src" else "src"
    count_degree = key == "dst"
    with nc.cleanup_on_exit():
        sb, sem = m.sb, m.sem
        wa = m.bufa[:B, :]
        names = ["key", "hi", "lo", "onehot", "scan", "tmp", "rank", "zero", "slot"]
        W = {n: wa[:, i * EC:(i + 1) * EC] for i, n in enumerate(names)}
        keyi = wa[:, 9 * EC:10 * EC].bitcast(I32)
        othi = wa[:, 10 * EC:11 * EC].bitcast(I32)
        iq = wa[:, 11 * EC:12 * EC].bitcast(I32)
        iq2 = wa[:, 12 * EC:13 * EC].bitcast(I32)
        attr = wa[:, 13 * EC:16 * EC]
        slot_new = wa[:, 16 * EC:17 * EC].bitcast(I32)
        pay = records(m, key)
        payv = pay.rearrange("p (c f) -> p c f", f=PF)
        fill = m.bufb[:, 3400:3400 + NT * PF]
        small = m.small
        cnt, tot, tiles, tstart, base, ti = [small[:B, 32 * i:32 * i + NBLK] for i in range(6)]
        tii = small[:B, 192:192 + NBLK].bitcast(I32)
        ohl = sb("ohl", [B, 2, 5, B], BF16)
        ohh = sb("ohh", [B, 2, 5, NBLK], BF16)
        blkf = sb("blkf", [1, NT], F32)
        ps, pd = m.psum("ps"), m.psum("pd")
        iota = m.cst[:B, C_IOTA:C_IOTA + NBLK]
        edges_in, filled, steps, counted = sem("edges_in"), sem("filled"), sem("steps"), sem("counted")
        prefixed, prefilled = sem("prefixed"), sem("prefilled")
        hot, hot_used = sem("hot"), sem("hot_used")
        clear_tokens = key == "dst"
        blank, tokens_clear = sem("blank"), sem("tokens_clear")
        zeros = m.bufb[:B, 6750:6750 + UR // B * D]
        run = scatter_records(m, other_list) if other_list else None
        with nc.Block() as block:
            @block.sync
            def _(sp):
                sp.dma_start(keyi, m.a[key]).then_inc(edges_in, 16)
                sp.dma_start(othi, m.a[other]).then_inc(edges_in, 16)
                sp.dma_start(attr, m.a["attr"]).then_inc(edges_in, 16)
                if clear_tokens:
                    sp.wait_ge(blank, 1)
                    for u in range(UNITS[1]):
                        sp.dma_start(m.tokens[u * UR:(u + 1) * UR, :].rearrange("(t p) w -> p t w", p=B),
                                     zeros.rearrange("p (t w) -> p t w", w=D)).then_inc(tokens_clear, 16)
                sp.wait_ge(filled, 1)
                sp.dma_start(m.ldram[key].rearrange("(p c) f -> p (c f)", p=P), fill).then_inc(prefilled, 16)
                sp.wait_ge(prefilled, 16)
                if clear_tokens:
                    sp.wait_ge(tokens_clear, 16 * UNITS[1])
                if run:
                    run.sync(sp)

            @block.gpsimd
            def _(pool):
                if run:
                    run.pool(pool)

            @block.tensor
            def _(pe):
                pe.wait_ge(counted, 1)
                pe.matmul(ps[:B, 0:NBLK], m.cst[:B, C_STRICT:C_STRICT + B], cnt, start=True, stop=True)
                pe.matmul(ps[:B, 32:32 + NBLK], m.cst[:B, C_ONE:C_ONE + B], cnt, start=True,
                          stop=True).then_inc(prefixed, 1)
                if count_degree:
                    pe.matmul(pd[:B, 0:NBLK], m.cst[:B, C_ONE:C_ONE + B], W["zero"][:, 0:NBLK], start=True,
                              stop=True, skip_group_check=True)
                    with pe.Fori(0, EC // 10) as i:
                        for g in range(2):
                            pe.wait_ge(hot, i * 2 + (g + 1))
                            for c in range(5):
                                mm = pe.matmul(pd[:B, 0:NBLK], ohl[:, g, c, :], ohh[:, g, c, :], start=False,
                                               stop=False, skip_group_check=True)
                            mm.then_inc(hot_used, 1)

            @block.vector
            def _(v):
                c = Chain(v, steps)
                link = c.link
                fv = fill.rearrange("p (c f) -> p c f", f=PF)
                if clear_tokens:
                    v.memset(zeros, 0.0).then_inc(blank, 1)
                link(v.memset(fill, 0.0))
                link(v.memset(fv[:, :, 6:7], -BIG))
                v.memset(fv[:, :, 1:2], -1.0).then_inc(filled, 1)
                v.memset(W["rank"], 0.0)
                v.memset(W["zero"], 0.0)
                v.memset(W["slot"], 0.0)
                link(v.memset(pay, 0.0))
                v.wait_ge(edges_in, 48)
                link(v.tensor_copy(W["key"], keyi))
                link(v.tensor_scalar(W["hi"], W["key"], float(B), None, ALU.is_ge))
                for b in range(2, NBLK):
                    link(v.scalar_tensor_tensor(W["hi"], W["key"], float(B * b), W["hi"], ALU.is_ge, ALU.add))
                link(v.scalar_tensor_tensor(W["lo"], W["hi"], -float(B), W["key"], ALU.mult, ALU.add))
                with v.Fori(0, NBLK) as b:
                    c.enter(b, 4)
                    link(v.tensor_scalar(W["onehot"], W["hi"], iota[:, ds(b, 1)], None, ALU.is_equal))
                    link(v.tensor_tensor_scan(W["scan"], W["onehot"], W["zero"], 0.0, ALU.add, ALU.add))
                    v.tensor_scalar(cnt[:, ds(b, 1)], W["scan"][:, EC - 1:EC], 1.0, None, ALU.mult)
                    link(v.tensor_tensor(W["tmp"], W["onehot"], W["scan"], ALU.mult))
                    link(v.tensor_tensor(W["rank"], W["rank"], W["tmp"], ALU.add))
                c.leave(NBLK)
                v.tensor_scalar(tiles, cnt, 1.0, None, ALU.mult).then_inc(counted, 1)
                v.wait_ge(prefixed, 1)
                link(v.tensor_scalar(tot, ps[:B, 32:32 + NBLK], float(P - 1), None, ALU.add))
                link(v.tensor_copy(tii, tot))
                link(v.tensor_scalar(tii, tii, 7, None, ALU.arith_shift_right))
                link(v.tensor_copy(tiles, tii))
                link(v.tensor_tensor_scan(tstart, tiles, W["zero"][:, 0:NBLK], 0.0, ALU.add, ALU.add))
                link(v.tensor_tensor(tstart, tstart, tiles, ALU.subtract))
                link(v.tensor_scalar(ti, tstart, float(P), -1.0, ALU.mult, ALU.add))
                link(v.tensor_tensor(base, ti, ps[:B, 0:NBLK], ALU.add))
                with v.Fori(0, NBLK) as b:
                    c.enter(b, 2)
                    link(v.tensor_scalar(W["tmp"], W["hi"], iota[:, ds(b, 1)], base[:, ds(b, 1)], ALU.is_equal,
                                         ALU.mult))
                    link(v.tensor_tensor(W["slot"], W["slot"], W["tmp"], ALU.add))
                c.leave(NBLK)
                link(v.tensor_tensor(W["slot"], W["slot"], W["rank"], ALU.add))
                link(v.tensor_copy(iq, W["slot"]))
                v.tensor_scalar(iq2, iq, 7, None, ALU.arith_shift_right)
                link(v.tensor_scalar(iq, iq, P - 1, None, ALU.bitwise_and))
                link(v.tensor_copy(W["tmp"], iq))
                link(v.tensor_copy(W["scan"], iq2))
                link(v.scalar_tensor_tensor(W["slot"], W["tmp"], float(NT), W["scan"], ALU.mult, ALU.add))
                v.tensor_copy(slot_new, W["slot"])
                link(v.tensor_scalar(blkf[:, :], m.cst[0:1, C_TILE:C_TILE + NT], tstart[0:1, 1:2], None, ALU.is_ge))
                with v.Fori(2, NBLK) as b:
                    c.enter(b - 2, 1)
                    link(v.scalar_tensor_tensor(blkf[:, :], m.cst[0:1, C_TILE:C_TILE + NT], tstart[0:1, ds(b, 1)],
                                                blkf[:, :], ALU.is_ge, ALU.add))
                c.leave(NBLK - 2)
                v.tensor_copy(m.blk[key][:, :], blkf[:, :])
                v.tensor_copy(payv[:, :, 0].bitcast(I32), othi)
                v.tensor_copy(payv[:, :, 1], W["lo"])
                v.tensor_copy(payv[:, :, 2:5], attr.rearrange("p (c f) -> p c f", f=3))
                link(v.memset(payv[:, :, 5:6], 1.0))
                if count_degree:
                    v.sem_inc(hot_used, 2)
                    with v.Fori(0, EC // 10) as i:
                        for g in range(2):
                            v.wait_ge(hot_used, i * 2 + (g + 1))
                            for q in range(5):
                                col = i * 10 + (g * 5 + q)
                                v.tensor_scalar(ohl[:, g, q, :], m.cst[:B, C_IOTA:C_IOTA + B],
                                                W["lo"][:, ds(col, 1)], None, ALU.is_equal)
                                last = v.tensor_scalar(ohh[:, g, q, :], iota, W["hi"][:, ds(col, 1)], None,
                                                       ALU.is_equal)
                            last.then_inc(hot, 1)
                    v.wait_ge(hot_used, 2 + EC // 5)
                    v.tensor_copy(m.deg, pd[:B, 0:NBLK])
    with nc.cleanup_on_exit():
        with nc.Block() as block:
            @block.vector
            def _(v):
                v.tensor_copy(m.slots[:, :], slot_new)


def layernorm(nc, m, src, dst):
    with nc.cleanup_on_exit():
        sem = m.sem
        st = m.small[:B, 0:6 * NBLK]
        f = st.rearrange("p (t s) -> p s t", s=6)
        mean, var, dif, std, inv, nb = [m.small[:B, 200 + 32 * i:200 + 32 * i + NBLK] for i in range(6)]
        steps, var_ready, std_ready = sem("steps"), sem("var_ready"), sem("std_ready")
        with nc.Block() as block:
            @block.vector
            def _(v):
                c = Chain(v, steps)
                link = c.link
                with v.Fori(0, NBLK // TU) as i:
                    c.enter(i, 1)
                    for k in range(TU):
                        ins = v.bn_stats(st[:, ds((i * TU + k) * 6, 6)], src[:, ds((i * TU + k) * D, D)])
                    link(ins)
                c.leave(NBLK // TU)
                link(v.tensor_tensor(mean, f[:, 1], f[:, 4], ALU.add))
                link(v.tensor_scalar(mean, mean, 0.5, None, ALU.mult))
                link(v.tensor_tensor(dif, f[:, 1], f[:, 4], ALU.subtract))
                link(v.tensor_tensor(dif, dif, dif, ALU.mult))
                link(v.tensor_scalar(dif, dif, 0.25, None, ALU.mult))
                link(v.tensor_tensor(var, f[:, 2], f[:, 5], ALU.add))
                v.scalar_tensor_tensor(var, var, 1.0 / D, dif, ALU.mult, ALU.add).then_inc(var_ready, 1)
                v.wait_ge(std_ready, 1)
                link(v.reciprocal(inv, std))
                link(v.scalar_tensor_tensor(nb, mean, -1.0, inv, ALU.mult, ALU.mult))
                with v.Fori(0, NBLK // TU) as i:
                    for k in range(TU):
                        t = i * TU + k
                        v.tensor_scalar(dst[:, ds(t * D, D)], src[:, ds(t * D, D)], inv[:, ds(t, 1)],
                                        nb[:, ds(t, 1)], ALU.mult, ALU.add)

            @block.scalar
            def _(act):
                act.wait_ge(var_ready, 1)
                act.activation(std, var, ACT.Sqrt, bias=m.cst[:B, C_EPS:C_EPS + 1]).then_inc(std_ready, 1)


def store_table(nc, m, src, table, width):
    with nc.cleanup_on_exit():
        stored = m.sem("stored")
        with nc.Block() as block:
            @block.sync
            def _(sp):
                sp.dma_start(table.rearrange("(t p) w -> p t w", p=B),
                             src.rearrange("p (t w) -> p t w", w=width)).then_inc(stored, 16)
                sp.wait_ge(stored, 16)


GROUPS = NT // EG
RING = 4
RT = RING * EG
assert NT % RT == 0


def over(eng, total, ring, *stages):
    ahead = max(lead for _, lead in stages)
    rounds = total // ring
    assert total == rounds * ring and ahead <= ring

    def step(i, g):
        for program, lead in stages:
            s = g + lead
            if not isinstance(i, int):
                program(i if s < ring else i + 1, s % ring)
            elif 0 <= i * ring + s < total:
                program((i * ring + s) // ring, s % ring)

    for g in range(-ahead, 0):
        step(0, g)
    with eng.Fori(0, rounds - 1) as i:
        for g in range(ring):
            step(i, g)
    for g in range(ring):
        step(rounds - 1, g)


def over_groups(eng, *stages):
    over(eng, GROUPS, RING, *stages)


def ring(g):
    return slice(g * EG, (g + 1) * EG)


class Arena:

    def __init__(self, view):
        self.view, self.at = view, 0

    def take(self, parts, shape, dtype=F32):
        n = int(np.prod(shape))
        cols = (n + 1) // 2 if dtype == BF16 else n
        v = self.view[:parts, self.at:self.at + cols]
        self.at += cols
        assert self.at <= self.view.shape[1]
        if dtype == BF16:
            v = v.bitcast(BF16)[:, 0:n]
        if len(shape) == 2:
            v = v.rearrange("p (a b) -> p a b", b=shape[1])
        return v


def fields(m, key):
    return m.lists[key][:, :].rearrange("p (c f) -> p c f", f=PF)


def pool_gathers(pool, m, key, idx, picked, free, unit, table, rows, gathered):
    lst = fields(m, key)

    def gather(i, g):
        hold(pool, free, i * (RING * unit) + (g * unit + unit))
        pool.tensor_copy(idx[:, ring(g)], lst[:, ds(i * RT + g * EG, EG), 0].bitcast(I32)).then_inc(picked, 1)
        hold(pool, picked, i * RING + (g + 1))
        for k in range(g * EG, (g + 1) * EG):
            pool.indirect_dma_start(
                out=rows(k), out_offset=None, in_=table,
                in_offset=bass.IndirectOffsetOnAxis(ap=idx[:, k:k + 1], axis=0)).then_inc(gathered[g], 16)

    over_groups(pool, (gather, 0))


def act_onehots(act, m, lst, i, g, dist, onehot, measured, hot_ready):
    d0 = (g % 2) * EG
    act.wait_ge(hot_ready, i * RING + (g + 1))
    for q in range(EG):
        d = act.activation(dist[:, d0 + q, :], m.cst[:, C_IOTA:C_IOTA + B], ACT.Abs, scale=-1.0,
                           bias=lst[:, ds(i * RT + (g * EG + q), 1), 1])
    d.then_inc(measured, 1)
    act.wait_ge(measured, i * RING + (g + 1))
    act.activation(onehot[:, ring(g), :], dist[:, d0:d0 + EG, :], ACT.Relu, scale=-1.0,
                   bias=m.cst[:, C_ONE:C_ONE + 1]).then_inc(hot_ready, 1)


def vector_onehots(v, m, lst, i, g, onehot, hot_ready):
    for q in range(EG):
        o = v.tensor_scalar(onehot[:, g * EG + q, :], m.cst[:, C_IOTA:C_IOTA + B],
                            lst[:, ds(i * RT + (g * EG + q), 1), 1], None, ALU.is_equal)
    o.then_inc(hot_ready, 1)


def block_of(eng, m, key, i, j):
    return eng.value_load(m.blk[key][0:1, ds(i * RT + j, 1)], min_val=0, max_val=NBLK - 1)


def aggregate(nc, m, key, table, width, count, clear, space):
    W = width + (1 if count else 0)
    NPS = 2 * EG
    acc = m.bufa[:B, 0:NBLK * W]
    lst = fields(m, key)
    with nc.cleanup_on_exit():
        sem = m.sem
        idx = m.sb("idx", [P, RT], I32)
        rows, onehot = space.take(P, [RT, W]), space.take(P, [RT, B])
        dist = m.sb("dist", [P, 2 * EG, B], BF16)
        ps = [m.psum(f"ps{i}") for i in range(NPS)]
        cleared, picked, measured, hot_ready = sem("cleared"), sem("picked"), sem("measured"), sem("hot_ready")
        summed, added = sem("summed"), sem("added")
        gathered = [sem(f"gathered{g}") for g in range(RING)]
        with nc.Block() as block:
            @block.vector
            def _(v):
                if count:
                    v.memset(rows[:, :, width:W], 1.0).then_inc(cleared, 1)
                    v.wait_ge(cleared, 1)
                if clear:
                    v.memset(acc, 0.0).then_inc(cleared, 1)
                    v.wait_ge(cleared, 1 + count)
                v.sem_inc(added, NPS)

                def add(i, g):
                    for j in range(g * EG, (g + 1) * EG):
                        b = block_of(v, m, key, i, j)
                        part = acc[:, ds(b * W, W)]
                        v.wait_ge(summed, i * RT + (j + 1 + RT))
                        v.wait_ge(added, i * RT + (j + NPS))
                        v.tensor_tensor(part, part, ps[j % NPS][:B, 0:W], ALU.add).then_inc(added, 1)

                over_groups(v, (add, 0))

            @block.gpsimd
            def _(pool):
                pool_gathers(pool, m, key, idx, picked, summed, EG, table, lambda k: rows[:, k, 0:width], gathered)

            @block.scalar
            def _(act):
                act.sem_inc(hot_ready, 2)

                def one_hots(i, g):
                    hold(act, summed, i * RT + (g * EG + EG))
                    act_onehots(act, m, lst, i, g, dist, onehot, measured, hot_ready)

                over_groups(act, (one_hots, 0))

            @block.tensor
            def _(pe):
                if count:
                    pe.wait_ge(cleared, 1)
                pe.sem_inc(summed, RT)

                def products(i, g):
                    pe.wait_ge(gathered[g], i * (16 * EG) + 16 * EG)
                    pe.wait_ge(hot_ready, i * RING + (g + 3))
                    for j in range(g * EG, (g + 1) * EG):
                        pe.wait_ge(added, i * RT + (j + 1))
                        pe.matmul(ps[j % NPS][:B, 0:W], onehot[:, j, :], rows[:, j, :], start=True,
                                  stop=True).then_inc(summed, 1)

                over_groups(pe, (products, 0))


def token_linear(nc, m, src, wdram, wide, evac, stage_add=None, keep=None):
    with nc.cleanup_on_exit():
        sb, sem = m.sb, m.sem
        w = sb("w", [P, 2, wide], F32)
        st = sb("st", [B, TU, D], F32)
        stT = sb("stT", [P, TU, 2 * B], F32)
        ps = [m.psum(f"ps{i}") for i in range(TU)]
        w_in, staged, turned, lifted = sem("w_in"), sem("staged"), sem("turned"), sem("lifted")
        product, out_done, kept = sem("product"), sem("out_done"), sem("kept")
        with nc.Block() as block:
            @block.sync
            def _(sp):
                sp.dma_start(w[:, :, :], wdram).then_inc(w_in, 16)
                sp.wait_ge(w_in, 16)

            @block.vector
            def _(v):
                v.sem_inc(out_done, TU)
                v.sem_inc(kept, TU)
                with v.Fori(0, NBLK // TU) as i:
                    for k in range(TU):
                        t = i * TU + k
                        v.wait_ge(turned, i * TU + TU)
                        if stage_add:
                            scale, other, ow = stage_add
                            v.scalar_tensor_tensor(st[:, k, :], other[:, ds(t * ow, D)], scale[:, ds(t, 1)],
                                                   src[:, ds(t * D, D)], ALU.mult, ALU.add).then_inc(staged, 1)
                        else:
                            v.tensor_scalar(st[:, k, :], src[:, ds(t * D, D)], 1.0, None,
                                            ALU.mult).then_inc(staged, 1)
                    for k in range(TU):
                        t = i * TU + k
                        if keep is not None:
                            v.wait_ge(lifted, t + 1)
                            for h in range(2):
                                kp = v.tensor_scalar(keep[:, ds(t * B + h * NODES, B)], stT[:, k, h * B:(h + 1) * B],
                                                     1.0, None, ALU.mult)
                            kp.then_inc(kept, 1)
                        v.wait_ge(product, t + (1 + TU))
                        evac(v, t, ps[k][:B, 2 * B:2 * B + wide]).then_inc(out_done, 1)
                if keep is not None:
                    v.wait_ge(kept, NBLK + TU)

            @block.scalar
            def _(act):
                with act.Fori(0, NBLK // TU) as i:
                    for k in range(TU):
                        act.wait_ge(turned, i * TU + (k + 1 + TU))
                        act.wait_ge(product, i * TU + TU)
                        if keep is not None:
                            act.wait_ge(kept, i * TU + TU)
                        act.activation(stT[:, k, :], ps[k][:, 0:2 * B], ACT.Copy).then_inc(lifted, 1)

            @block.tensor
            def _(pe):
                pe.sem_inc(turned, TU)
                pe.sem_inc(product, TU)
                pe.wait_ge(w_in, 16)
                with pe.Fori(0, NBLK // TU) as i:
                    for k in range(TU):
                        pe.wait_ge(staged, i * TU + (k + 1))
                        pe.wait_ge(out_done, i * TU + (k + 1))
                        for h in range(2):
                            tr = pe.transpose(ps[k][:, h * B:(h + 1) * B], st[:, k, h * P:(h + 1) * P],
                                              m.cst[:B, C_ID:C_ID + B])
                        tr.then_inc(turned, 1)
                    for k in range(TU):
                        pe.wait_ge(lifted, i * TU + (k + 1))
                        for h in range(2):
                            mm = pe.matmul(ps[k][:B, 2 * B:2 * B + wide], stT[:, k, h * B:(h + 1) * B], w[:, h, :],
                                           start=(h == 0), stop=(h == 1))
                        mm.then_inc(product, 1)


def sage_layer(nc, m, l, XN):
    W = D + 1
    acc = m.bufa[:B, 0:NBLK * W]
    deg = acc.rearrange("p (t w) -> p t w", w=W)[:, :, D]
    rdeg = m.small[:B, 400:400 + NBLK]
    H = m.bufb[:B, XW:2 * XW]
    with nc.cleanup_on_exit():
        steps = m.sem("steps")
        with nc.Block() as block:
            @block.vector
            def _(v):
                c = Chain(v, steps)
                c.link(v.tensor_scalar(rdeg, deg, 1.0, None, ALU.max))
                c.link(v.reciprocal(rdeg, rdeg))
    at = row_at(f"L0_gnn_b{l}")
    bias = m.rows[:B, at:at + D]
    token_linear(nc, m, XN, m.a[f"L0_gnn_W{l}"], D,
                 lambda v, t, ps: v.tensor_tensor(H[:, ds(t * D, D)], ps, bias, ALU.add),
                 stage_add=(rdeg, acc, W))
    layernorm(nc, m, H, H)
    with nc.cleanup_on_exit():
        steps, affine, gate = (m.sem(n) for n in ("steps", "affine", "gate"))
        g = m.rows[:B, row_at(f"L0_gnn_g{l}"):][:, 0:D]
        be = m.rows[:B, row_at(f"L0_gnn_beta{l}"):][:, 0:D]
        with nc.Block() as block:
            @block.vector
            def _(v):
                c = Chain(v, steps)
                hv = H.rearrange("p (t w) -> p t w", w=D)
                c.link(v.tensor_tensor(hv, hv, g.unsqueeze(1).broadcast_to([B, NBLK, D]), ALU.mult))
                v.tensor_tensor(hv, hv, be.unsqueeze(1).broadcast_to([B, NBLK, D]), ALU.add).then_inc(affine, 1)
                v.wait_ge(gate, 1)
                v.tensor_tensor(XN, H, m.bufa[:B, 0:XW], ALU.mult)

            @block.scalar
            def _(act):
                act.wait_ge(affine, 1)
                act.activation(m.bufa[:B, 0:XW], H, ACT.Sigmoid).then_inc(gate, 1)


def residual(nc, m, src):
    with nc.cleanup_on_exit():
        with nc.Block() as block:
            @block.vector
            def _(v):
                v.tensor_tensor(m.X[:, :], m.X[:, :], src, ALU.add)


def spread(ap, n):
    return ap.unsqueeze(2).broadcast_to([ap.shape[0], ap.shape[1], n])


FFN = {0: dict(F=1024, act=ACT.Relu), 1: dict(F=512, act=ACT.Relu), 2: dict(F=256, act=ACT.Relu),
       3: dict(F=512, act=ACT.Gelu)}


def gates(nc, m, l, LG, coef):
    G = NBLK * EXP
    with nc.cleanup_on_exit():
        sem = m.sem
        mx, sm, ix, t1 = [m.small[:B, 600 + 32 * i:600 + 32 * i + NBLK] for i in range(4)]
        w1 = m.small[:B, 730:730 + NBLK]
        E = m.small[:B, 760:760 + G]
        OH = m.small[:B, 960:960 + G]
        v3 = lambda ap: ap.rearrange("p (t e) -> p t e", e=EXP)
        lg, ev, oh, cf = v3(LG), v3(E), v3(OH), v3(coef)
        io8 = m.cst[:B, C_IOTA:C_IOTA + EXP].unsqueeze(1).broadcast_to([B, NBLK, EXP])
        T = m.sb("gt", [B, 5, G], F32)
        a1, a2, a3, first, second = (v3(T[:, i, :]) for i in range(5))
        zero, ucount, ustart, hits = (m.sb(n, [B, w], F32) for n, w in (
            ("zero", NBLK), ("ucount", EXP), ("ustart", EXP), ("hits", UNITS[1] * EXP)))
        posn, kept, away = (m.sb(n, [B, NBLK], F32) for n in ("posn", "kept", "away"))
        uf = m.sb("uf", [1, UNITS[1]], F32)
        ps = m.psum("ps")
        steps, shifted, exped, picked, counted = (sem(n) for n in ("steps", "shifted", "exped", "picked", "counted"))
        with nc.Block() as block:
            @block.vector
            def _(v):
                c = Chain(v, steps)
                link = c.link

                def first_max(values, largest, onehot):
                    link(v.tensor_tensor(a1, values, spread(largest, EXP), ALU.is_equal))
                    link(v.tensor_scalar(a1, a1, -float(EXP), float(EXP), ALU.mult, ALU.add))
                    link(v.tensor_tensor(a1, a1, io8, ALU.add))
                    link(v.tensor_reduce(ix, a1, AX.X, ALU.min))
                    link(v.tensor_tensor(onehot, io8, spread(ix, EXP), ALU.is_equal))

                def places():
                    v.sem_inc(picked, 1)
                    v.wait_ge(counted, 1)
                    tot = v3(ps[:B, 256:256 + G])
                    link(v.memset(zero[:, :], 0.0))
                    for e in range(EXP):
                        link(v.tensor_tensor_scan(a2[:, :, e], tot[:, :, e], zero[:, :], 0.0, ALU.add, ALU.add))
                    link(v.tensor_tensor(hits[:, 0:7 * EXP].rearrange("p (e j) -> p e j", j=7),
                                         a2[:, NBLK - 1, :].unsqueeze(2).broadcast_to([B, EXP, 7]),
                                         m.cst[:B, C_STEP:C_STEP + 7].unsqueeze(1).broadcast_to([B, EXP, 7]),
                                         ALU.is_gt))
                    link(v.tensor_reduce(ucount[:, :], hits[:, 0:7 * EXP].rearrange("p (e j) -> p e j", j=7), AX.X,
                                         ALU.add))
                    link(v.tensor_tensor(a2, a2, tot, ALU.subtract))
                    link(v.tensor_tensor(a2, a2, v3(ps[:B, 0:G]), ALU.add))

                def row_of(onehot, k):
                    link(v.tensor_tensor(a1, a2, onehot, ALU.mult))
                    link(v.tensor_reduce(posn[:, :], a1, AX.X, ALU.add))
                    link(v.tensor_copy(m.answer_row[k], posn[:, :]))
                    link(v.tensor_copy(m.token_row[k], posn[:, :]))

                link(v.tensor_reduce(mx, lg, AX.X, ALU.max))
                if l in (0, 2):
                    v.tensor_tensor(ev, lg, spread(mx, EXP), ALU.subtract).then_inc(shifted, 1)
                    v.wait_ge(exped, 1)
                    link(v.tensor_reduce(sm, ev, AX.X, ALU.add))
                    link(v.reciprocal(sm, sm))
                    if l == 2:
                        v.tensor_tensor(cf, ev, spread(sm, EXP), ALU.mult)
                        return
                    link(v.tensor_reduce(mx, ev, AX.X, ALU.max))
                    first_max(ev, mx, oh)
                    places()
                    link(v.tensor_tensor(a1, a2, oh, ALU.mult))
                    link(v.tensor_reduce(posn[:, :], a1, AX.X, ALU.add))
                    link(v.tensor_scalar(kept[:, :], posn[:, :], float(CAP), None, ALU.is_le))
                    link(v.tensor_tensor(t1, mx, sm, ALU.mult))
                    v.tensor_tensor(m.weight[0], kept[:, :], t1, ALU.mult)
                    link(v.tensor_scalar(posn[:, :], posn[:, :], float(CAP), -1.0, ALU.min, ALU.add))
                    link(v.scalar_tensor_tensor(posn[:, :], ix, float(UR), posn[:, :], ALU.mult, ALU.add))
                    v.tensor_copy(m.answer_row[0], posn[:, :])
                    link(v.tensor_tensor(away[:, :], m.cst[:B, C_SPARE:C_SPARE + NBLK], posn[:, :], ALU.subtract))
                    link(v.tensor_scalar(kept[:, :], kept[:, :], -1.0, 1.0, ALU.mult, ALU.add))
                    link(v.tensor_tensor(away[:, :], away[:, :], kept[:, :], ALU.mult))
                    link(v.tensor_tensor(posn[:, :], posn[:, :], away[:, :], ALU.add))
                    v.tensor_copy(m.token_row[0], posn[:, :])
                    v.tensor_copy(m.units[0:1, 0:EXP], m.cst[0:1, C_IOTA:C_IOTA + EXP])
                    return
                first_max(lg, mx, first)
                link(v.scalar_tensor_tensor(a3, first, -BIG, lg, ALU.mult, ALU.add))
                link(v.tensor_reduce(sm, a3, AX.X, ALU.max))
                first_max(a3, sm, second)
                link(v.tensor_tensor(oh, first, second, ALU.add))
                places()
                link(v.tensor_tensor_scan(ustart[:, :], ucount[:, :], zero[:, 0:EXP], 0.0, ALU.add, ALU.add))
                link(v.tensor_tensor(ustart[:, :], ustart[:, :], ucount[:, :], ALU.subtract))
                link(v.tensor_scalar(ucount[:, :], ustart[:, :], float(UR), -1.0, ALU.mult, ALU.add))
                link(v.tensor_tensor(a2, a2, ucount[:, :].unsqueeze(1).broadcast_to([B, NBLK, EXP]), ALU.add))
                row_of(first, 0)
                row_of(second, 1)
                U = UNITS[l]
                hv = hits[0:1, 0:U * 7].rearrange("p (u e) -> p u e", e=7)
                link(v.tensor_tensor(hv, m.cst[0:1, C_IOTA:C_IOTA + U].unsqueeze(2).broadcast_to([1, U, 7]),
                                     ustart[0:1, 1:EXP].unsqueeze(1).broadcast_to([1, U, 7]), ALU.is_ge))
                link(v.tensor_reduce(uf[:, :], hv, AX.X, ALU.add))
                v.tensor_copy(m.units[:, :], uf[:, :])
                if l == 3:
                    v.memset(m.weight[0], 1.0)
                    v.memset(m.weight[1], 1.0)
                    return
                v.tensor_tensor(t1, sm, mx, ALU.subtract).then_inc(shifted, 1)
                v.wait_ge(exped, 1)
                link(v.tensor_scalar(sm, t1, 1.0, None, ALU.add))
                link(v.reciprocal(w1, sm))
                v.tensor_tensor(m.weight[1], t1, w1, ALU.mult)
                v.tensor_copy(m.weight[0], w1)

            @block.scalar
            def _(act):
                if l in (0, 2):
                    act.wait_ge(shifted, 1)
                    act.activation(E, E, ACT.Exp).then_inc(exped, 1)
                if l == 1:
                    act.wait_ge(shifted, 1)
                    act.activation(t1, t1, ACT.Exp).then_inc(exped, 1)

            @block.tensor
            def _(pe):
                if l != 2:
                    pe.wait_ge(picked, 1)
                    pe.matmul(ps[:B, 0:G], m.cst[:B, C_UPTO:C_UPTO + B], OH, start=True, stop=True)
                    pe.matmul(ps[:B, 256:256 + G], m.cst[:B, C_ONE:C_ONE + B], OH, start=True,
                              stop=True).then_inc(counted, 1)


def ffn(nc, m, l, XN):
    LG = m.small[:B, 0:NBLK * EXP]
    coef = m.small[:B, 200:200 + NBLK * EXP]
    XT = m.bufa[:, 0:2 * NODES]
    gb = m.rows[:B, row_at({0: "L0_ffn_gate_b", 1: "L1_ffn_bg", 2: "L2_ffn_br", 3: "L3_ffn_bg"}[l]):][:, 0:EXP]
    token_linear(nc, m, XN, m.a[GATES[l]], EXP,
                 lambda v, t, ps: v.tensor_tensor(LG[:, ds(t * EXP, EXP)], ps, gb, ALU.add),
                 keep=XT if l == 2 else None)
    if l == 1:
        with nc.cleanup_on_exit():
            with nc.Block() as block:
                @block.vector
                def _(v):
                    lg = LG.rearrange("p (t e) -> p t e", e=EXP)
                    b = m.rows[:B, row_at("L1_ffn_bias"):][:, 0:EXP].unsqueeze(1).broadcast_to([B, NBLK, EXP])
                    v.tensor_tensor(lg, lg, b, ALU.add)
    gates(nc, m, l, LG, coef)
    if l == 2:
        bias_out(nc, m, l, coef, m.X[:, :], False)
        experts(nc, m, l, XT, coef, m.X[:, :])
        return
    K = 1 if l == 0 else 2
    send_tokens(nc, m, K, XN)
    unit_experts(nc, m, l)
    take_answers(nc, m, l, K)
    if l == 0:
        finite_residual(nc, m, m.bufb[:B, 0:XW])


def send_tokens(nc, m, K, XN):
    with nc.cleanup_on_exit():
        sent = m.sem("sent")
        with nc.Block() as block:
            @block.gpsimd
            def _(pool):
                for t in range(NBLK):
                    for k in range(K):
                        pool.indirect_dma_start(
                            out=m.tokens, out_offset=bass.IndirectOffsetOnAxis(ap=m.token_row[k][:, t:t + 1], axis=0),
                            in_=XN[:, t * D:(t + 1) * D], in_offset=None).then_inc(sent, 16)
                pool.wait_ge(sent, 16 * NBLK * K)


def take_answers(nc, m, l, K):
    got = lambda t, k: m.bufb[:B, (k * NBLK + t) * D:(k * NBLK + t + 1) * D]
    with nc.cleanup_on_exit():
        arrived = [m.sem(f"arrived{g}") for g in range(CH)]
        first_added = m.sem("first_added")
        with nc.Block() as block:
            @block.gpsimd
            def _(pool):
                for t in range(NBLK):
                    for k in range(K):
                        pool.indirect_dma_start(
                            out=got(t, k), out_offset=None, in_=m.answers[0:UNITS[l] * UR, :],
                            in_offset=bass.IndirectOffsetOnAxis(ap=m.answer_row[k][:, t:t + 1], axis=0)
                        ).then_inc(arrived[t // TU], 16)

            @block.vector
            def _(v):
                for g in range(CH):
                    v.wait_ge(arrived[g], 16 * TU * K)
                    for k in range(K):
                        for t in range(g * TU, (g + 1) * TU):
                            w = m.weight[k][:, t:t + 1]
                            x = m.X[:, t * D:(t + 1) * D]
                            if K == 1:
                                v.tensor_scalar(got(t, k), got(t, k), w, None, ALU.mult)
                            else:
                                add = v.scalar_tensor_tensor(x, got(t, k), w, x, ALU.mult, ALU.add)
                        if K == 2 and k == 0:
                            add.then_inc(first_added, 1)
                            v.wait_ge(first_added, g + 1)


def unit_experts(nc, m, l):
    F, func, U = FFN[l]["F"], FFN[l]["act"], UNITS[l]
    FC, TT = F // P, UR // B
    with nc.cleanup_on_exit():
        sem = m.sem
        wide, more = Arena(m.bufa), Arena(m.bufb)
        ht = [wide.take(P, [FC, UR]) for _ in range(2)]
        xT = [wide.take(P, [2, UR]) for _ in range(2)]
        xin = [wide.take(B, [TT, D]) for _ in range(2)]
        w1, w2 = [more.take(P, [2, F]) for _ in range(2)], [more.take(P, [FC, D]) for _ in range(2)]
        b2, y = [more.take(B, [D]) for _ in range(2)], [more.take(B, [TT, D]) for _ in range(2)]
        pt, psy = ([m.psum(f"{n}{i}") for i in range(2)] for n in ("pt", "psy"))
        psh = [m.psum(f"psh{i}") for i in range(4)]
        w_in, stored = ([sem(f"{n}{k}") for k in range(2)] for n in ("w_in", "stored"))
        turned, lifted = sem("turned"), sem("lifted")
        h_ready, h_done = sem("h_ready"), sem("h_done")
        y_ready, y_out = sem("y_ready"), sem("y_out")
        b1 = m.cols[:, col_at(f"L{l}_ffn_b1"):][:, 0:EXP * FC]
        rows_of = lambda table, u: table[ds(u * UR, UR), :].rearrange("(t p) w -> p t w", p=B)

        def expert_of(eng, u):
            return eng.value_load(m.units[0:1, ds(u, 1)], min_val=0, max_val=EXP - 1)

        with nc.Block() as block:
            @block.sync
            def _(sp):
                def load_unit(u, k):
                    e = expert_of(sp, u)
                    sp.dma_start(xin[k], rows_of(m.tokens, u)).then_inc(w_in[k], 16)
                    sp.dma_start(w1[k], m.a[f"L{l}_ffn_W1"][ds(e, 1)].rearrange(
                        "a p c f -> (a p) c f")).then_inc(w_in[k], 16)
                    sp.dma_start(w2[k], m.a[f"L{l}_ffn_W2"][ds(e, 1)].rearrange(
                        "a p c f -> (a p) c f")).then_inc(w_in[k], 16)
                    sp.dma_start(b2[k], m.a[B2S[l]][ds(e, 1), :].broadcast_to([B, D])).then_inc(w_in[k], 16)

                def store(i, k):
                    sp.wait_ge(y_out, i * (2 * TT) + (k * TT + TT + 2))
                    sp.dma_start(rows_of(m.answers, i * 2 + k), y[k]).then_inc(stored[k], 16)

                for k in range(2):
                    load_unit(k, k)
                with sp.Fori(0, U // 2 - 1) as i:
                    for k in range(2):
                        store(i, k)
                        load_unit(i * 2 + (k + 2), k)
                for k in range(2):
                    store(U // 2 - 1, k)
                for k in range(2):
                    sp.wait_ge(stored[k], 16 * (U // 2) + 16)

            @block.tensor
            def _(pe):
                pe.sem_inc(h_ready, 2 * FC)
                pe.sem_inc(y_ready, 2 * TT)

                def transposes(i, k):
                    pe.wait_ge(w_in[k], i * 64 + 64)
                    pe.wait_ge(lifted, i * 2 + (k + 1))
                    for h in range(2):
                        for t in range(TT):
                            tr = pe.transpose(pt[h][:, t * B:(t + 1) * B], xin[k][:, t, h * P:(h + 1) * P],
                                              m.cst[:B, C_ID:C_ID + B])
                    tr.then_inc(turned, 1)

                def hidden(i, k):
                    pe.wait_ge(lifted, i * 2 + (k + 2))
                    for f in range(FC):
                        pe.wait_ge(h_done, i * (2 * FC) + (k * FC + f + 1))
                        for h in range(2):
                            mm = pe.matmul(psh[f % 4][:, 0:UR], w1[k][:, h, f * P:(f + 1) * P], xT[k][:, h, :],
                                           start=(h == 0), stop=(h == 1))
                        mm.then_inc(h_ready, 1)

                def outputs(i, k):
                    pe.wait_ge(h_done, i * (2 * FC) + (k * FC + FC + 4))
                    for t in range(TT):
                        pe.wait_ge(y_out, i * (2 * TT) + (k * TT + t + 1))
                        for f in range(FC):
                            mm = pe.matmul(psy[t % 2][:B, 0:D], ht[k][:, f, t * B:(t + 1) * B], w2[k][:, f, :],
                                           start=(f == 0), stop=(f == FC - 1))
                        mm.then_inc(y_ready, 1)

                over(pe, U, 2, (hidden, 0), (transposes, 1), (outputs, 0))

            @block.scalar
            def _(act):
                act.sem_inc(h_done, 4)
                act.sem_inc(lifted, 1)

                def activate(i, k):
                    e = expert_of(act, i * 2 + k)
                    hold(act, y_ready, i * (2 * TT) + (k * TT + TT))
                    for f in range(FC):
                        hold(act, h_ready, i * (2 * FC) + (k * FC + f + 1 + 2 * FC))
                        act.activation(ht[k][:, f, :], psh[f % 4][:, 0:UR], func,
                                       bias=b1[:, ds(e * FC + f, 1)]).then_inc(h_done, 1)

                def lift(i, k):
                    act.wait_ge(turned, i * 2 + (k + 1))
                    act.wait_ge(h_ready, i * (2 * FC) + (k * FC + FC))
                    for h in range(2):
                        up = act.activation(xT[k][:, h, :], pt[h][:, 0:UR], ACT.Copy)
                    up.then_inc(lifted, 1)

                over(act, U, 2, (activate, 0), (lift, 1))

            @block.vector
            def _(v):
                v.sem_inc(y_out, 2)
                for k in range(2):
                    v.sem_inc(stored[k], 16)

                def out(i, k):
                    v.wait_ge(stored[k], i * 16 + 16)
                    for t in range(TT):
                        v.wait_ge(y_ready, i * (2 * TT) + (k * TT + t + 1 + 2 * TT))
                        v.tensor_tensor(y[k][:, t, :], psy[t % 2][:B, 0:D], b2[k], ALU.add).then_inc(y_out, 1)

                over(v, U, 2, (out, 0))


def bias_out(nc, m, l, coef, Y, fresh):
    with nc.cleanup_on_exit():
        sb, sem = m.sb, m.sem
        b2 = sb("b2", [EXP, D], F32)
        st = sb("st", [B, TU, EXP], F32)
        cT = sb("cT", [EXP, TU, B], F32)
        ps = [m.psum(f"ps{i}") for i in range(TU)]
        w_in, staged, turned, lifted, product, added = (
            sem(n) for n in ("w_in", "staged", "turned", "lifted", "product", "added"))
        with nc.Block() as block:
            @block.sync
            def _(sp):
                sp.dma_start(b2[:, :], m.a[B2S[l]]).then_inc(w_in, 16)
                sp.wait_ge(w_in, 16)

            @block.vector
            def _(v):
                v.sem_inc(added, TU)
                with v.Fori(0, NBLK // TU) as i:
                    v.wait_ge(turned, i * TU + TU)
                    for k in range(TU):
                        v.tensor_scalar(st[:, k, :], coef[:, ds((i * TU + k) * EXP, EXP)], 1.0, None,
                                        ALU.mult).then_inc(staged, 1)
                    for k in range(TU):
                        v.wait_ge(product, i * TU + (k + 1 + TU))
                        y = Y[:, ds((i * TU + k) * D, D)]
                        if fresh:
                            v.tensor_scalar(y, ps[k][:B, P:P + D], 1.0, None, ALU.mult).then_inc(added, 1)
                        else:
                            v.tensor_tensor(y, y, ps[k][:B, P:P + D], ALU.add).then_inc(added, 1)

            @block.scalar
            def _(act):
                with act.Fori(0, NBLK // TU) as i:
                    for k in range(TU):
                        act.wait_ge(turned, i * TU + (k + 1 + TU))
                        act.wait_ge(product, i * TU + TU)
                        act.activation(cT[:, k, :], ps[k][:EXP, 0:B], ACT.Copy).then_inc(lifted, 1)

            @block.tensor
            def _(pe):
                pe.sem_inc(turned, TU)
                pe.sem_inc(product, TU)
                pe.wait_ge(w_in, 16)
                with pe.Fori(0, NBLK // TU) as i:
                    for k in range(TU):
                        pe.wait_ge(staged, i * TU + (k + 1))
                        pe.wait_ge(added, i * TU + (k + 1))
                        pe.transpose(ps[k][:EXP, 0:B], st[:, k, :], m.cst[:B, C_ID:C_ID + B]).then_inc(turned, 1)
                    for k in range(TU):
                        pe.wait_ge(lifted, i * TU + (k + 1))
                        pe.matmul(ps[k][:B, P:P + D], cT[:, k, :], b2[:, :], start=True,
                                  stop=True).then_inc(product, 1)


HALVES = [(0, 3), (3, 2)]
CH = NBLK // TU


def experts(nc, m, l, XT, coef, Y):
    F, func = FFN[l]["F"], FFN[l]["act"]
    FC = F // P
    deep = l == 2
    layers = 2 if deep else 1
    with nc.cleanup_on_exit():
        sb, sem = m.sb, m.sem
        w1 = [m.bufb[:, k * 2 * F:(k + 1) * 2 * F].rearrange("p (c f) -> p c f", c=2) for k in range(2)]
        wm = [sb(f"wm_{k}", [P, 2, F], F32) for k in range(2)] if deep else None
        w2 = [sb(f"w2_{k}", [P, FC, D], F32) for k in range(2)]
        ht = [m.bufa[:, 2 * NODES + k * FC * 375:2 * NODES + (k + 1) * FC * 375] for k in range(2)]
        ht2 = [m.bufa[:, 2 * NODES + (2 + k) * FC * 375:2 * NODES + (3 + k) * FC * 375] for k in range(2)] if deep else None
        sc = sb("sc", [P, 4, EXP * FC], F32) if deep else None
        psh = [m.psum(f"psh{i}") for i in range(4)]
        psy = [m.psum(f"psy{i}") for i in range(4)]
        w_in = [sem(f"w_in{k}") for k in range(2)]
        h_ready, h_done, y_ready, y_done = (sem(n) for n in ("h_ready", "h_done", "y_ready", "y_done"))
        scaled, steps, variances, stds = sem("scaled"), sem("steps"), sem("variances"), sem("stds")
        ndma = 3 if deep else 2
        b1 = m.cols[:, col_at(f"L{l}_ffn_b1"):][:, 0:EXP * FC]
        HB = FC * layers
        with nc.Block() as block:
            @block.sync
            def _(sp):
                def load_expert(e, k):
                    sp.dma_start(w1[k], m.a[f"L{l}_ffn_W1"][ds(e, 1)].rearrange(
                        "a p c f -> (a p) c f")).then_inc(w_in[k], 16)
                    if deep:
                        sp.dma_start(wm[k][:, :, :], m.a["L2_ffn_Wm"][ds(e, 1)].rearrange(
                            "a p c f -> (a p) c f")).then_inc(w_in[k], 16)
                    sp.dma_start(w2[k][:, :, :], m.a[f"L{l}_ffn_W2"][ds(e, 1)].rearrange(
                        "a p c f -> (a p) c f")).then_inc(w_in[k], 16)

                for k in range(2):
                    load_expert(k, k)
                with sp.Fori(1, EXP // 2) as e2:
                    for k in range(2):
                        sp.wait_ge(y_ready, (e2 * 2 + k) * NBLK - NBLK + YR)
                        load_expert(e2 * 2 + k, k)
                for k in range(2):
                    sp.wait_ge(w_in[k], 16 * ndma * (EXP // 2))

            @block.tensor
            def _(pe):
                pe.sem_inc(y_ready, YR)
                with pe.Fori(0, EXP // 2) as e2:
                    for k in range(2):
                        hold(pe, w_in[k], e2 * (16 * ndma) + 16 * ndma)
                        with pe.Fori(0, CH) as c:
                            for half, (t0, tn) in enumerate(HALVES):
                                u = ((e2 * 2 + k) * CH + c) * 2 + half
                                n = tn * B
                                for f in range(FC):
                                    pe.wait_ge(h_done, u * HB + (f + 1))
                                    for h in range(2):
                                        mm = pe.matmul(psh[f % 4][:, 0:n], w1[k][:, h, f * P:(f + 1) * P],
                                                       XT[:, ds(c * (TU * B) + (h * NODES + t0 * B), n)],
                                                       start=(h == 0), stop=(h == 1))
                                    mm.then_inc(h_ready, 1)
                                src = ht[half]
                                if deep:
                                    for f in range(FC):
                                        pe.wait_ge(h_done, u * HB + (FC + 4))
                                        for h in range(FC):
                                            mm = pe.matmul(psh[(FC + f) % 4][:, 0:n], wm[k][:, h, f * P:(f + 1) * P],
                                                           src[:, h * 375:h * 375 + n], start=(h == 0),
                                                           stop=(h == FC - 1))
                                        mm.then_inc(h_ready, 1)
                                    src = ht2[half]
                                pe.wait_ge(h_done, u * HB + (HB + 4))
                                for t in range(tn):
                                    pe.wait_ge(y_done, ((e2 * 2 + k) * CH + c) * TU + (t0 + t + 1 if t0 + t else YB))
                                    for f in range(FC):
                                        mm = pe.matmul(psy[(t0 + t) % 4][:B, 0:D],
                                                       src[:, f * 375 + t * B:f * 375 + (t + 1) * B],
                                                       w2[k][:, f, :], start=(f == 0), stop=(f == FC - 1))
                                    mm.then_inc(y_ready, 1)

            @block.scalar
            def _(act):
                act.sem_inc(h_done, 4)
                if deep:
                    act.wait_ge(variances, 1)
                    act.activation(sc[:, 0:1, :], sc[:, 0:1, :], ACT.Sqrt, bias=m.cst[:, C_EPS + 1:C_EPS + 2])
                    act.activation(sc[:, 2:3, :], sc[:, 2:3, :], ACT.Sqrt,
                                   bias=m.cst[:, C_EPS + 1:C_EPS + 2]).then_inc(stds, 1)
                    act.wait_ge(scaled, 1)
                with act.Fori(0, EXP * CH) as ec:
                    for half, (t0, tn) in enumerate(HALVES):
                        u = ec * 2 + half
                        n = tn * B
                        hold(act, y_ready, ec * TU + (t0 + tn) - TU + YR)
                        for lay in range(layers):
                            dst = (ht, ht2)[lay][half]
                            for f in range(FC):
                                at = (ec // CH) * FC + f
                                hold(act, h_ready, u * HB + (lay * FC + f + 1))
                                if deep:
                                    act.activation(dst[:, f * 375:f * 375 + n], psh[(lay * FC + f) % 4][:, 0:n], func,
                                                   bias=sc[:, 2 * lay + 1, ds(at, 1)],
                                                   scale=sc[:, 2 * lay, ds(at, 1)]).then_inc(h_done, 1)
                                else:
                                    act.activation(dst[:, f * 375:f * 375 + n], psh[f % 4][:, 0:n], func,
                                                   bias=b1[:, ds(at, 1)]).then_inc(h_done, 1)

            @block.vector
            def _(v):
                ch = Chain(v, steps)
                link = ch.link
                if deep:
                    col = lambda n: m.cols[:, col_at(f"L2_ffn_{n}"):][:, 0:EXP * FC]
                    link(v.tensor_copy(sc[:, 0, :], col("v1")))
                    link(v.tensor_copy(sc[:, 2, :], col("v2")))
                    v.sem_inc(variances, 1)
                    v.wait_ge(stds, 1)
                    for i in range(2):
                        s, t = sc[:, 2 * i, :], sc[:, 2 * i + 1, :]
                        link(v.reciprocal(s, s))
                        link(v.tensor_tensor(s, s, col(f"g{i + 1}"), ALU.mult))
                        link(v.tensor_tensor(t, col(f"b{i + 1}"), col(f"m{i + 1}"), ALU.subtract))
                        link(v.tensor_tensor(t, t, s, ALU.mult))
                        link(v.tensor_tensor(t, t, col(f"be{i + 1}"), ALU.add))
                    v.sem_inc(scaled, 1)
                v.sem_inc(y_done, YB)
                with v.Fori(0, EXP * CH) as ec:
                    for t in range(TU):
                        tile = (ec % CH) * TU + t
                        y = Y[:, ds(tile * D, D)]
                        v.wait_ge(y_ready, ec * TU + (t + 1 + YR))
                        v.scalar_tensor_tensor(y, psy[t % 4][:B, 0:D], coef[:, ds(tile * EXP + ec // CH, 1)], y,
                                               ALU.mult, ALU.add).then_inc(y_done, 1)


YB = 4
YR = TU


def finite_residual(nc, m, Y):
    T = m.bufa[:B, 0:XW]
    big = 3.4028234663852886e38
    with nc.cleanup_on_exit():
        steps = m.sem("steps")
        mask = m.bufa[:B, XW:2 * XW].bitcast(I32)
        with nc.Block() as block:
            @block.vector
            def _(v):
                c = Chain(v, steps)
                c.link(v.memset(T, 0.0))
                c.link(v.tensor_tensor(mask, Y, Y, ALU.is_equal))
                c.link(v.copy_predicated(T, mask, Y))
                c.link(v.tensor_scalar(mask, T, big, None, ALU.is_gt))
                c.link(v.memset(Y, 1e4))
                c.link(v.copy_predicated(T, mask, Y))
                c.link(v.tensor_scalar(mask, T, -big, None, ALU.is_lt))
                c.link(v.memset(Y, -1e4))
                c.link(v.copy_predicated(T, mask, Y))
                v.tensor_tensor(m.X[:, :], m.X[:, :], T, ALU.add)


def gcn(nc, m, XN):
    dinv = m.small[:B, 1330:1355]
    HT = m.bufb[:, 0:4 * NODES]
    bns = m.small[:, 400:416]
    with nc.cleanup_on_exit():
        rooted = m.sem("rooted")
        with nc.Block() as block:
            @block.scalar
            def _(act):
                act.activation(dinv, m.deg, ACT.Sqrt, bias=m.cst[:B, C_ONE:C_ONE + 1]).then_inc(rooted, 1)

            @block.vector
            def _(v):
                v.wait_ge(rooted, 1)
                v.reciprocal(dinv, dinv).then_inc(rooted, 1)
                v.wait_ge(rooted, 2)
                with v.Fori(0, NBLK // TU) as i:
                    for k in range(TU):
                        t = i * TU + k
                        v.tensor_scalar(m.bufa[:B, ds(t * D, D)], XN[:, ds(t * D, D)], dinv[:, ds(t, 1)], None,
                                        ALU.mult)
    agg = m.bufa[:B, 0:XW]
    store_table(nc, m, agg, m.table, D)
    aggregate(nc, m, "dst", m.table, D, False, False, Arena(m.bufb))
    vT = m.bufa[:, XW:XW + 2 * NODES]
    to_features(nc, m, agg, D, dinv, vT, None)
    feature_linear(nc, m, vT, "L1_gnn_W1", m.cols[:, col_at("L1_gnn_b1"):][:, 0:4], HT)
    batch_stats(nc, m, HT, 1, bns)
    wide_agg = m.bufa[:B, 0:NBLK * HID]
    bn_linear(nc, m, HT, bns, "L1_gnn_W2", HID, dinv, wide_agg)
    store_table(nc, m, wide_agg, m.table2, HID)
    aggregate(nc, m, "dst", m.table2, HID, False, False, Arena(m.bufb))
    to_features(nc, m, wide_agg, HID, dinv, HT, m.cols[:, col_at("L1_gnn_b2"):][:, 0:4])
    batch_stats(nc, m, HT, 2, bns)
    bn_linear(nc, m, HT, bns, "L1_gnn_W3", D, dinv, agg)
    store_table(nc, m, agg, m.table, D)
    aggregate(nc, m, "dst", m.table, D, False, False, Arena(m.bufb))
    with nc.cleanup_on_exit():
        steps = m.sem("steps")
        with nc.Block() as block:
            @block.vector
            def _(v):
                c = Chain(v, steps)
                b3 = m.rows[:B, row_at("L1_gnn_b3"):][:, 0:D].unsqueeze(1).broadcast_to([B, NBLK, D])
                xv = m.X[:, :].rearrange("p (t w) -> p t w", w=D)
                with v.Fori(0, NBLK // TU) as i:
                    c.enter(i, 1)
                    for k in range(TU):
                        t = i * TU + k
                        x = m.X[:, ds(t * D, D)]
                        last = v.scalar_tensor_tensor(x, agg[:, ds(t * D, D)], dinv[:, ds(t, 1)], x, ALU.mult, ALU.add)
                    c.link(last)
                c.leave(NBLK // TU)
                v.tensor_tensor(xv, xv, b3, ALU.add)


def to_features(nc, m, src, width, scale, dst, bias):
    KC = width // P
    with nc.cleanup_on_exit():
        st = m.sb("st", [B, TU, width], F32)
        ps = [m.psum(f"ps{i}") for i in range(TU)]
        staged, turned, lifted = m.sem("staged"), m.sem("turned"), m.sem("lifted")
        with nc.Block() as block:
            @block.vector
            def _(v):
                with v.Fori(0, NBLK // TU) as i:
                    v.wait_ge(turned, i * TU + TU)
                    for k in range(TU):
                        t = i * TU + k
                        v.tensor_scalar(st[:, k, :], src[:, ds(t * width, width)], scale[:, ds(t, 1)], None,
                                        ALU.mult).then_inc(staged, 1)

            @block.tensor
            def _(pe):
                pe.sem_inc(turned, TU)
                with pe.Fori(0, NBLK // TU) as i:
                    for k in range(TU):
                        pe.wait_ge(staged, i * TU + (k + 1))
                        pe.wait_ge(lifted, i * TU + (k + 1))
                        for h in range(KC):
                            tr = pe.transpose(ps[k][:, h * B:(h + 1) * B], st[:, k, h * P:(h + 1) * P],
                                              m.cst[:B, C_ID:C_ID + B])
                        tr.then_inc(turned, 1)

            @block.scalar
            def _(act):
                act.sem_inc(lifted, TU)
                with act.Fori(0, NBLK // TU) as i:
                    for k in range(TU):
                        t = i * TU + k
                        hold(act, turned, t + (1 + TU))
                        for h in range(KC):
                            o = dst[:, ds(t * B + h * NODES, B)]
                            pt = ps[k][:, h * B:(h + 1) * B]
                            if bias is None:
                                up = act.activation(o, pt, ACT.Copy)
                            else:
                                up = act.activation(o, pt, ACT.Identity, bias=bias[:, h:h + 1])
                        up.then_inc(lifted, 1)


def feature_linear(nc, m, src, wname, bias, dst):
    with nc.cleanup_on_exit():
        w = m.sb("w", [P, 2, HID], F32)
        ps = [m.psum(f"ps{i}") for i in range(8)]
        w_in, ready, lifted = m.sem("w_in"), m.sem("ready"), m.sem("lifted")
        with nc.Block() as block:
            @block.sync
            def _(sp):
                sp.dma_start(w[:, :, :], m.a[wname]).then_inc(w_in, 16)
                sp.wait_ge(w_in, 16)

            @block.tensor
            def _(pe):
                pe.wait_ge(w_in, 16)
                with pe.Fori(0, CH) as c:
                    for half, (t0, tn) in enumerate(HALVES):
                        for f in range(4):
                            pe.wait_ge(lifted, c * 8 + (half * 4 + f + 1))
                            for h in range(2):
                                mm = pe.matmul(ps[half * 4 + f][:, 0:tn * B], w[:, h, f * P:(f + 1) * P],
                                               src[:, ds(c * (TU * B) + (h * NODES + t0 * B), tn * B)],
                                               start=(h == 0), stop=(h == 1))
                            mm.then_inc(ready, 1)

            @block.scalar
            def _(act):
                act.sem_inc(lifted, 8)
                with act.Fori(0, CH) as c:
                    for half, (t0, tn) in enumerate(HALVES):
                        for f in range(4):
                            hold(act, ready, c * 8 + (half * 4 + f + 1))
                            act.activation(dst[:, ds(c * (TU * B) + (f * NODES + t0 * B), tn * B)],
                                           ps[half * 4 + f][:, 0:tn * B], ACT.Identity,
                                           bias=bias[:, f:f + 1]).then_inc(lifted, 1)


def batch_stats(nc, m, HT, n, bns):
    with nc.cleanup_on_exit():
        st = m.sb("st", [P, 4, 2 * CH, 6], F32)
        mv = m.sb("mv", [P, 4, 2], F32)
        std = m.sb("std", [P, 4], F32)
        steps, var_ready, std_ready = m.sem("steps"), m.sem("var_ready"), m.sem("std_ready")
        with nc.Block() as block:
            @block.vector
            def _(v):
                c = Chain(v, steps)
                for ch in range(2 * CH):
                    t0, tn = HALVES[ch % 2]
                    at = (ch // 2) * TU * B + t0 * B
                    for f in range(4):
                        last = v.bn_stats(st[:, f, ch, :], HT[:, f * NODES + at:f * NODES + at + tn * B])
                c.link(last)
                for f in range(4):
                    last = v.bn_aggr(mv[:, f, :], st[:, f, :, :].rearrange("p c s -> p (c s)"))
                last.then_inc(var_ready, 1)
                v.wait_ge(std_ready, 1)
                c.link(v.reciprocal(std[:, :], std[:, :]))
                g = m.cols[:, col_at(f"L1_gnn_g{n}"):][:, 0:4]
                be = m.cols[:, col_at(f"L1_gnn_be{n}"):][:, 0:4]
                c.link(v.tensor_tensor(bns[:, 0:4], std[:, :], g, ALU.mult))
                c.link(v.tensor_tensor(std[:, :], mv[:, :, 0], bns[:, 0:4], ALU.mult))
                v.tensor_tensor(bns[:, 4:8], be, std[:, :], ALU.subtract)

            @block.scalar
            def _(act):
                act.wait_ge(var_ready, 1)
                act.activation(std[:, :], mv[:, :, 1], ACT.Sqrt,
                               bias=m.cst[:, C_EPS:C_EPS + 1]).then_inc(std_ready, 1)


def bn_linear(nc, m, HT, bns, wname, wide, dinv, dst):
    with nc.cleanup_on_exit():
        w = m.sb("w", [P, 4, wide], F32)
        st = m.sb("st", [P, TU, 4 * B], F32)
        ps = [m.psum(f"ps{i}") for i in range(TU)]
        w_in, staged, product, taken = m.sem("w_in"), m.sem("staged"), m.sem("product"), m.sem("taken")
        with nc.Block() as block:
            @block.sync
            def _(sp):
                sp.dma_start(w[:, :, :], m.a[wname]).then_inc(w_in, 16)
                sp.wait_ge(w_in, 16)

            @block.scalar
            def _(act):
                with act.Fori(0, NBLK // TU) as i:
                    hold(act, product, i * TU + TU)
                    for k in range(TU):
                        for f in range(4):
                            up = act.activation(st[:, k, f * B:(f + 1) * B],
                                                HT[:, ds((i * TU + k) * B + f * NODES, B)], ACT.Relu,
                                                bias=bns[:, 4 + f:5 + f], scale=bns[:, f:f + 1])
                        up.then_inc(staged, 1)

            @block.tensor
            def _(pe):
                pe.sem_inc(product, TU)
                pe.wait_ge(w_in, 16)
                with pe.Fori(0, NBLK // TU) as i:
                    for k in range(TU):
                        pe.wait_ge(staged, i * TU + (k + 1))
                        pe.wait_ge(taken, i * TU + (k + 1))
                        for f in range(4):
                            mm = pe.matmul(ps[k][:B, 0:wide], st[:, k, f * B:(f + 1) * B], w[:, f, :],
                                           start=(f == 0), stop=(f == 3))
                        mm.then_inc(product, 1)

            @block.vector
            def _(v):
                v.sem_inc(taken, TU)
                with v.Fori(0, NBLK // TU) as i:
                    for k in range(TU):
                        t = i * TU + k
                        v.wait_ge(product, i * TU + (k + 1 + TU))
                        v.tensor_scalar(dst[:, ds(t * wide, wide)], ps[k][:B, 0:wide], dinv[:, ds(t, 1)], None,
                                        ALU.mult).then_inc(taken, 1)




def gat(nc, m, l, XN):
    H = 8 if l == 2 else 4
    C = D // H
    W = D + H
    HB = m.bufa[:B, 0:NBLK * W]
    hb3 = HB.rearrange("p (t w) -> p t w", w=W)
    acc = m.bufb[:B, NT * 8:NT * 8 + NBLK * W]
    acc3 = acc.rearrange("p (t w) -> p t w", w=W)
    alpha = m.bufb[:, 0:NT * H]
    M = m.small[:B, 0:NBLK * H]
    asrc = m.small[:B, 200:200 + NBLK * H]
    self_e = m.small[:B, 400:400 + NBLK * H]
    names = {2: ("L2_gnn_a_src", "L2_gnn_a_dst", "L2_gnn_bias"),
             3: ("L3_gnn_att_src", "L3_gnn_att_dst", "L3_gnn_bias")}[l]
    vec = [m.rows[:B, row_at(n):][:, 0:D].unsqueeze(1).broadcast_to([B, NBLK, D]) for n in names]
    t3 = lambda ap: ap.rearrange("p (t h) -> p t h", h=H)
    token_linear(nc, m, XN, m.a[f"L{l}_gnn_W"], D,
                 lambda v, t, ps: v.tensor_scalar(HB[:, ds(t * W, D)], ps, 1.0, None, ALU.mult))
    with nc.cleanup_on_exit():
        steps, tables = m.sem("steps"), m.sem("tables")
        ready = m.sem("ready")
        tmp = m.bufb[:B, 0:XW]
        with nc.Block() as block:
            @block.vector
            def _(v):
                c = Chain(v, steps)
                tv = tmp.rearrange("p (t w) -> p t w", w=D)
                c.link(v.tensor_tensor(tv, hb3[:, :, 0:D], vec[0], ALU.mult))
                v.tensor_reduce(asrc, tmp.rearrange("p (q c) -> p q c", c=C), AX.X, ALU.add).then_inc(ready, 1)
                v.wait_ge(ready, 1)
                c.link(v.tensor_tensor(tv, hb3[:, :, 0:D], vec[1], ALU.mult))
                c.link(v.tensor_reduce(self_e, tmp.rearrange("p (q c) -> p q c", c=C), AX.X, ALU.add))
                c.link(v.tensor_scalar(hb3[:, :, D:W], t3(self_e), 1.0, None, ALU.mult))
                if l == 2:
                    v.memset(M, -BIG)
                else:
                    c.link(v.tensor_tensor(self_e, self_e, asrc, ALU.add))
                    c.link(v.scalar_tensor_tensor(self_e, self_e, 0.2, self_e, ALU.mult, ALU.max))
                    v.tensor_copy(M, self_e)

            @block.sync
            def _(sp):
                sp.dma_start(m.table.rearrange("(t p) w -> p t w", p=B), hb3[:, :, 0:D]).then_inc(tables, 16)
                sp.wait_ge(ready, 1)
                sp.dma_start(m.tablea[H].rearrange("(t p) w -> p t w", p=B), t3(asrc)).then_inc(tables, 16)
                sp.wait_ge(tables, 32)
    edge_scores(nc, m, H, l == 2, HB, W, alpha)
    edge_maxima(nc, m, H, alpha, M, Arena(m.bufa[:, NBLK * W:]))
    if l == 2:
        with nc.cleanup_on_exit():
            with nc.Block() as block:
                @block.vector
                def _(v):
                    v.memset(acc, 0.0)
    else:
        with nc.cleanup_on_exit():
            steps, shifted, exped = m.sem("steps"), m.sem("shifted"), m.sem("exped")
            with nc.Block() as block:
                @block.vector
                def _(v):
                    v.tensor_tensor(self_e, self_e, M, ALU.subtract).then_inc(shifted, 1)
                    v.wait_ge(exped, 1)
                    v.tensor_scalar(acc3[:, :, D:W], t3(self_e), 1.0, None, ALU.mult)
                    with v.Fori(0, NBLK) as t:
                        for h in range(H):
                            v.tensor_scalar(acc[:, ds(t * W + h * C, C)], HB[:, ds(t * W + h * C, C)],
                                            self_e[:, ds(t * H + h, 1)], None, ALU.mult)

                @block.scalar
                def _(act):
                    act.wait_ge(shifted, 1)
                    act.activation(self_e, self_e, ACT.Exp).then_inc(exped, 1)
    edge_messages(nc, m, H, alpha, M, acc, W)
    with nc.cleanup_on_exit():
        steps, squared, rooted = m.sem("steps"), m.sem("squared"), m.sem("rooted")
        inv = M
        o = m.bufa[:B, 0:XW]
        ov = o.rearrange("p (t w) -> p t w", w=D)
        ss = m.small[:B, 700:700 + NBLK]
        with nc.Block() as block:
            @block.vector
            def _(v):
                c = Chain(v, steps)
                c.link(v.tensor_scalar(t3(inv), acc3[:, :, D:W], 1e-10, None, ALU.max))
                c.link(v.reciprocal(inv, inv))
                with v.Fori(0, NBLK) as t:
                    c.enter(t, 1)
                    for h in range(H):
                        last = v.tensor_scalar(o[:, ds(t * D + h * C, C)], acc[:, ds(t * W + h * C, C)],
                                               inv[:, ds(t * H + h, 1)], None, ALU.mult)
                    c.link(last)
                c.leave(NBLK)
                c.link(v.tensor_tensor(ov, ov, vec[2], ALU.add))
                if l == 3:
                    sq = acc[:, 0:XW]
                    c.link(v.tensor_scalar(o, o, 0.0, None, ALU.max))
                    c.link(v.tensor_tensor(sq, o, o, ALU.mult))
                    v.tensor_reduce(ss, sq.rearrange("p (t w) -> p t w", w=D), AX.X, ALU.add).then_inc(squared, 1)
                    v.wait_ge(rooted, 1)
                    c.link(v.tensor_scalar(ss, ss, 1e-12, None, ALU.max))
                    c.link(v.reciprocal(ss, ss))
                    with v.Fori(0, NBLK) as t:
                        x = m.X[:, ds(t * D, D)]
                        v.scalar_tensor_tensor(x, o[:, ds(t * D, D)], ss[:, ds(t, 1)], x, ALU.mult, ALU.add)
                else:
                    v.tensor_tensor(m.X[:, :], m.X[:, :], o, ALU.add)

            @block.scalar
            def _(act):
                if l == 3:
                    act.wait_ge(squared, 1)
                    act.activation(ss, ss, ACT.Sqrt).then_inc(rooted, 1)


def edge_scores(nc, m, H, encoded, HB, W, alpha):
    lst = fields(m, "dst")
    n0 = 0 if encoded else D
    NW = W - n0
    C = D // H
    with nc.cleanup_on_exit():
        sb, sem, psum = m.sb, m.sem, m.psum
        space = Arena(m.bufb[:, NT * 8:])
        idx = sb("idx", [P, RT], I32)
        sums, part, asg = (space.take(P, [RT, H]) for _ in range(3))
        onehot, onehotT = space.take(P, [RT, B]), space.take(B, [RT, P])
        rec, recT = space.take(P, [RT, PF]), space.take(PF, [2 * EG, P])
        enc = space.take(P, [2 * EG, D]) if encoded else None
        ew = sb("ew", [PF, D], F32)
        pt, pr, pw, pe_ = ([psum(f"{n}{i}") for i in range(2)] for n in ("pt", "pr", "pw", "pe"))
        picked, hot_ready, turned, lifted = sem("picked"), sem("hot_ready"), sem("turned"), sem("lifted")
        spread_done, enc_sums, enc_done, combined, steps = (
            sem(n) for n in ("spread_done", "enc_sums", "enc_done", "combined", "steps"))
        w_in, scored = sem("w_in"), sem("scored")
        gathered = [sem(f"gathered{g}") for g in range(RING)]
        with nc.Block() as block:
            @block.sync
            def _(sp):
                sp.dma_start(ew[:, :], m.a["edge_w"]).then_inc(w_in, 16)
                sp.wait_ge(w_in, 16)

            @block.gpsimd
            def _(pool):
                pool_gathers(pool, m, "dst", idx, picked, scored, 1, m.tablea[H], lambda k: asg[:, k, :], gathered)

            @block.vector
            def _(v):
                v.sem_inc(combined, 2)
                v.sem_inc(scored, RING)

                def one_hots(i, g):
                    v.wait_ge(turned, i * RING + (g + 1))
                    if encoded:
                        v.tensor_scalar(rec[:, ring(g), :].rearrange("p c f -> p (c f)").bitcast(I32),
                                        lst[:, ds(i * RT + g * EG, EG), :].rearrange("p c f -> p (c f)").bitcast(I32),
                                        0, None, ALU.bitwise_or)
                    vector_onehots(v, m, lst, i, g, onehot, hot_ready)

                def combine(i, g):
                    G1 = i * RING + (g + 1)
                    s3 = sums[:, ring(g), :]
                    v.wait_ge(gathered[g], i * (16 * EG) + 16 * EG)
                    if encoded:
                        for j in range(g * EG, (g + 1) * EG):
                            q = j % (2 * EG)
                            tgt = pw[j % 2]
                            v.wait_ge(spread_done, i * RT + (j + 1))
                            if j % 2 == 0:
                                v.wait_ge(enc_done, i * (RT // 2) + (j // 2 + 3))
                            v.tensor_tensor(enc[:, q, :], enc[:, q, :], tgt[:, 0:D], ALU.mult)
                            v.scalar_tensor_tensor(sums[:, j, :], asg[:, j, :], lst[:, ds(i * RT + j, 1), 6],
                                                   tgt[:, NW - H:NW], ALU.add, ALU.add).then_inc(combined, 1)
                        v.wait_ge(combined, i * RT + (g * EG + EG + 2))
                        q0 = (g % 2) * EG
                        v.tensor_reduce(part[:, ring(g), :],
                                        enc[:, q0:q0 + EG, :].rearrange("p k (h c) -> p k h c", c=C),
                                        AX.X, ALU.add).then_inc(steps, 1)
                        v.wait_ge(steps, i * (2 * RING) + (2 * g + 1))
                        v.tensor_tensor(s3, s3, part[:, ring(g), :], ALU.add).then_inc(steps, 1)
                        v.wait_ge(steps, i * (2 * RING) + (2 * g + 2))
                    else:
                        v.wait_ge(spread_done, i * RING + (g + 1 + RING))
                        v.tensor_tensor(s3, asg[:, ring(g), :],
                                        pw[g % 2][:, 0:EG * H].rearrange("p (k h) -> p k h", h=H),
                                        ALU.add).then_inc(combined, 1)
                        v.wait_ge(combined, i * RING + (g + 3))
                        for j in range(g * EG, (g + 1) * EG):
                            o = v.tensor_scalar(sums[:, j, :], sums[:, j, :], lst[:, ds(i * RT + j, 1), 6], None,
                                                ALU.add)
                        o.then_inc(steps, 1)
                        v.wait_ge(steps, G1)
                    sv = s3.rearrange("p c h -> p (c h)")
                    v.scalar_tensor_tensor(alpha[:, ds(i * (RT * H) + g * EG * H, EG * H)], sv, 0.2, sv, ALU.mult,
                                           ALU.max).then_inc(scored, 1)

                over_groups(v, (one_hots, 3), (combine, 0))

            @block.tensor
            def _(pe):
                pe.sem_inc(turned, RING)
                pe.sem_inc(*((enc_sums, 4) if encoded else (spread_done, RING)))
                pe.wait_ge(w_in, 16)

                def transposes(i, g):
                    G1 = i * RING + (g + 1)
                    pe.wait_ge(hot_ready, G1)
                    pe.wait_ge(lifted, G1)
                    for q in range(EG):
                        tr = pe.transpose(pt[g % 2][:B, q * P:(q + 1) * P], onehot[:, g * EG + q, :],
                                          m.cst[:, C_ID:C_ID + P])
                        if encoded:
                            tr = pe.transpose(pr[g % 2][:PF, q * P:(q + 1) * P], rec[:, g * EG + q, :],
                                              m.cst[:, C_ID:C_ID + P])
                    tr.then_inc(turned, 1)

                def spreads(i, g):
                    pe.wait_ge(lifted, i * RING + (g + 3))
                    if not encoded:
                        hold(pe, combined, i * RING + (g + 1))
                    for j in range(g * EG, (g + 1) * EG):
                        b = block_of(pe, m, "dst", i, j)
                        if encoded:
                            hold(pe, combined, i * RT + (j + 1))
                            pe.matmul(pw[j % 2][:, 0:NW], onehotT[:, j, :], HB[:, ds(b * W, NW)], start=True,
                                      stop=True).then_inc(spread_done, 1)
                        else:
                            mm = pe.matmul(pw[g % 2][:, (j % EG) * H:(j % EG + 1) * H], onehotT[:, j, :],
                                           HB[:, ds(b * W + n0, NW)], start=True, stop=True)
                    if not encoded:
                        mm.then_inc(spread_done, 1)

                def encodings(i, g):
                    pe.wait_ge(lifted, i * RING + (g + 3))
                    for j in range(g * EG, (g + 1) * EG, 2):
                        pe.wait_ge(enc_done, i * (RT // 2) + (j // 2 + 1))
                        for h in range(2):
                            mm = pe.matmul(pe_[(j // 2) % 2][:, h * D:(h + 1) * D], recT[:, (j + h) % (2 * EG), :],
                                           ew[:, :], start=True, stop=True)
                        mm.then_inc(enc_sums, 1)

                if encoded:
                    over_groups(pe, (transposes, 2), (encodings, 1), (spreads, 0))
                else:
                    over_groups(pe, (transposes, 1), (spreads, 0))

            @block.scalar
            def _(act):
                act.sem_inc(lifted, 2)
                if encoded:
                    act.sem_inc(enc_done, 2)

                def lift(i, g):
                    act.wait_ge(turned, i * RING + (g + 1 + RING))
                    if encoded:
                        act.wait_ge(enc_sums, i * (RT // 2) + (g * 2 + 2))
                        act.activation(recT[:, (g % 2) * EG:(g % 2 + 1) * EG, :].rearrange("p c e -> p (c e)"),
                                       pr[g % 2][:PF, :], ACT.Copy)
                    else:
                        act.wait_ge(spread_done, i * RING + (g + 1))
                    act.activation(onehotT[:, ring(g), :].rearrange("p c e -> p (c e)"), pt[g % 2][:B, :],
                                   ACT.Copy).then_inc(lifted, 1)

                def encode(i, g):
                    for h in range(EG // 2):
                        q = (g % 2) * EG + 2 * h
                        act.wait_ge(enc_sums, i * (RT // 2) + (g * 2 + h + 5))
                        act.wait_ge(scored, i * RING + (g + 3))
                        act.activation(enc[:, q:q + 2, :].rearrange("p c e -> p (c e)"), pe_[h % 2][:, :],
                                       ACT.Relu).then_inc(enc_done, 1)

                if encoded:
                    over_groups(act, (lift, 1), (encode, 0))
                else:
                    over_groups(act, (lift, 0))


def edge_maxima(nc, m, H, alpha, M, space):
    lst = fields(m, "dst")
    HG = H // 4
    K = 2 * H + 1
    NB = 4 // HG
    with nc.cleanup_on_exit():
        sem = m.sem
        dist, onehot = space.take(P, [2 * EG, B], BF16), space.take(P, [RT, B], BF16)
        al, alT = space.take(P, [RT, K + 1], BF16), space.take(K, [RT, P], BF16)
        identb, bigi = space.take(P, [P], BF16), space.take(P, [4, P], BF16)
        sel, top = space.take(K, [H, B], BF16), space.take(B, [RT, H])
        pt = [nc.alloc_psum_tensor(m.name(f"pt{i}"), [P, 1024], BF16) for i in range(2)]
        pm = [[m.psum(f"pm{i}{g}") for g in range(HG)] for i in range(NB)]
        made, al_ready, measured, hot_ready = sem("made"), sem("al_ready"), sem("measured"), sem("hot_ready")
        turned, lifted, masked, reduced, steps = (
            sem(n) for n in ("turned", "lifted", "masked", "reduced", "steps"))
        split, raised = sem("split"), sem("raised")
        with nc.Block() as block:
            @block.vector
            def _(v):
                c = Chain(v, steps)
                v.tensor_scalar(bigi, m.cst[:, C_ID:C_ID + P].unsqueeze(1).broadcast_to([P, 4, P]), BIG,
                                None, ALU.mult)
                v.tensor_scalar(identb, m.cst[:, C_ID:C_ID + P], 1.0, None, ALU.mult)
                v.memset(al, -BIG)
                c.link(v.tensor_tensor(m.small[:K, 1100:1100 + H], m.cst[:K, C_ID:C_ID + H],
                                       m.cst[:K, C_ID + H:C_ID + 2 * H], ALU.add))
                c.link(v.tensor_tensor(m.small[:K, 1100:1100 + H], m.small[:K, 1100:1100 + H],
                                       m.cst[:K, C_ID + 2 * H:C_ID + K].broadcast_to([K, H]), ALU.add))
                c.link(v.tensor_scalar(sel, m.small[:K, 1100:1100 + H].unsqueeze(2).broadcast_to([K, H, B]),
                                       1.0, None, ALU.mult))
                v.sem_inc(made, 1)
                v.sem_inc(reduced, NB)
                v.sem_inc(raised, 1)

                def parts(i, g):
                    a = alpha[:, ds(i * (RT * H) + g * EG * H, EG * H)].rearrange("p (c h) -> p c h", h=H)
                    v.wait_ge(turned, i * RING + (g + 1))
                    v.tensor_scalar(al[:, ring(g), 0:H], a, 1.0, None, ALU.mult).then_inc(split, 1)
                    v.wait_ge(split, i * RING + (g + 1))
                    v.tensor_tensor(al[:, ring(g), H:2 * H], a, al[:, ring(g), 0:H],
                                    ALU.subtract).then_inc(al_ready, 1)

                def reduce(i, g):
                    for j in range(g * EG, (g + 1) * EG):
                        v.wait_ge(masked, i * RT + (j + 1 + RT))
                        for h in range(HG):
                            r = v.tensor_reduce(top[:, j, 4 * h:4 * h + 4],
                                                pm[j % NB][h][:B, :].rearrange("p (h e) -> p h e", e=P), AX.X,
                                                ALU.max)
                        r.then_inc(reduced, 1)
                        if j > g * EG:
                            raise_max(i, j - 1)
                    raise_max(i, g * EG + EG - 1)

                def raise_max(i, j):
                    b = block_of(v, m, "dst", i, j)
                    part = M[:, ds(b * H, H)]
                    v.wait_ge(reduced, i * RT + (j + 1 + NB))
                    v.wait_ge(raised, i * RT + (j + 1))
                    v.tensor_tensor(part, part, top[:, j, :], ALU.max).then_inc(raised, 1)

                over_groups(v, (parts, 2), (reduce, 0))

            @block.tensor
            def _(pe):
                pe.sem_inc(masked, RT)
                pe.sem_inc(turned, RING)
                pe.wait_ge(made, 1)

                def transposes(i, g):
                    pe.wait_ge(al_ready, i * RING + (g + 1))
                    pe.wait_ge(lifted, i * RING + (g + 1))
                    for q in range(EG):
                        tr = pe.transpose(pt[g % 2][:K, q * P:(q + 1) * P], al[:, g * EG + q, 0:K], identb)
                    tr.then_inc(turned, 1)

                def masks(i, g):
                    pe.wait_ge(hot_ready, i * RING + (g + 3))
                    pe.wait_ge(lifted, i * RING + (g + 3))
                    for j in range(g * EG, (g + 1) * EG):
                        pe.wait_ge(reduced, i * RT + (j + 1))
                        for h in range(HG):
                            o = pm[j % NB][h][:B, :]
                            pe.matmul(o, onehot[:, j, :], bigi.rearrange("p a b -> p (a b)"), start=True,
                                      stop=False, skip_group_check=True)
                            for q in range(4):
                                mm = pe.matmul(o[:, q * P:(q + 1) * P], sel[:, 4 * h + q, :], alT[:, j, :],
                                               start=False, stop=(q == 3), skip_group_check=True)
                        mm.then_inc(masked, 1)

                over_groups(pe, (transposes, 1), (masks, 0))

            @block.scalar
            def _(act):
                act.sem_inc(lifted, 2)
                act.sem_inc(hot_ready, 2)

                def one_hots(i, g):
                    hold(act, masked, i * RT + (g * EG + EG))
                    act_onehots(act, m, lst, i, g, dist, onehot, measured, hot_ready)

                def lift(i, g):
                    act.wait_ge(turned, i * RING + (g + 1 + RING))
                    act.wait_ge(masked, i * RT + (g * EG + EG))
                    act.activation(alT[:, ring(g), :].rearrange("p c e -> p (c e)"), pt[g % 2][:K, 0:EG * P],
                                   ACT.Copy).then_inc(lifted, 1)

                over_groups(act, (one_hots, 1), (lift, 0))


def edge_messages(nc, m, H, alpha, M, acc, W):
    lst = fields(m, "dst")
    C = D // H
    with nc.cleanup_on_exit():
        sem, psum = m.sem, m.psum
        space = Arena(m.bufa)
        idx = m.sb("idx", [P, RT], I32)
        rows, onehot, onehotT = space.take(P, [RT, D]), space.take(P, [RT, B]), space.take(B, [RT, P])
        wt, msg = space.take(P, [RT, H]), space.take(P, [2 * EG, W])
        pt, pm = ([psum(f"{n}{i}") for i in range(2)] for n in ("pt", "pm"))
        pa = [psum(f"pa{i}") for i in range(EG)]
        picked, hot_ready, turned, lifted = sem("picked"), sem("hot_ready"), sem("turned"), sem("lifted")
        spread_done, shifted, exped = sem("spread_done"), sem("shifted"), sem("exped")
        msg_ready = sem("msg_ready")
        summed, added = sem("summed"), sem("added")
        gathered = [sem(f"gathered{g}") for g in range(RING)]
        with nc.Block() as block:
            @block.gpsimd
            def _(pool):
                pool_gathers(pool, m, "dst", idx, picked, msg_ready, 1, m.table, lambda k: rows[:, k, :], gathered)

            @block.vector
            def _(v):
                v.sem_inc(added, EG)
                v.sem_inc(shifted, 2)
                v.sem_inc(msg_ready, RING)

                def one_hots(i, g):
                    v.wait_ge(summed, i * RT + (g * EG + EG))
                    vector_onehots(v, m, lst, i, g, onehot, hot_ready)

                def shift(i, g):
                    v.wait_ge(spread_done, i * RING + (g + 1 + RING))
                    v.tensor_tensor(wt[:, ring(g), :].rearrange("p c h -> p (c h)"),
                                    alpha[:, ds(i * (RT * H) + g * EG * H, EG * H)], pm[g % 2][:, 0:EG * H],
                                    ALU.subtract).then_inc(shifted, 1)

                def messages(i, g):
                    q0 = (g % 2) * EG
                    v.wait_ge(exped, i * RING + (g + 1))
                    v.wait_ge(gathered[g], i * (16 * EG) + 16 * EG)
                    v.wait_ge(summed, i * RT + (g * EG + EG + RT // 2))
                    v.tensor_scalar(msg[:, q0:q0 + EG, D:W], wt[:, ring(g), :], 1.0, None, ALU.mult)
                    v.tensor_tensor(msg[:, q0:q0 + EG, 0:D].rearrange("p k (h c) -> p k h c", c=C),
                                    rows[:, ring(g), :].rearrange("p k (h c) -> p k h c", c=C),
                                    wt[:, ring(g), :].unsqueeze(3).broadcast_to([P, EG, H, C]),
                                    ALU.mult).then_inc(msg_ready, 1)

                def add(i, g):
                    for j in range(g * EG, (g + 1) * EG):
                        b = block_of(v, m, "dst", i, j)
                        part = acc[:, ds(b * W, W)]
                        v.wait_ge(summed, i * RT + (j + 1 + RT))
                        v.wait_ge(added, i * RT + (j + EG))
                        v.tensor_tensor(part, part, pa[j % EG][:B, 0:W], ALU.add).then_inc(added, 1)

                over_groups(v, (one_hots, 3), (messages, 1), (add, 0), (shift, 2))

            @block.tensor
            def _(pe):
                pe.sem_inc(spread_done, RING)
                pe.sem_inc(summed, RT)

                def transposes(i, g):
                    pe.wait_ge(hot_ready, i * RING + (g + 1))
                    pe.wait_ge(lifted, i * RING + (g + 1))
                    for q in range(EG):
                        tr = pe.transpose(pt[g % 2][:B, q * P:(q + 1) * P], onehot[:, g * EG + q, :],
                                          m.cst[:, C_ID:C_ID + P])
                    tr.then_inc(turned, 1)

                def spreads(i, g):
                    pe.wait_ge(lifted, i * RING + (g + 3))
                    hold(pe, shifted, i * RING + (g + 1))
                    for q in range(EG):
                        b = block_of(pe, m, "dst", i, g * EG + q)
                        mm = pe.matmul(pm[g % 2][:, q * H:(q + 1) * H], onehotT[:, g * EG + q, :],
                                       M[:, ds(b * H, H)], start=True, stop=True)
                    mm.then_inc(spread_done, 1)

                def sums(i, g):
                    pe.wait_ge(msg_ready, i * RING + (g + 1 + RING))
                    for j in range(g * EG, (g + 1) * EG):
                        pe.wait_ge(added, i * RT + (j + 1))
                        pe.matmul(pa[j % EG][:B, 0:W], onehot[:, j, :], msg[:, j % (2 * EG), :], start=True,
                                  stop=True).then_inc(summed, 1)

                over_groups(pe, (sums, 0), (spreads, 2), (transposes, 3))

            @block.scalar
            def _(act):
                act.sem_inc(lifted, 2)

                def lift(i, g):
                    act.wait_ge(turned, i * RING + (g + 1))
                    act.wait_ge(spread_done, i * RING + (g + 1))
                    act.activation(onehotT[:, ring(g), :].rearrange("p c e -> p (c e)"), pt[g % 2][:B, :],
                                   ACT.Copy).then_inc(lifted, 1)

                def exps(i, g):
                    act.wait_ge(shifted, i * RING + (g + 3))
                    w = wt[:, ring(g), :]
                    act.activation(w, w, ACT.Exp).then_inc(exped, 1)

                over_groups(act, (exps, 0), (lift, 1))


def spread_cols(v, fc):
    v = np.asarray(v).reshape(-1, fc, P)
    return np.ascontiguousarray(v.transpose(2, 0, 1).reshape(P, -1))


def consts():
    c = np.zeros((P, C_END), np.float32)
    c[:, C_ID:C_ID + P] = np.eye(P)
    c[:, C_IOTA:C_IOTA + P] = np.arange(P)
    r = np.arange(B)
    c[:B, C_STRICT:C_STRICT + B] = r[:, None] < r[None]
    c[:B, C_UPTO:C_UPTO + B] = r[:, None] <= r[None]
    c[:, C_ONE:C_ONE + P] = 1
    c[:, C_TILE:C_TILE + NT] = np.arange(NT)
    c[:B, C_SPARE:C_SPARE + NBLK] = SPARE + np.arange(NBLK)[None] * B + r[:, None]
    c[:, C_STEP:C_STEP + 7] = UR * np.arange(7)
    c[:, C_EPS] = LN_EPS
    c[:, C_EPS + 1] = FBN_EPS
    return c


def kernel(**inp):
    import concourse.bacc as bacc
    from concourse.bass_utils import run_bass_kernel_spmd

    v = {k: np.asarray(x) for k, x in inp.items()}
    arr = {"consts": consts(), "x": v["x"]}
    arr["src"] = v["src"].reshape(B, EC)
    arr["dst"] = v["dst"].reshape(B, EC)
    arr["attr"] = v["edge_attr_3"].reshape(B, EC * 3)
    flat = np.concatenate([v[n].reshape(-1) for n in ROWS + GATEB])
    arr["rows"] = np.broadcast_to(flat, (P, ROWN))
    fc = {64: 8, 32: 4, 16: 2, 4: 4}
    arr["cols"] = np.concatenate([spread_cols(v[n], fc[w]) for n, w in COLS], axis=1)

    def kmajor(w):
        w = w.reshape(w.shape[:-2] + (w.shape[-2] // P, P, w.shape[-1]))
        return np.swapaxes(w, -3, -2)

    for l in range(2):
        arr[f"L0_gnn_W{l}"] = kmajor(v[f"L0_gnn_W{l}"].T)
    for n in ("L1_gnn_W1", "L1_gnn_W2", "L1_gnn_W3"):
        arr[n] = kmajor(v[n])
    arr["L2_gnn_W"] = kmajor(v["L2_gnn_W"].T)
    arr["L3_gnn_W"] = kmajor(v["L3_gnn_W"])
    ew = np.zeros((PF, D), np.float32)
    ew[2:5] = v["L2_gnn_edge_W"].T
    ew[5] = v["L2_gnn_edge_b"]
    arr["edge_w"] = ew
    for n in GATES:
        arr[n] = kmajor(v[n])
    for n in B2S:
        arr[n] = v[n]
    arr["L0_ffn_W1"], arr["L0_ffn_W2"] = kmajor(v["L0_ffn_w1"]), kmajor(v["L0_ffn_w2"])
    for l in (1, 3):
        arr[f"L{l}_ffn_W1"], arr[f"L{l}_ffn_W2"] = kmajor(v[f"L{l}_ffn_W1"]), kmajor(v[f"L{l}_ffn_W2"])
    arr["L2_ffn_W1"], arr["L2_ffn_Wm"], arr["L2_ffn_W2"] = (kmajor(v[f"L2_ffn_{n}"]) for n in ("W1", "W2", "Wo"))

    nc = bacc.Bacc("TRN2", target_bir_lowering=False, num_devices=1)
    arr = {k: np.ascontiguousarray(x) for k, x in arr.items()}
    a = {k: nc.dram_tensor(f"in_{k}", x.shape, mybir.dt.from_np(x.dtype), kind="ExternalInput").ap()
         for k, x in arr.items()}
    out = nc.dram_tensor("out", (NODES, D), F32, kind="ExternalOutput").ap()
    build(nc, a, out, UPTO)
    r = run_bass_kernel_spmd(nc, [{f"in_{k}": x for k, x in arr.items()}], core_ids=[0])
    return r.results[0]["out"]


UPTO = 7
```

```python
import numpy as np
import concourse.bass as bass
from concourse import mybir

F32, I32, BF16 = mybir.dt.float32, mybir.dt.int32, mybir.dt.bfloat16
ALU, ACT, AX = mybir.AluOpType, mybir.ActivationFunctionType, mybir.AxisListType
ds = bass.ds

P = 128
NODES, D = 3125, 256
B = 125
NBLK = NODES // B
EDGES = 50000
EC = EDGES // B
EXP = 8
UR = 4 * B
UNITS = {0: EXP, 1: (2 * NODES + EXP * (UR - 1)) // UR, 3: (2 * NODES + EXP * (UR - 1)) // UR}
SPARE = UNITS[1] * UR
CAP = 489
TU = 5
NTMIN = EDGES // P + NBLK
NT = 416
EU = 8
EG = EU // 2
assert NTMIN <= NT and NT % EU == 0 and EC % EU == 0
PF = 8
BIG = float(2.0 ** 100)
XW = NBLK * D
HID = 512
BUFW = NBLK * 514
LN_EPS, GBN_EPS, FBN_EPS = 1e-5, 1e-5, 1e-3

C_ID, C_IOTA, C_STRICT, C_UPTO, C_ONE, C_TILE, C_EPS = 0, 128, 256, 381, 506, 634, 1050
C_SPARE, C_STEP = 1054, 1079
C_END = C_STEP + 7
ROWS = ["L0_gnn_b0", "L0_gnn_g0", "L0_gnn_beta0", "L0_gnn_b1", "L0_gnn_g1", "L0_gnn_beta1", "L1_gnn_b3",
        "L2_gnn_bias", "L2_gnn_a_src", "L2_gnn_a_dst", "L3_gnn_bias", "L3_gnn_att_src", "L3_gnn_att_dst"]
GATEB = ["L0_ffn_gate_b", "L1_ffn_bg", "L1_ffn_bias", "L2_ffn_br", "L3_ffn_bg"]
ROWN = 256 * len(ROWS) + EXP * len(GATEB)
COLS = [("L0_ffn_b1", 64), ("L1_gnn_b1", 4), ("L1_gnn_g1", 4), ("L1_gnn_be1", 4), ("L1_gnn_b2", 4),
        ("L1_gnn_g2", 4), ("L1_gnn_be2", 4), ("L1_ffn_b1", 32), ("L2_ffn_b1", 16), ("L2_ffn_g1", 16),
        ("L2_ffn_be1", 16), ("L2_ffn_m1", 16), ("L2_ffn_v1", 16), ("L2_ffn_b2", 16), ("L2_ffn_g2", 16),
        ("L2_ffn_be2", 16), ("L2_ffn_m2", 16), ("L2_ffn_v2", 16), ("L3_ffn_b1", 32)]
COLN = sum(n for _, n in COLS)
GATES = ["L0_ffn_gate_w", "L1_ffn_Wg", "L2_ffn_Wr", "L3_ffn_Wg"]
B2S = ["L0_ffn_b2", "L1_ffn_b2", "L2_ffn_bo", "L3_ffn_b2"]


def row_at(name):
    if name in ROWS:
        return 256 * ROWS.index(name)
    return 256 * len(ROWS) + EXP * GATEB.index(name)


def col_at(name):
    at = 0
    for n, w in COLS:
        if n == name:
            return at
        at += w
    raise KeyError(name)


class Chain:

    def __init__(self, eng, sem):
        self.eng, self.sem, self.n, self.i, self.per, self.k = eng, sem, 0, None, 0, 0

    def enter(self, i, per):
        self.i, self.per, self.k = i, per, 0

    def leave(self, rounds):
        assert self.k == self.per, (self.k, self.per)
        self.n += rounds * self.per
        self.i, self.k = None, 0

    def value(self):
        return self.n + self.k if self.i is None else self.i * self.per + (self.n + self.k)

    def link(self, ins):
        if self.i is None:
            self.n += 1
        else:
            self.k += 1
        ins.then_inc(self.sem, 1)
        self.eng.wait_ge(self.sem, self.value())


def hold(eng, sem, value):
    eng.wait_ge(sem, value)
    eng.nop(nofuse=True)


class Mem:

    def __init__(self, nc):
        self.nc, self.made = nc, 0

    def name(self, name):
        self.made += 1
        return f"{name}_{self.made}"

    def sb(self, name, shape, dtype):
        return self.nc.alloc_sbuf_tensor(self.name(name), shape, dtype)

    def psum(self, name):
        return self.nc.alloc_psum_tensor(self.name(name), [P, 512], F32)

    def sem(self, name):
        return self.nc.alloc_semaphore(self.name(name))


def build(nc, a, out):
    m = Mem(nc)
    sb = m.sb
    m.X = sb("x_res", [B, XW], F32)
    m.bufa = sb("bufa", [P, BUFW], F32)
    m.bufb = sb("bufb", [P, BUFW], F32)
    m.cst = sb("cst", [P, C_END], F32)
    m.rows = sb("rows", [P, ROWN], F32)
    m.cols = sb("cols", [P, COLN], F32)
    m.lists = {k: sb(f"list_{k}", [P, NT * PF], F32) for k in ("src", "dst")}
    m.blk = {k: sb(f"blk_{k}", [1, NT], I32) for k in ("src", "dst")}
    m.slots = sb("slots", [B, EC], I32)
    m.small = sb("small", [P, 1400], F32)
    m.weight = [m.small[:B, 200 + 32 * k:200 + 32 * k + NBLK] for k in range(2)]
    m.answer_row, m.token_row = ([m.small[:B, at + 32 * k:at + 32 * k + NBLK].bitcast(I32) for k in range(2)]
                                 for at in (264, 328))
    m.deg = m.small[:B, 1300:1325]
    m.table = nc.dram_tensor("table", (NODES, D), F32, kind="Internal").ap()
    m.table2 = nc.dram_tensor("table2", (NODES, HID), F32, kind="Internal").ap()
    m.tablea = {h: nc.dram_tensor(f"tablea{h}", (NODES, h), F32, kind="Internal").ap() for h in (4, 8)}
    m.tokens = nc.dram_tensor("tokens", (SPARE + NODES, D), F32, kind="Internal").ap()
    m.answers = nc.dram_tensor("answers", (SPARE, D), F32, kind="Internal").ap()
    m.units = sb("units", [1, UNITS[1]], I32)
    m.ldram = {k: nc.dram_tensor(f"edges_{k}", (P * NT, PF), F32, kind="Internal").ap() for k in ("src", "dst")}
    m.a = a

    load(nc, m)
    bin_slots(nc, m, "src", None)
    bin_slots(nc, m, "dst", "src")
    m.placed = 0
    m.block_regs = {}
    X, XN = m.X, m.bufb[:B, 0:XW]
    layernorm(nc, m, X[:], XN, meanwhile(m, 2))
    for l in range(2):
        store_table(nc, m, XN, m.table, D)
        aggregate(nc, m, "src", m.table, D, True, True, Arena(m.bufb[:, XW:]))
        sage_layer(nc, m, l, XN)
    residual(nc, m, XN)
    layernorm(nc, m, X[:], XN, meanwhile(m, 2))
    ffn(nc, m, 0, XN)
    layernorm(nc, m, X[:], XN, fetch_list(m))
    gcn(nc, m, XN)
    layernorm(nc, m, X[:], XN)
    ffn(nc, m, 1, XN)
    for l in (2, 3):
        layernorm(nc, m, X[:], XN)
        gat(nc, m, l, XN)
        layernorm(nc, m, X[:], XN)
        ffn(nc, m, l, XN)
    with nc.cleanup_on_exit():
        stored = m.sem("stored")
        with nc.Block() as block:
            @block.sync
            def _(sp):
                sp.dma_start(out.rearrange("(t p) w -> p t w", p=B),
                             m.X[:, :].rearrange("p (t w) -> p t w", w=D)).then_inc(stored, 16)
                sp.wait_ge(stored, 16)


def load(nc, m):
    with nc.cleanup_on_exit():
        loaded = m.sem("loaded")
        with nc.Block() as block:
            @block.sync
            def _(sp):
                sp.dma_start(m.cst[:, :], m.a["consts"]).then_inc(loaded, 16)
                sp.dma_start(m.rows[:, :], m.a["rows"]).then_inc(loaded, 16)
                sp.dma_start(m.cols[:, :], m.a["cols"]).then_inc(loaded, 16)
                sp.dma_start(m.X[:, :].rearrange("p (t w) -> p t w", w=D),
                             m.a["x"].rearrange("(t p) w -> p t w", p=B)).then_inc(loaded, 16)
                sp.wait_ge(loaded, 64)


class Scatter:
    pass


def records(m, key):
    return m.bufb[:B, 0:EC * PF] if key == "src" else m.lists["dst"][:B, 0:EC * PF]


def scatter_records(m, key, r0=0, r1=EC // EU):
    stage = m.sb("recordstage", [B, EU, PF], F32)
    slot = m.sb("slotstage", [B, EU], I32)
    copied = m.sem("copied")
    sent = [m.sem(f"sent{k}") for k in range(EU)]
    listed = m.sem("listed")
    pay = records(m, key)
    run = Scatter()

    def group(pool, i, g, value):
        pool.tensor_copy(stage[:, g * EG:(g + 1) * EG, :].rearrange("p c f -> p (c f)"),
                         pay[:, ds(i * (EU * PF) + g * EG * PF, EG * PF)]).then_inc(copied, 1)
        pool.tensor_copy(slot[:, g * EG:(g + 1) * EG], m.slots[:, ds(i * EU + g * EG, EG)]).then_inc(copied, 1)
        hold(pool, copied, value)
        for k in range(g * EG, (g + 1) * EG):
            pool.indirect_dma_start(
                out=m.ldram[key], out_offset=bass.IndirectOffsetOnAxis(ap=slot[:, k:k + 1], axis=0),
                in_=stage[:, k, :], in_offset=None).then_inc(sent[k], 16)

    def pool_program(pool):
        for g in range(2):
            group(pool, r0, g, 2 * g + 2)
        if r1 > r0 + 1:
            with pool.Fori(r0 + 1, r1) as i:
                for g in range(2):
                    for k in range(g * EG, (g + 1) * EG):
                        hold(pool, sent[k], i * 16 - 16 * r0)
                    group(pool, i, g, i * 4 + (2 * g + 2) - 4 * r0)
        for k in range(EU):
            pool.wait_ge(sent[k], 16 * (r1 - r0))

    def sync_program(sp):
        for k in range(EU):
            sp.wait_ge(sent[k], 16 * (r1 - r0))
        sp.dma_start(m.lists[key][:, :], m.ldram[key].rearrange("(p c) f -> p (c f)", p=P)).then_inc(listed, 16)
        sp.wait_ge(listed, 16)

    run.pool, run.sync = pool_program, sync_program
    return run


def meanwhile(m, rounds):
    def also(block):
        r0 = m.placed
        m.placed = r0 + rounds
        block.gpsimd(scatter_records(m, "dst", r0, m.placed).pool)
    return also


def fetch_list(m):
    def also(block):
        assert m.placed == EC // EU
        listed = m.sem("listed")

        @block.sync
        def _(sp):
            sp.dma_start(m.lists["dst"][:, :], m.ldram["dst"].rearrange("(p c) f -> p (c f)", p=P)
                         ).then_inc(listed, 16)
            sp.wait_ge(listed, 16)
    return also


def bin_slots(nc, m, key, other_list):
    other = "dst" if key == "src" else "src"
    count_degree = key == "dst"
    with nc.cleanup_on_exit():
        sb, sem = m.sb, m.sem
        wa = m.bufa[:B, :]
        names = ["key", "hi", "lo", "onehot", "scan", "tmp", "rank", "zero", "slot"]
        W = {n: wa[:, i * EC:(i + 1) * EC] for i, n in enumerate(names)}
        keyi = wa[:, 9 * EC:10 * EC].bitcast(I32)
        othi = wa[:, 10 * EC:11 * EC].bitcast(I32)
        iq = wa[:, 11 * EC:12 * EC].bitcast(I32)
        iq2 = wa[:, 12 * EC:13 * EC].bitcast(I32)
        attr = wa[:, 13 * EC:16 * EC]
        slot_new = wa[:, 16 * EC:17 * EC].bitcast(I32)
        pay = records(m, key)
        payv = pay.rearrange("p (c f) -> p c f", f=PF)
        fill = m.bufb[:, 3400:3400 + NT * PF]
        small = m.small
        cnt, tot, tiles, tstart, base, ti = [small[:B, 32 * i:32 * i + NBLK] for i in range(6)]
        tii = small[:B, 192:192 + NBLK].bitcast(I32)
        ohl = sb("ohl", [B, 2, 5, B], BF16)
        ohh = sb("ohh", [B, 2, 5, NBLK], BF16)
        blkf = sb("blkf", [1, NT], F32)
        ps, pd = m.psum("ps"), m.psum("pd")
        iota = m.cst[:B, C_IOTA:C_IOTA + NBLK]
        edges_in, filled, steps, counted = sem("edges_in"), sem("filled"), sem("steps"), sem("counted")
        prefixed, prefilled = sem("prefixed"), sem("prefilled")
        hot, hot_used = sem("hot"), sem("hot_used")
        clear_tokens = key == "dst"
        blank, tokens_clear = sem("blank"), sem("tokens_clear")
        zeros = m.bufb[:B, 6750:6750 + UR // B * D]
        run = scatter_records(m, other_list) if other_list else None
        with nc.Block() as block:
            @block.sync
            def _(sp):
                sp.dma_start(keyi, m.a[key]).then_inc(edges_in, 16)
                sp.dma_start(othi, m.a[other]).then_inc(edges_in, 16)
                sp.dma_start(attr, m.a["attr"]).then_inc(edges_in, 16)
                if clear_tokens:
                    sp.wait_ge(blank, 1)
                    for u in range(UNITS[1]):
                        sp.dma_start(m.tokens[u * UR:(u + 1) * UR, :].rearrange("(t p) w -> p t w", p=B),
                                     zeros.rearrange("p (t w) -> p t w", w=D)).then_inc(tokens_clear, 16)
                sp.wait_ge(filled, 1)
                sp.dma_start(m.ldram[key].rearrange("(p c) f -> p (c f)", p=P), fill).then_inc(prefilled, 16)
                sp.wait_ge(prefilled, 16)
                if clear_tokens:
                    sp.wait_ge(tokens_clear, 16 * UNITS[1])
                if run:
                    run.sync(sp)

            @block.gpsimd
            def _(pool):
                if run:
                    run.pool(pool)

            @block.tensor
            def _(pe):
                pe.wait_ge(counted, 1)
                pe.matmul(ps[:B, 0:NBLK], m.cst[:B, C_STRICT:C_STRICT + B], cnt, start=True, stop=True)
                pe.matmul(ps[:B, 32:32 + NBLK], m.cst[:B, C_ONE:C_ONE + B], cnt, start=True,
                          stop=True).then_inc(prefixed, 1)
                if count_degree:
                    pe.matmul(pd[:B, 0:NBLK], m.cst[:B, C_ONE:C_ONE + B], W["zero"][:, 0:NBLK], start=True,
                              stop=True, skip_group_check=True)
                    with pe.Fori(0, EC // 10) as i:
                        for g in range(2):
                            pe.wait_ge(hot, i * 2 + (g + 1))
                            for c in range(5):
                                mm = pe.matmul(pd[:B, 0:NBLK], ohl[:, g, c, :], ohh[:, g, c, :], start=False,
                                               stop=False, skip_group_check=True)
                            mm.then_inc(hot_used, 1)

            @block.vector
            def _(v):
                c = Chain(v, steps)
                link = c.link
                fv = fill.rearrange("p (c f) -> p c f", f=PF)
                if clear_tokens:
                    v.memset(zeros, 0.0).then_inc(blank, 1)
                link(v.memset(fill, 0.0))
                link(v.memset(fv[:, :, 6:7], -BIG))
                v.memset(fv[:, :, 1:2], -1.0).then_inc(filled, 1)
                v.memset(W["rank"], 0.0)
                v.memset(W["zero"], 0.0)
                v.memset(W["slot"], 0.0)
                link(v.memset(pay, 0.0))
                v.wait_ge(edges_in, 48)
                link(v.tensor_copy(W["key"], keyi))
                link(v.tensor_scalar(W["hi"], W["key"], float(B), None, ALU.is_ge))
                for b in range(2, NBLK):
                    link(v.scalar_tensor_tensor(W["hi"], W["key"], float(B * b), W["hi"], ALU.is_ge, ALU.add))
                link(v.scalar_tensor_tensor(W["lo"], W["hi"], -float(B), W["key"], ALU.mult, ALU.add))
                with v.Fori(0, NBLK) as b:
                    c.enter(b, 4)
                    link(v.tensor_scalar(W["onehot"], W["hi"], iota[:, ds(b, 1)], None, ALU.is_equal))
                    link(v.tensor_tensor_scan(W["scan"], W["onehot"], W["zero"], 0.0, ALU.add, ALU.add))
                    v.tensor_scalar(cnt[:, ds(b, 1)], W["scan"][:, EC - 1:EC], 1.0, None, ALU.mult)
                    link(v.tensor_tensor(W["tmp"], W["onehot"], W["scan"], ALU.mult))
                    link(v.tensor_tensor(W["rank"], W["rank"], W["tmp"], ALU.add))
                c.leave(NBLK)
                v.tensor_scalar(tiles, cnt, 1.0, None, ALU.mult).then_inc(counted, 1)
                v.wait_ge(prefixed, 1)
                link(v.tensor_scalar(tot, ps[:B, 32:32 + NBLK], float(P - 1), None, ALU.add))
                link(v.tensor_copy(tii, tot))
                link(v.tensor_scalar(tii, tii, 7, None, ALU.arith_shift_right))
                link(v.tensor_copy(tiles, tii))
                link(v.tensor_tensor_scan(tstart, tiles, W["zero"][:, 0:NBLK], 0.0, ALU.add, ALU.add))
                link(v.tensor_tensor(tstart, tstart, tiles, ALU.subtract))
                link(v.tensor_scalar(ti, tstart, float(P), -1.0, ALU.mult, ALU.add))
                link(v.tensor_tensor(base, ti, ps[:B, 0:NBLK], ALU.add))
                with v.Fori(0, NBLK) as b:
                    c.enter(b, 2)
                    link(v.tensor_scalar(W["tmp"], W["hi"], iota[:, ds(b, 1)], base[:, ds(b, 1)], ALU.is_equal,
                                         ALU.mult))
                    link(v.tensor_tensor(W["slot"], W["slot"], W["tmp"], ALU.add))
                c.leave(NBLK)
                link(v.tensor_tensor(W["slot"], W["slot"], W["rank"], ALU.add))
                link(v.tensor_copy(iq, W["slot"]))
                v.tensor_scalar(iq2, iq, 7, None, ALU.arith_shift_right)
                link(v.tensor_scalar(iq, iq, P - 1, None, ALU.bitwise_and))
                link(v.tensor_copy(W["tmp"], iq))
                link(v.tensor_copy(W["scan"], iq2))
                link(v.scalar_tensor_tensor(W["slot"], W["tmp"], float(NT), W["scan"], ALU.mult, ALU.add))
                v.tensor_copy(slot_new, W["slot"])
                link(v.tensor_scalar(blkf[:, :], m.cst[0:1, C_TILE:C_TILE + NT], tstart[0:1, 1:2], None, ALU.is_ge))
                with v.Fori(2, NBLK) as b:
                    c.enter(b - 2, 1)
                    link(v.scalar_tensor_tensor(blkf[:, :], m.cst[0:1, C_TILE:C_TILE + NT], tstart[0:1, ds(b, 1)],
                                                blkf[:, :], ALU.is_ge, ALU.add))
                c.leave(NBLK - 2)
                v.tensor_copy(m.blk[key][:, :], blkf[:, :])
                v.tensor_copy(payv[:, :, 0].bitcast(I32), othi)
                v.tensor_copy(payv[:, :, 1], W["lo"])
                v.tensor_copy(payv[:, :, 2:5], attr.rearrange("p (c f) -> p c f", f=3))
                link(v.memset(payv[:, :, 5:6], 1.0))
                if count_degree:
                    v.sem_inc(hot_used, 2)
                    with v.Fori(0, EC // 10) as i:
                        for g in range(2):
                            v.wait_ge(hot_used, i * 2 + (g + 1))
                            for q in range(5):
                                col = i * 10 + (g * 5 + q)
                                v.tensor_scalar(ohl[:, g, q, :], m.cst[:B, C_IOTA:C_IOTA + B],
                                                W["lo"][:, ds(col, 1)], None, ALU.is_equal)
                                last = v.tensor_scalar(ohh[:, g, q, :], iota, W["hi"][:, ds(col, 1)], None,
                                                       ALU.is_equal)
                            last.then_inc(hot, 1)
                    v.wait_ge(hot_used, 2 + EC // 5)
                    v.tensor_copy(m.deg, pd[:B, 0:NBLK])
    with nc.cleanup_on_exit():
        with nc.Block() as block:
            @block.vector
            def _(v):
                v.tensor_copy(m.slots[:, :], slot_new)


def layernorm(nc, m, src, dst, also=None):
    with nc.cleanup_on_exit():
        sem = m.sem
        st = m.small[:B, 0:6 * NBLK]
        f = st.rearrange("p (t s) -> p s t", s=6)
        mean, var, dif, std, inv, nb = [m.small[:B, 200 + 32 * i:200 + 32 * i + NBLK] for i in range(6)]
        steps, var_ready, std_ready = sem("steps"), sem("var_ready"), sem("std_ready")
        with nc.Block() as block:
            if also:
                also(block)

            @block.vector
            def _(v):
                c = Chain(v, steps)
                link = c.link
                with v.Fori(0, NBLK // TU) as i:
                    c.enter(i, 1)
                    for k in range(TU):
                        ins = v.bn_stats(st[:, ds((i * TU + k) * 6, 6)], src[:, ds((i * TU + k) * D, D)])
                    link(ins)
                c.leave(NBLK // TU)
                link(v.tensor_tensor(mean, f[:, 1], f[:, 4], ALU.add))
                link(v.tensor_scalar(mean, mean, 0.5, None, ALU.mult))
                link(v.tensor_tensor(dif, f[:, 1], f[:, 4], ALU.subtract))
                link(v.tensor_tensor(dif, dif, dif, ALU.mult))
                link(v.tensor_scalar(dif, dif, 0.25, None, ALU.mult))
                link(v.tensor_tensor(var, f[:, 2], f[:, 5], ALU.add))
                v.scalar_tensor_tensor(var, var, 1.0 / D, dif, ALU.mult, ALU.add).then_inc(var_ready, 1)
                v.wait_ge(std_ready, 1)
                link(v.reciprocal(inv, std))
                link(v.scalar_tensor_tensor(nb, mean, -1.0, inv, ALU.mult, ALU.mult))
                with v.Fori(0, NBLK // TU) as i:
                    for k in range(TU):
                        t = i * TU + k
                        v.tensor_scalar(dst[:, ds(t * D, D)], src[:, ds(t * D, D)], inv[:, ds(t, 1)],
                                        nb[:, ds(t, 1)], ALU.mult, ALU.add)

            @block.scalar
            def _(act):
                act.wait_ge(var_ready, 1)
                act.activation(std, var, ACT.Sqrt, bias=m.cst[:B, C_EPS:C_EPS + 1]).then_inc(std_ready, 1)


def store_table(nc, m, src, table, width):
    with nc.cleanup_on_exit():
        stored = m.sem("stored")
        with nc.Block() as block:
            @block.sync
            def _(sp):
                sp.dma_start(table.rearrange("(t p) w -> p t w", p=B),
                             src.rearrange("p (t w) -> p t w", w=width)).then_inc(stored, 16)
                sp.wait_ge(stored, 16)


GROUPS = NT // EG
RING = 4
RT = RING * EG
assert NT % RT == 0


def over(eng, total, ring, *stages):
    ahead = max(lead for _, lead in stages)
    rounds = total // ring
    assert total == rounds * ring and ahead <= ring

    def step(i, g):
        for program, lead in stages:
            s = g + lead
            if not isinstance(i, int):
                program(i if s < ring else i + 1, s % ring)
            elif 0 <= i * ring + s < total:
                program((i * ring + s) // ring, s % ring)

    for g in range(-ahead, 0):
        step(0, g)
    with eng.Fori(0, rounds - 1) as i:
        for g in range(ring):
            step(i, g)
    for g in range(ring):
        step(rounds - 1, g)


def over_groups(eng, *stages):
    over(eng, GROUPS, RING, *stages)


def ring(g):
    return slice(g * EG, (g + 1) * EG)


class Arena:

    def __init__(self, view):
        self.view, self.at = view, 0

    def take(self, parts, shape, dtype=F32):
        n = int(np.prod(shape))
        cols = (n + 1) // 2 if dtype == BF16 else n
        v = self.view[:parts, self.at:self.at + cols]
        self.at += cols
        assert self.at <= self.view.shape[1]
        if dtype == BF16:
            v = v.bitcast(BF16)[:, 0:n]
        if len(shape) == 2:
            v = v.rearrange("p (a b) -> p a b", b=shape[1])
        return v


def fields(m, key):
    return m.lists[key][:, :].rearrange("p (c f) -> p c f", f=PF)


def pool_gathers(pool, m, key, idx, picked, free, unit, table, rows, gathered):
    lst = fields(m, key)

    def gather(i, g):
        hold(pool, free, i * (RING * unit) + (g * unit + unit))
        pool.tensor_copy(idx[:, ring(g)], lst[:, ds(i * RT + g * EG, EG), 0].bitcast(I32)).then_inc(picked, 1)
        hold(pool, picked, i * RING + (g + 1))
        for k in range(g * EG, (g + 1) * EG):
            pool.indirect_dma_start(
                out=rows(k), out_offset=None, in_=table,
                in_offset=bass.IndirectOffsetOnAxis(ap=idx[:, k:k + 1], axis=0)).then_inc(gathered[g], 16)

    over_groups(pool, (gather, 0))


def act_onehots(act, m, lst, i, g, dist, onehot, measured, hot_ready):
    d0 = (g % 2) * EG
    act.wait_ge(hot_ready, i * RING + (g + 1))
    for q in range(EG):
        d = act.activation(dist[:, d0 + q, :], m.cst[:, C_IOTA:C_IOTA + B], ACT.Abs, scale=-1.0,
                           bias=lst[:, ds(i * RT + (g * EG + q), 1), 1])
    d.then_inc(measured, 1)
    act.wait_ge(measured, i * RING + (g + 1))
    act.activation(onehot[:, ring(g), :], dist[:, d0:d0 + EG, :], ACT.Relu, scale=-1.0,
                   bias=m.cst[:, C_ONE:C_ONE + 1]).then_inc(hot_ready, 1)


def vector_onehots(v, m, lst, i, g, onehot, hot_ready):
    for q in range(EG):
        o = v.tensor_scalar(onehot[:, g * EG + q, :], m.cst[:, C_IOTA:C_IOTA + B],
                            lst[:, ds(i * RT + (g * EG + q), 1), 1], None, ALU.is_equal)
    o.then_inc(hot_ready, 1)


def blocks_of(eng, m, key, i, g):
    regs = m.block_regs.get(type(eng).__name__)
    if regs is None:
        regs = m.block_regs[type(eng).__name__] = [eng.alloc_register(f"block{q}") for q in range(EG)]
    eng.load(regs, m.blk[key][0:1, ds(i * RT + g * EG, EG)])
    return [eng.snap(r, min_val=0, max_val=NBLK - 1) for r in regs]


def aggregate(nc, m, key, table, width, count, clear, space):
    W = width + (1 if count else 0)
    NPS = 2 * EG
    acc = m.bufa[:B, 0:NBLK * W]
    lst = fields(m, key)
    with nc.cleanup_on_exit():
        sem = m.sem
        idx = m.sb("idx", [P, RT], I32)
        rows, onehot = space.take(P, [RT, W]), space.take(P, [RT, B])
        dist = m.sb("dist", [P, 2 * EG, B], BF16)
        ps = [m.psum(f"ps{i}") for i in range(NPS)]
        cleared, picked, measured, hot_ready = sem("cleared"), sem("picked"), sem("measured"), sem("hot_ready")
        summed, added = sem("summed"), sem("added")
        gathered = [sem(f"gathered{g}") for g in range(RING)]
        with nc.Block() as block:
            @block.vector
            def _(v):
                if count:
                    v.memset(rows[:, :, width:W], 1.0).then_inc(cleared, 1)
                    v.wait_ge(cleared, 1)
                if clear:
                    v.memset(acc, 0.0).then_inc(cleared, 1)
                    v.wait_ge(cleared, 1 + count)
                v.sem_inc(added, NPS)

                def add(i, g):
                    blocks = blocks_of(v, m, key, i, g)
                    for j in range(g * EG, (g + 1) * EG):
                        part = acc[:, ds(blocks[j % EG] * W, W)]
                        v.wait_ge(summed, i * RT + (j + 1 + RT))
                        v.wait_ge(added, i * RT + (j + NPS))
                        v.tensor_tensor(part, part, ps[j % NPS][:B, 0:W], ALU.add).then_inc(added, 1)

                over_groups(v, (add, 0))

            @block.gpsimd
            def _(pool):
                pool_gathers(pool, m, key, idx, picked, summed, EG, table, lambda k: rows[:, k, 0:width], gathered)

            @block.scalar
            def _(act):
                act.sem_inc(hot_ready, 2)

                def one_hots(i, g):
                    hold(act, summed, i * RT + (g * EG + EG))
                    act_onehots(act, m, lst, i, g, dist, onehot, measured, hot_ready)

                over_groups(act, (one_hots, 0))

            @block.tensor
            def _(pe):
                if count:
                    pe.wait_ge(cleared, 1)
                pe.sem_inc(summed, RT)

                def products(i, g):
                    pe.wait_ge(gathered[g], i * (16 * EG) + 16 * EG)
                    pe.wait_ge(hot_ready, i * RING + (g + 3))
                    for j in range(g * EG, (g + 1) * EG):
                        pe.wait_ge(added, i * RT + (j + 1))
                        pe.matmul(ps[j % NPS][:B, 0:W], onehot[:, j, :], rows[:, j, :], start=True,
                                  stop=True).then_inc(summed, 1)

                over_groups(pe, (products, 0))


def token_linear(nc, m, src, wdram, wide, evac, stage_add=None, keep=None, also=None):
    with nc.cleanup_on_exit():
        sb, sem = m.sb, m.sem
        w = sb("w", [P, 2, wide], F32)
        st = sb("st", [B, TU, D], F32)
        stT = sb("stT", [P, TU, 2 * B], F32)
        ps = [m.psum(f"ps{i}") for i in range(TU)]
        w_in, staged, turned, lifted = sem("w_in"), sem("staged"), sem("turned"), sem("lifted")
        product, out_done, kept = sem("product"), sem("out_done"), sem("kept")
        with nc.Block() as block:
            if also:
                also(block)

            @block.sync
            def _(sp):
                sp.dma_start(w[:, :, :], wdram).then_inc(w_in, 16)
                sp.wait_ge(w_in, 16)

            @block.vector
            def _(v):
                v.sem_inc(out_done, TU)
                v.sem_inc(kept, TU)

                def stage(i, k):
                    t = i * TU + k
                    v.wait_ge(turned, t + 1)
                    if stage_add:
                        scale, other, ow = stage_add
                        v.scalar_tensor_tensor(st[:, k, :], other[:, ds(t * ow, D)], scale[:, ds(t, 1)],
                                               src[:, ds(t * D, D)], ALU.mult, ALU.add).then_inc(staged, 1)
                    else:
                        v.tensor_scalar(st[:, k, :], src[:, ds(t * D, D)], 1.0, None, ALU.mult).then_inc(staged, 1)

                def evacuate(i, k):
                    t = i * TU + k
                    if keep is not None:
                        v.wait_ge(lifted, t + 1)
                        for h in range(2):
                            kp = v.tensor_scalar(keep[:, ds(t * B + h * NODES, B)], stT[:, k, h * B:(h + 1) * B],
                                                 1.0, None, ALU.mult)
                        kp.then_inc(kept, 1)
                    v.wait_ge(product, t + (1 + TU))
                    evac(v, t, ps[k][:B, 2 * B:2 * B + wide]).then_inc(out_done, 1)

                over(v, NBLK, TU, (stage, 3), (evacuate, 0))
                if keep is not None:
                    v.wait_ge(kept, NBLK + TU)

            @block.scalar
            def _(act):
                def lift(i, k):
                    t = i * TU + k
                    act.wait_ge(turned, t + (1 + TU))
                    act.wait_ge(product, t + 1)
                    if keep is not None:
                        act.wait_ge(kept, t + 1)
                    act.activation(stT[:, k, :], ps[k][:, 0:2 * B], ACT.Copy).then_inc(lifted, 1)

                over(act, NBLK, TU, (lift, 0))

            @block.tensor
            def _(pe):
                pe.sem_inc(turned, TU)
                pe.sem_inc(product, TU)
                pe.wait_ge(w_in, 16)

                def transposes(i, k):
                    t = i * TU + k
                    pe.wait_ge(staged, t + 1)
                    pe.wait_ge(out_done, t + 1)
                    for h in range(2):
                        tr = pe.transpose(ps[k][:, h * B:(h + 1) * B], st[:, k, h * P:(h + 1) * P],
                                          m.cst[:B, C_ID:C_ID + B])
                    tr.then_inc(turned, 1)

                def products(i, k):
                    pe.wait_ge(lifted, i * TU + (k + 1))
                    for h in range(2):
                        mm = pe.matmul(ps[k][:B, 2 * B:2 * B + wide], stT[:, k, h * B:(h + 1) * B], w[:, h, :],
                                       start=(h == 0), stop=(h == 1))
                    mm.then_inc(product, 1)

                over(pe, NBLK, TU, (transposes, 2), (products, 0))


def sage_layer(nc, m, l, XN):
    W = D + 1
    acc = m.bufa[:B, 0:NBLK * W]
    deg = acc.rearrange("p (t w) -> p t w", w=W)[:, :, D]
    rdeg = m.small[:B, 400:400 + NBLK]
    H = m.bufb[:B, XW:2 * XW]
    with nc.cleanup_on_exit():
        steps = m.sem("steps")
        with nc.Block() as block:
            @block.vector
            def _(v):
                c = Chain(v, steps)
                c.link(v.tensor_scalar(rdeg, deg, 1.0, None, ALU.max))
                c.link(v.reciprocal(rdeg, rdeg))
    at = row_at(f"L0_gnn_b{l}")
    bias = m.rows[:B, at:at + D]
    token_linear(nc, m, XN, m.a[f"L0_gnn_W{l}"], D,
                 lambda v, t, ps: v.tensor_tensor(H[:, ds(t * D, D)], ps, bias, ALU.add),
                 stage_add=(rdeg, acc, W), also=meanwhile(m, 4))
    layernorm(nc, m, H, H, meanwhile(m, 2))
    with nc.cleanup_on_exit():
        steps, affine, gate = (m.sem(n) for n in ("steps", "affine", "gate"))
        g = m.rows[:B, row_at(f"L0_gnn_g{l}"):][:, 0:D]
        be = m.rows[:B, row_at(f"L0_gnn_beta{l}"):][:, 0:D]
        with nc.Block() as block:
            meanwhile(m, 2)(block)

            @block.vector
            def _(v):
                c = Chain(v, steps)
                hv = H.rearrange("p (t w) -> p t w", w=D)
                c.link(v.tensor_tensor(hv, hv, g.unsqueeze(1).broadcast_to([B, NBLK, D]), ALU.mult))
                v.tensor_tensor(hv, hv, be.unsqueeze(1).broadcast_to([B, NBLK, D]), ALU.add).then_inc(affine, 1)
                v.wait_ge(gate, 1)
                v.tensor_tensor(XN, H, m.bufa[:B, 0:XW], ALU.mult)

            @block.scalar
            def _(act):
                act.wait_ge(affine, 1)
                act.activation(m.bufa[:B, 0:XW], H, ACT.Sigmoid).then_inc(gate, 1)


def residual(nc, m, src):
    with nc.cleanup_on_exit():
        with nc.Block() as block:
            @block.vector
            def _(v):
                v.tensor_tensor(m.X[:, :], m.X[:, :], src, ALU.add)


def spread(ap, n):
    return ap.unsqueeze(2).broadcast_to([ap.shape[0], ap.shape[1], n])


FFN = {0: dict(F=1024, act=ACT.Relu), 1: dict(F=512, act=ACT.Relu), 2: dict(F=256, act=ACT.Relu),
       3: dict(F=512, act=ACT.Gelu)}


def gates(nc, m, l, LG, coef):
    G = NBLK * EXP
    with nc.cleanup_on_exit():
        sem = m.sem
        mx, sm, ix, t1 = [m.small[:B, 600 + 32 * i:600 + 32 * i + NBLK] for i in range(4)]
        w1 = m.small[:B, 730:730 + NBLK]
        E = m.small[:B, 760:760 + G]
        OH = m.small[:B, 960:960 + G]
        v3 = lambda ap: ap.rearrange("p (t e) -> p t e", e=EXP)
        lg, ev, oh, cf = v3(LG), v3(E), v3(OH), v3(coef)
        io8 = m.cst[:B, C_IOTA:C_IOTA + EXP].unsqueeze(1).broadcast_to([B, NBLK, EXP])
        T = m.sb("gt", [B, 5, G], F32)
        a1, a2, a3, first, second = (v3(T[:, i, :]) for i in range(5))
        zero, ucount, ustart, hits = (m.sb(n, [B, w], F32) for n, w in (
            ("zero", NBLK), ("ucount", EXP), ("ustart", EXP), ("hits", UNITS[1] * EXP)))
        posn, kept, away = (m.sb(n, [B, NBLK], F32) for n in ("posn", "kept", "away"))
        uf = m.sb("uf", [1, UNITS[1]], F32)
        ps = m.psum("ps")
        steps, shifted, exped, picked, counted = (sem(n) for n in ("steps", "shifted", "exped", "picked", "counted"))
        with nc.Block() as block:
            @block.vector
            def _(v):
                c = Chain(v, steps)
                link = c.link

                def first_max(values, largest, onehot):
                    link(v.tensor_tensor(a1, values, spread(largest, EXP), ALU.is_equal))
                    link(v.tensor_scalar(a1, a1, -float(EXP), float(EXP), ALU.mult, ALU.add))
                    link(v.tensor_tensor(a1, a1, io8, ALU.add))
                    link(v.tensor_reduce(ix, a1, AX.X, ALU.min))
                    link(v.tensor_tensor(onehot, io8, spread(ix, EXP), ALU.is_equal))

                def places():
                    v.sem_inc(picked, 1)
                    v.wait_ge(counted, 1)
                    tot = v3(ps[:B, 256:256 + G])
                    link(v.memset(zero[:, :], 0.0))
                    for e in range(EXP):
                        link(v.tensor_tensor_scan(a2[:, :, e], tot[:, :, e], zero[:, :], 0.0, ALU.add, ALU.add))
                    link(v.tensor_tensor(hits[:, 0:7 * EXP].rearrange("p (e j) -> p e j", j=7),
                                         a2[:, NBLK - 1, :].unsqueeze(2).broadcast_to([B, EXP, 7]),
                                         m.cst[:B, C_STEP:C_STEP + 7].unsqueeze(1).broadcast_to([B, EXP, 7]),
                                         ALU.is_gt))
                    link(v.tensor_reduce(ucount[:, :], hits[:, 0:7 * EXP].rearrange("p (e j) -> p e j", j=7), AX.X,
                                         ALU.add))
                    link(v.tensor_tensor(a2, a2, tot, ALU.subtract))
                    link(v.tensor_tensor(a2, a2, v3(ps[:B, 0:G]), ALU.add))

                def row_of(onehot, k):
                    link(v.tensor_tensor(a1, a2, onehot, ALU.mult))
                    link(v.tensor_reduce(posn[:, :], a1, AX.X, ALU.add))
                    link(v.tensor_copy(m.answer_row[k], posn[:, :]))
                    link(v.tensor_copy(m.token_row[k], posn[:, :]))

                link(v.tensor_reduce(mx, lg, AX.X, ALU.max))
                if l in (0, 2):
                    v.tensor_tensor(ev, lg, spread(mx, EXP), ALU.subtract).then_inc(shifted, 1)
                    v.wait_ge(exped, 1)
                    link(v.tensor_reduce(sm, ev, AX.X, ALU.add))
                    link(v.reciprocal(sm, sm))
                    if l == 2:
                        v.tensor_tensor(cf, ev, spread(sm, EXP), ALU.mult)
                        return
                    link(v.tensor_reduce(mx, ev, AX.X, ALU.max))
                    first_max(ev, mx, oh)
                    places()
                    link(v.tensor_tensor(a1, a2, oh, ALU.mult))
                    link(v.tensor_reduce(posn[:, :], a1, AX.X, ALU.add))
                    link(v.tensor_scalar(kept[:, :], posn[:, :], float(CAP), None, ALU.is_le))
                    link(v.tensor_tensor(t1, mx, sm, ALU.mult))
                    v.tensor_tensor(m.weight[0], kept[:, :], t1, ALU.mult)
                    link(v.tensor_scalar(posn[:, :], posn[:, :], float(CAP), -1.0, ALU.min, ALU.add))
                    link(v.scalar_tensor_tensor(posn[:, :], ix, float(UR), posn[:, :], ALU.mult, ALU.add))
                    v.tensor_copy(m.answer_row[0], posn[:, :])
                    link(v.tensor_tensor(away[:, :], m.cst[:B, C_SPARE:C_SPARE + NBLK], posn[:, :], ALU.subtract))
                    link(v.tensor_scalar(kept[:, :], kept[:, :], -1.0, 1.0, ALU.mult, ALU.add))
                    link(v.tensor_tensor(away[:, :], away[:, :], kept[:, :], ALU.mult))
                    link(v.tensor_tensor(posn[:, :], posn[:, :], away[:, :], ALU.add))
                    v.tensor_copy(m.token_row[0], posn[:, :])
                    v.tensor_copy(m.units[0:1, 0:EXP], m.cst[0:1, C_IOTA:C_IOTA + EXP])
                    return
                first_max(lg, mx, first)
                link(v.scalar_tensor_tensor(a3, first, -BIG, lg, ALU.mult, ALU.add))
                link(v.tensor_reduce(sm, a3, AX.X, ALU.max))
                first_max(a3, sm, second)
                link(v.tensor_tensor(oh, first, second, ALU.add))
                places()
                link(v.tensor_tensor_scan(ustart[:, :], ucount[:, :], zero[:, 0:EXP], 0.0, ALU.add, ALU.add))
                link(v.tensor_tensor(ustart[:, :], ustart[:, :], ucount[:, :], ALU.subtract))
                link(v.tensor_scalar(ucount[:, :], ustart[:, :], float(UR), -1.0, ALU.mult, ALU.add))
                link(v.tensor_tensor(a2, a2, ucount[:, :].unsqueeze(1).broadcast_to([B, NBLK, EXP]), ALU.add))
                row_of(first, 0)
                row_of(second, 1)
                U = UNITS[l]
                hv = hits[0:1, 0:U * 7].rearrange("p (u e) -> p u e", e=7)
                link(v.tensor_tensor(hv, m.cst[0:1, C_IOTA:C_IOTA + U].unsqueeze(2).broadcast_to([1, U, 7]),
                                     ustart[0:1, 1:EXP].unsqueeze(1).broadcast_to([1, U, 7]), ALU.is_ge))
                link(v.tensor_reduce(uf[:, :], hv, AX.X, ALU.add))
                v.tensor_copy(m.units[:, :], uf[:, :])
                if l == 3:
                    v.memset(m.weight[0], 1.0)
                    v.memset(m.weight[1], 1.0)
                    return
                v.tensor_tensor(t1, sm, mx, ALU.subtract).then_inc(shifted, 1)
                v.wait_ge(exped, 1)
                link(v.tensor_scalar(sm, t1, 1.0, None, ALU.add))
                link(v.reciprocal(w1, sm))
                v.tensor_tensor(m.weight[1], t1, w1, ALU.mult)
                v.tensor_copy(m.weight[0], w1)

            @block.scalar
            def _(act):
                if l in (0, 2):
                    act.wait_ge(shifted, 1)
                    act.activation(E, E, ACT.Exp).then_inc(exped, 1)
                if l == 1:
                    act.wait_ge(shifted, 1)
                    act.activation(t1, t1, ACT.Exp).then_inc(exped, 1)

            @block.tensor
            def _(pe):
                if l != 2:
                    pe.wait_ge(picked, 1)
                    pe.matmul(ps[:B, 0:G], m.cst[:B, C_UPTO:C_UPTO + B], OH, start=True, stop=True)
                    pe.matmul(ps[:B, 256:256 + G], m.cst[:B, C_ONE:C_ONE + B], OH, start=True,
                              stop=True).then_inc(counted, 1)


def ffn(nc, m, l, XN):
    LG = m.small[:B, 0:NBLK * EXP]
    coef = m.small[:B, 200:200 + NBLK * EXP]
    XT = m.bufa[:, 0:2 * NODES]
    gb = m.rows[:B, row_at({0: "L0_ffn_gate_b", 1: "L1_ffn_bg", 2: "L2_ffn_br", 3: "L3_ffn_bg"}[l]):][:, 0:EXP]
    token_linear(nc, m, XN, m.a[GATES[l]], EXP,
                 lambda v, t, ps: v.tensor_tensor(LG[:, ds(t * EXP, EXP)], ps, gb, ALU.add),
                 keep=XT if l == 2 else None, also=meanwhile(m, 3) if l == 0 else None)
    if l == 1:
        with nc.cleanup_on_exit():
            with nc.Block() as block:
                @block.vector
                def _(v):
                    lg = LG.rearrange("p (t e) -> p t e", e=EXP)
                    b = m.rows[:B, row_at("L1_ffn_bias"):][:, 0:EXP].unsqueeze(1).broadcast_to([B, NBLK, EXP])
                    v.tensor_tensor(lg, lg, b, ALU.add)
    gates(nc, m, l, LG, coef)
    if l == 2:
        bias_out(nc, m, l, coef, m.X[:, :], False)
        dense_experts(nc, m, XT, coef, m.X[:, :])
        return
    K = 1 if l == 0 else 2
    send_tokens(nc, m, K, XN)
    unit_experts(nc, m, l, meanwhile(m, 22) if l == 0 else None)
    take_answers(nc, m, l, K)
    if l == 0:
        finite_residual(nc, m, m.bufb[:B, 0:XW], meanwhile(m, 5))


def send_tokens(nc, m, K, XN):
    with nc.cleanup_on_exit():
        sent = m.sem("sent")
        with nc.Block() as block:
            @block.gpsimd
            def _(pool):
                for t in range(NBLK):
                    for k in range(K):
                        pool.indirect_dma_start(
                            out=m.tokens, out_offset=bass.IndirectOffsetOnAxis(ap=m.token_row[k][:, t:t + 1], axis=0),
                            in_=XN[:, t * D:(t + 1) * D], in_offset=None).then_inc(sent, 16)
                pool.wait_ge(sent, 16 * NBLK * K)


def take_answers(nc, m, l, K):
    got = lambda t, k: m.bufb[:B, (k * NBLK + t) * D:(k * NBLK + t + 1) * D]
    with nc.cleanup_on_exit():
        arrived = [m.sem(f"arrived{g}") for g in range(CH)]
        first_added = m.sem("first_added")
        with nc.Block() as block:
            @block.gpsimd
            def _(pool):
                for t in range(NBLK):
                    for k in range(K):
                        pool.indirect_dma_start(
                            out=got(t, k), out_offset=None, in_=m.answers[0:UNITS[l] * UR, :],
                            in_offset=bass.IndirectOffsetOnAxis(ap=m.answer_row[k][:, t:t + 1], axis=0)
                        ).then_inc(arrived[t // TU], 16)

            @block.vector
            def _(v):
                for g in range(CH):
                    v.wait_ge(arrived[g], 16 * TU * K)
                    for k in range(K):
                        for t in range(g * TU, (g + 1) * TU):
                            w = m.weight[k][:, t:t + 1]
                            x = m.X[:, t * D:(t + 1) * D]
                            if K == 1:
                                v.tensor_scalar(got(t, k), got(t, k), w, None, ALU.mult)
                            else:
                                add = v.scalar_tensor_tensor(x, got(t, k), w, x, ALU.mult, ALU.add)
                        if K == 2 and k == 0:
                            add.then_inc(first_added, 1)
                            v.wait_ge(first_added, g + 1)


def unit_experts(nc, m, l, also=None):
    F, func, U = FFN[l]["F"], FFN[l]["act"], UNITS[l]
    FC, TT = F // P, UR // B
    with nc.cleanup_on_exit():
        sem = m.sem
        wide, more = Arena(m.bufa), Arena(m.bufb)
        ht = [wide.take(P, [FC, UR]) for _ in range(2)]
        xT = [wide.take(P, [2, UR]) for _ in range(2)]
        xin = [wide.take(B, [TT, D]) for _ in range(2)]
        w1, w2 = [more.take(P, [2, F]) for _ in range(2)], [more.take(P, [FC, D]) for _ in range(2)]
        b2, y = [more.take(B, [D]) for _ in range(2)], [more.take(B, [TT, D]) for _ in range(2)]
        pt, psy = ([m.psum(f"{n}{i}") for i in range(2)] for n in ("pt", "psy"))
        psh = [m.psum(f"psh{i}") for i in range(4)]
        w_in, stored = ([sem(f"{n}{k}") for k in range(2)] for n in ("w_in", "stored"))
        turned, lifted = sem("turned"), sem("lifted")
        h_ready, h_done = sem("h_ready"), sem("h_done")
        y_ready, y_out = sem("y_ready"), sem("y_out")
        b1 = m.cols[:, col_at(f"L{l}_ffn_b1"):][:, 0:EXP * FC]
        rows_of = lambda table, u: table[ds(u * UR, UR), :].rearrange("(t p) w -> p t w", p=B)

        def expert_of(eng, u):
            return eng.value_load(m.units[0:1, ds(u, 1)], min_val=0, max_val=EXP - 1)

        with nc.Block() as block:
            if also:
                also(block)

            @block.sync
            def _(sp):
                def load_unit(u, k):
                    e = expert_of(sp, u)
                    sp.dma_start(xin[k], rows_of(m.tokens, u)).then_inc(w_in[k], 16)
                    sp.dma_start(w1[k], m.a[f"L{l}_ffn_W1"][ds(e, 1)].rearrange(
                        "a p c f -> (a p) c f")).then_inc(w_in[k], 16)
                    sp.dma_start(w2[k], m.a[f"L{l}_ffn_W2"][ds(e, 1)].rearrange(
                        "a p c f -> (a p) c f")).then_inc(w_in[k], 16)
                    sp.dma_start(b2[k], m.a[B2S[l]][ds(e, 1), :].broadcast_to([B, D])).then_inc(w_in[k], 16)

                def store(i, k):
                    sp.wait_ge(y_out, i * (2 * TT) + (k * TT + TT + 2))
                    sp.dma_start(rows_of(m.answers, i * 2 + k), y[k]).then_inc(stored[k], 16)

                for k in range(2):
                    load_unit(k, k)
                with sp.Fori(0, U // 2 - 1) as i:
                    for k in range(2):
                        store(i, k)
                        load_unit(i * 2 + (k + 2), k)
                for k in range(2):
                    store(U // 2 - 1, k)
                for k in range(2):
                    sp.wait_ge(stored[k], 16 * (U // 2) + 16)

            @block.tensor
            def _(pe):
                pe.sem_inc(h_ready, 2 * FC)
                pe.sem_inc(y_ready, 2 * TT)

                def transposes(i, k):
                    pe.wait_ge(w_in[k], i * 64 + 64)
                    pe.wait_ge(lifted, i * 2 + (k + 1))
                    for h in range(2):
                        for t in range(TT):
                            tr = pe.transpose(pt[h][:, t * B:(t + 1) * B], xin[k][:, t, h * P:(h + 1) * P],
                                              m.cst[:B, C_ID:C_ID + B])
                    tr.then_inc(turned, 1)

                def hidden(i, k):
                    pe.wait_ge(lifted, i * 2 + (k + 2))
                    for f in range(FC):
                        pe.wait_ge(h_done, i * (2 * FC) + (k * FC + f + 1))
                        for h in range(2):
                            mm = pe.matmul(psh[f % 4][:, 0:UR], w1[k][:, h, f * P:(f + 1) * P], xT[k][:, h, :],
                                           start=(h == 0), stop=(h == 1))
                        mm.then_inc(h_ready, 1)

                def outputs(i, k):
                    pe.wait_ge(h_done, i * (2 * FC) + (k * FC + FC + 4))
                    for t in range(TT):
                        pe.wait_ge(y_out, i * (2 * TT) + (k * TT + t + 1))
                        for f in range(FC):
                            mm = pe.matmul(psy[t % 2][:B, 0:D], ht[k][:, f, t * B:(t + 1) * B], w2[k][:, f, :],
                                           start=(f == 0), stop=(f == FC - 1))
                        mm.then_inc(y_ready, 1)

                over(pe, U, 2, (hidden, 0), (transposes, 1), (outputs, 0))

            @block.scalar
            def _(act):
                act.sem_inc(h_done, 4)
                act.sem_inc(lifted, 1)

                def activate(i, k):
                    e = expert_of(act, i * 2 + k)
                    hold(act, y_ready, i * (2 * TT) + (k * TT + TT))
                    for f in range(FC):
                        hold(act, h_ready, i * (2 * FC) + (k * FC + f + 1 + 2 * FC))
                        act.activation(ht[k][:, f, :], psh[f % 4][:, 0:UR], func,
                                       bias=b1[:, ds(e * FC + f, 1)]).then_inc(h_done, 1)

                def lift(i, k):
                    act.wait_ge(turned, i * 2 + (k + 1))
                    act.wait_ge(h_ready, i * (2 * FC) + (k * FC + FC))
                    for h in range(2):
                        up = act.activation(xT[k][:, h, :], pt[h][:, 0:UR], ACT.Copy)
                    up.then_inc(lifted, 1)

                over(act, U, 2, (activate, 0), (lift, 1))

            @block.vector
            def _(v):
                v.sem_inc(y_out, 2)
                for k in range(2):
                    v.sem_inc(stored[k], 16)

                def out(i, k):
                    v.wait_ge(stored[k], i * 16 + 16)
                    for t in range(TT):
                        v.wait_ge(y_ready, i * (2 * TT) + (k * TT + t + 1 + 2 * TT))
                        v.tensor_tensor(y[k][:, t, :], psy[t % 2][:B, 0:D], b2[k], ALU.add).then_inc(y_out, 1)

                over(v, U, 2, (out, 0))


def bias_out(nc, m, l, coef, Y, fresh):
    with nc.cleanup_on_exit():
        sb, sem = m.sb, m.sem
        b2 = sb("b2", [EXP, D], F32)
        st = sb("st", [B, TU, EXP], F32)
        cT = sb("cT", [EXP, TU, B], F32)
        ps = [m.psum(f"ps{i}") for i in range(TU)]
        w_in, staged, turned, lifted, product, added = (
            sem(n) for n in ("w_in", "staged", "turned", "lifted", "product", "added"))
        with nc.Block() as block:
            @block.sync
            def _(sp):
                sp.dma_start(b2[:, :], m.a[B2S[l]]).then_inc(w_in, 16)
                sp.wait_ge(w_in, 16)

            @block.vector
            def _(v):
                v.sem_inc(added, TU)
                with v.Fori(0, NBLK // TU) as i:
                    v.wait_ge(turned, i * TU + TU)
                    for k in range(TU):
                        v.tensor_scalar(st[:, k, :], coef[:, ds((i * TU + k) * EXP, EXP)], 1.0, None,
                                        ALU.mult).then_inc(staged, 1)
                    for k in range(TU):
                        v.wait_ge(product, i * TU + (k + 1 + TU))
                        y = Y[:, ds((i * TU + k) * D, D)]
                        if fresh:
                            v.tensor_scalar(y, ps[k][:B, P:P + D], 1.0, None, ALU.mult).then_inc(added, 1)
                        else:
                            v.tensor_tensor(y, y, ps[k][:B, P:P + D], ALU.add).then_inc(added, 1)

            @block.scalar
            def _(act):
                with act.Fori(0, NBLK // TU) as i:
                    for k in range(TU):
                        act.wait_ge(turned, i * TU + (k + 1 + TU))
                        act.wait_ge(product, i * TU + TU)
                        act.activation(cT[:, k, :], ps[k][:EXP, 0:B], ACT.Copy).then_inc(lifted, 1)

            @block.tensor
            def _(pe):
                pe.sem_inc(turned, TU)
                pe.sem_inc(product, TU)
                pe.wait_ge(w_in, 16)
                with pe.Fori(0, NBLK // TU) as i:
                    for k in range(TU):
                        pe.wait_ge(staged, i * TU + (k + 1))
                        pe.wait_ge(added, i * TU + (k + 1))
                        pe.transpose(ps[k][:EXP, 0:B], st[:, k, :], m.cst[:B, C_ID:C_ID + B]).then_inc(turned, 1)
                    for k in range(TU):
                        pe.wait_ge(lifted, i * TU + (k + 1))
                        pe.matmul(ps[k][:B, P:P + D], cT[:, k, :], b2[:, :], start=True,
                                  stop=True).then_inc(product, 1)


HALVES = [(0, 3), (3, 2)]
CH = NBLK // TU


def dense_experts(nc, m, XT, coef, Y):
    F, func = FFN[2]["F"], FFN[2]["act"]
    FC = F // P
    with nc.cleanup_on_exit():
        sb, sem = m.sb, m.sem
        w1 = [m.bufb[:, k * 2 * F:(k + 1) * 2 * F].rearrange("p (c f) -> p c f", c=2) for k in range(2)]
        wm, w2 = ([sb(f"{n}_{k}", [P, FC, w], F32) for k in range(2)] for n, w in (("wm", F), ("w2", D)))
        space = Arena(m.bufa[:, 2 * NODES:])
        ht, ht2 = ([space.take(P, [FC, 3 * B]) for _ in range(2)] for _ in range(2))
        sc = sb("sc", [P, 4, EXP * FC], F32)
        ps1, ps2 = ([m.psum(f"{n}{i}") for i in range(FC)] for n in ("ps1", "ps2"))
        psy = [m.psum(f"psy{i}") for i in range(4)]
        w_in = [sem(f"w_in{k}") for k in range(2)]
        ready1, done1, ready2, done2 = (sem(n) for n in ("ready1", "done1", "ready2", "done2"))
        y_ready, y_done = sem("y_ready"), sem("y_done")
        scaled, steps, variances, stds = sem("scaled"), sem("steps"), sem("variances"), sem("stds")
        with nc.Block() as block:
            @block.sync
            def _(sp):
                def load_expert(e, k):
                    for w, n in ((w1[k], "W1"), (wm[k][:, :, :], "Wm"), (w2[k][:, :, :], "W2")):
                        sp.dma_start(w, m.a[f"L2_ffn_{n}"][ds(e, 1)].rearrange(
                            "a p c f -> (a p) c f")).then_inc(w_in[k], 16)

                for k in range(2):
                    load_expert(k, k)
                with sp.Fori(1, EXP // 2) as e2:
                    for k in range(2):
                        sp.wait_ge(y_ready, (e2 * 2 + k) * NBLK - NBLK + YR)
                        load_expert(e2 * 2 + k, k)
                for k in range(2):
                    sp.wait_ge(w_in[k], 48 * (EXP // 2))

            @block.tensor
            def _(pe):
                pe.sem_inc(y_ready, YR)
                pe.sem_inc(ready2, 2 * FC)

                def expert(e, k):
                    def first(c, half):
                        u = (e * CH + c) * 2 + half
                        t0, tn = HALVES[half]
                        for f in range(FC):
                            pe.wait_ge(done1, u * FC + (f + 1))
                            for h in range(2):
                                mm = pe.matmul(ps1[f][:, 0:tn * B], w1[k][:, h, f * P:(f + 1) * P],
                                               XT[:, ds(c * (TU * B) + (h * NODES + t0 * B), tn * B)],
                                               start=(h == 0), stop=(h == 1))
                            mm.then_inc(ready1, 1)

                    def second(c, half):
                        u = (e * CH + c) * 2 + half
                        n = HALVES[half][1] * B
                        pe.wait_ge(done1, u * FC + 2 * FC)
                        for f in range(FC):
                            pe.wait_ge(done2, u * FC + (f + 1))
                            for h in range(FC):
                                mm = pe.matmul(ps2[f][:, 0:n], wm[k][:, h, f * P:(f + 1) * P], ht[half][:, h, 0:n],
                                               start=(h == 0), stop=(h == FC - 1))
                            mm.then_inc(ready2, 1)

                    def output(c, half):
                        t0, tn = HALVES[half]
                        pe.wait_ge(done2, ((e * CH + c) * 2 + half) * FC + 2 * FC)
                        for t in range(tn):
                            pe.wait_ge(y_done, (e * CH + c) * TU + (t0 + t + 1 if t0 + t else YB))
                            for f in range(FC):
                                mm = pe.matmul(psy[(t0 + t) % 4][:B, 0:D], ht2[half][:, f, t * B:(t + 1) * B],
                                               w2[k][:, f, :], start=(f == 0), stop=(f == FC - 1))
                            mm.then_inc(y_ready, 1)

                    over(pe, 2 * CH, 2, (output, 0), (second, 1), (first, 2))

                with pe.Fori(0, EXP // 2) as e2:
                    for k in range(2):
                        hold(pe, w_in[k], e2 * 48 + 48)
                        expert(e2 * 2 + k, k)

            @block.scalar
            def _(act):
                act.sem_inc(done1, FC)
                act.sem_inc(done2, FC)
                act.wait_ge(variances, 1)
                act.activation(sc[:, 0:1, :], sc[:, 0:1, :], ACT.Sqrt, bias=m.cst[:, C_EPS + 1:C_EPS + 2])
                act.activation(sc[:, 2:3, :], sc[:, 2:3, :], ACT.Sqrt,
                               bias=m.cst[:, C_EPS + 1:C_EPS + 2]).then_inc(stds, 1)
                act.wait_ge(scaled, 1)
                with act.Fori(0, EXP) as e:
                    def layer(n, src, ready, credit, dst, done, u, half):
                        w = HALVES[half][1] * B
                        for f in range(FC):
                            hold(act, ready, u * FC + (f + 1 + credit))
                            act.activation(dst[half][:, f, 0:w], src[f][:, 0:w], func,
                                           bias=sc[:, 2 * n + 1, ds(e * FC + f, 1)],
                                           scale=sc[:, 2 * n, ds(e * FC + f, 1)]).then_inc(done, 1)

                    def first(c, half):
                        u = (e * CH + c) * 2 + half
                        hold(act, ready2, u * FC + FC)
                        layer(0, ps1, ready1, 0, ht, done1, u, half)

                    def second(c, half):
                        t0, tn = HALVES[half]
                        hold(act, y_ready, (e * CH + c) * TU + (t0 + tn))
                        layer(1, ps2, ready2, 2 * FC, ht2, done2, (e * CH + c) * 2 + half, half)

                    over(act, 2 * CH, 2, (second, 1), (first, 2))

            @block.vector
            def _(v):
                ch = Chain(v, steps)
                link = ch.link
                col = lambda n: m.cols[:, col_at(f"L2_ffn_{n}"):][:, 0:EXP * FC]
                link(v.tensor_copy(sc[:, 0, :], col("v1")))
                link(v.tensor_copy(sc[:, 2, :], col("v2")))
                v.sem_inc(variances, 1)
                v.wait_ge(stds, 1)
                for i in range(2):
                    s, t = sc[:, 2 * i, :], sc[:, 2 * i + 1, :]
                    link(v.reciprocal(s, s))
                    link(v.tensor_tensor(s, s, col(f"g{i + 1}"), ALU.mult))
                    link(v.tensor_tensor(t, col(f"b{i + 1}"), col(f"m{i + 1}"), ALU.subtract))
                    link(v.tensor_tensor(t, t, s, ALU.mult))
                    link(v.tensor_tensor(t, t, col(f"be{i + 1}"), ALU.add))
                v.sem_inc(scaled, 1)
                v.sem_inc(y_done, YB)
                with v.Fori(0, EXP * CH) as ec:
                    for t in range(TU):
                        tile = (ec % CH) * TU + t
                        y = Y[:, ds(tile * D, D)]
                        v.wait_ge(y_ready, ec * TU + (t + 1 + YR))
                        v.scalar_tensor_tensor(y, psy[t % 4][:B, 0:D], coef[:, ds(tile * EXP + ec // CH, 1)], y,
                                               ALU.mult, ALU.add).then_inc(y_done, 1)


YB = 4
YR = TU


def finite_residual(nc, m, Y, also=None):
    T = m.bufa[:B, 0:XW]
    big = 3.4028234663852886e38
    with nc.cleanup_on_exit():
        steps = m.sem("steps")
        mask = m.bufa[:B, XW:2 * XW].bitcast(I32)
        with nc.Block() as block:
            if also:
                also(block)

            @block.vector
            def _(v):
                c = Chain(v, steps)
                c.link(v.memset(T, 0.0))
                c.link(v.tensor_tensor(mask, Y, Y, ALU.is_equal))
                c.link(v.copy_predicated(T, mask, Y))
                c.link(v.tensor_scalar(mask, T, big, None, ALU.is_gt))
                c.link(v.memset(Y, 1e4))
                c.link(v.copy_predicated(T, mask, Y))
                c.link(v.tensor_scalar(mask, T, -big, None, ALU.is_lt))
                c.link(v.memset(Y, -1e4))
                c.link(v.copy_predicated(T, mask, Y))
                v.tensor_tensor(m.X[:, :], m.X[:, :], T, ALU.add)


def gcn(nc, m, XN):
    dinv = m.small[:B, 1330:1355]
    HT = m.bufb[:, 0:4 * NODES]
    bns = m.small[:, 400:416]
    with nc.cleanup_on_exit():
        rooted = m.sem("rooted")
        with nc.Block() as block:
            @block.scalar
            def _(act):
                act.activation(dinv, m.deg, ACT.Sqrt, bias=m.cst[:B, C_ONE:C_ONE + 1]).then_inc(rooted, 1)

            @block.vector
            def _(v):
                v.wait_ge(rooted, 1)
                v.reciprocal(dinv, dinv).then_inc(rooted, 1)
                v.wait_ge(rooted, 2)
                with v.Fori(0, NBLK // TU) as i:
                    for k in range(TU):
                        t = i * TU + k
                        v.tensor_scalar(m.bufa[:B, ds(t * D, D)], XN[:, ds(t * D, D)], dinv[:, ds(t, 1)], None,
                                        ALU.mult)
    agg = m.bufa[:B, 0:XW]
    store_table(nc, m, agg, m.table, D)
    aggregate(nc, m, "dst", m.table, D, False, False, Arena(m.bufb))
    vT = m.bufa[:, XW:XW + 2 * NODES]
    to_features(nc, m, agg, D, dinv, vT, None)
    feature_linear(nc, m, vT, "L1_gnn_W1", m.cols[:, col_at("L1_gnn_b1"):][:, 0:4], HT)
    batch_stats(nc, m, HT, 1, bns)
    wide_agg = m.bufa[:B, 0:NBLK * HID]
    bn_linear(nc, m, HT, bns, "L1_gnn_W2", HID, dinv, wide_agg)
    store_table(nc, m, wide_agg, m.table2, HID)
    aggregate(nc, m, "dst", m.table2, HID, False, False, Arena(m.bufb))
    to_features(nc, m, wide_agg, HID, dinv, HT, m.cols[:, col_at("L1_gnn_b2"):][:, 0:4])
    batch_stats(nc, m, HT, 2, bns)
    bn_linear(nc, m, HT, bns, "L1_gnn_W3", D, dinv, agg)
    store_table(nc, m, agg, m.table, D)
    aggregate(nc, m, "dst", m.table, D, False, False, Arena(m.bufb))
    with nc.cleanup_on_exit():
        steps = m.sem("steps")
        with nc.Block() as block:
            @block.vector
            def _(v):
                c = Chain(v, steps)
                b3 = m.rows[:B, row_at("L1_gnn_b3"):][:, 0:D].unsqueeze(1).broadcast_to([B, NBLK, D])
                xv = m.X[:, :].rearrange("p (t w) -> p t w", w=D)
                with v.Fori(0, NBLK // TU) as i:
                    c.enter(i, 1)
                    for k in range(TU):
                        t = i * TU + k
                        x = m.X[:, ds(t * D, D)]
                        last = v.scalar_tensor_tensor(x, agg[:, ds(t * D, D)], dinv[:, ds(t, 1)], x, ALU.mult, ALU.add)
                    c.link(last)
                c.leave(NBLK // TU)
                v.tensor_tensor(xv, xv, b3, ALU.add)


def to_features(nc, m, src, width, scale, dst, bias):
    KC = width // P
    with nc.cleanup_on_exit():
        st = m.sb("st", [B, TU, width], F32)
        ps = [m.psum(f"ps{i}") for i in range(TU)]
        staged, turned, lifted = m.sem("staged"), m.sem("turned"), m.sem("lifted")
        with nc.Block() as block:
            @block.vector
            def _(v):
                with v.Fori(0, NBLK // TU) as i:
                    v.wait_ge(turned, i * TU + TU)
                    for k in range(TU):
                        t = i * TU + k
                        v.tensor_scalar(st[:, k, :], src[:, ds(t * width, width)], scale[:, ds(t, 1)], None,
                                        ALU.mult).then_inc(staged, 1)

            @block.tensor
            def _(pe):
                pe.sem_inc(turned, TU)
                with pe.Fori(0, NBLK // TU) as i:
                    for k in range(TU):
                        pe.wait_ge(staged, i * TU + (k + 1))
                        pe.wait_ge(lifted, i * TU + (k + 1))
                        for h in range(KC):
                            tr = pe.transpose(ps[k][:, h * B:(h + 1) * B], st[:, k, h * P:(h + 1) * P],
                                              m.cst[:B, C_ID:C_ID + B])
                        tr.then_inc(turned, 1)

            @block.scalar
            def _(act):
                act.sem_inc(lifted, TU)
                with act.Fori(0, NBLK // TU) as i:
                    for k in range(TU):
                        t = i * TU + k
                        hold(act, turned, t + (1 + TU))
                        for h in range(KC):
                            o = dst[:, ds(t * B + h * NODES, B)]
                            pt = ps[k][:, h * B:(h + 1) * B]
                            if bias is None:
                                up = act.activation(o, pt, ACT.Copy)
                            else:
                                up = act.activation(o, pt, ACT.Identity, bias=bias[:, h:h + 1])
                        up.then_inc(lifted, 1)


def feature_linear(nc, m, src, wname, bias, dst):
    with nc.cleanup_on_exit():
        w = m.sb("w", [P, 2, HID], F32)
        ps = [m.psum(f"ps{i}") for i in range(8)]
        w_in, ready, lifted = m.sem("w_in"), m.sem("ready"), m.sem("lifted")
        with nc.Block() as block:
            @block.sync
            def _(sp):
                sp.dma_start(w[:, :, :], m.a[wname]).then_inc(w_in, 16)
                sp.wait_ge(w_in, 16)

            @block.tensor
            def _(pe):
                pe.wait_ge(w_in, 16)
                with pe.Fori(0, CH) as c:
                    for half, (t0, tn) in enumerate(HALVES):
                        for f in range(4):
                            pe.wait_ge(lifted, c * 8 + (half * 4 + f + 1))
                            for h in range(2):
                                mm = pe.matmul(ps[half * 4 + f][:, 0:tn * B], w[:, h, f * P:(f + 1) * P],
                                               src[:, ds(c * (TU * B) + (h * NODES + t0 * B), tn * B)],
                                               start=(h == 0), stop=(h == 1))
                            mm.then_inc(ready, 1)

            @block.scalar
            def _(act):
                act.sem_inc(lifted, 8)
                with act.Fori(0, CH) as c:
                    for half, (t0, tn) in enumerate(HALVES):
                        for f in range(4):
                            hold(act, ready, c * 8 + (half * 4 + f + 1))
                            act.activation(dst[:, ds(c * (TU * B) + (f * NODES + t0 * B), tn * B)],
                                           ps[half * 4 + f][:, 0:tn * B], ACT.Identity,
                                           bias=bias[:, f:f + 1]).then_inc(lifted, 1)


def batch_stats(nc, m, HT, n, bns):
    with nc.cleanup_on_exit():
        st = m.sb("st", [P, 4, 2 * CH, 6], F32)
        mv = m.sb("mv", [P, 4, 2], F32)
        std = m.sb("std", [P, 4], F32)
        steps, var_ready, std_ready = m.sem("steps"), m.sem("var_ready"), m.sem("std_ready")
        with nc.Block() as block:
            @block.vector
            def _(v):
                c = Chain(v, steps)
                for ch in range(2 * CH):
                    t0, tn = HALVES[ch % 2]
                    at = (ch // 2) * TU * B + t0 * B
                    for f in range(4):
                        last = v.bn_stats(st[:, f, ch, :], HT[:, f * NODES + at:f * NODES + at + tn * B])
                c.link(last)
                for f in range(4):
                    last = v.bn_aggr(mv[:, f, :], st[:, f, :, :].rearrange("p c s -> p (c s)"))
                last.then_inc(var_ready, 1)
                v.wait_ge(std_ready, 1)
                c.link(v.reciprocal(std[:, :], std[:, :]))
                g = m.cols[:, col_at(f"L1_gnn_g{n}"):][:, 0:4]
                be = m.cols[:, col_at(f"L1_gnn_be{n}"):][:, 0:4]
                c.link(v.tensor_tensor(bns[:, 0:4], std[:, :], g, ALU.mult))
                c.link(v.tensor_tensor(std[:, :], mv[:, :, 0], bns[:, 0:4], ALU.mult))
                v.tensor_tensor(bns[:, 4:8], be, std[:, :], ALU.subtract)

            @block.scalar
            def _(act):
                act.wait_ge(var_ready, 1)
                act.activation(std[:, :], mv[:, :, 1], ACT.Sqrt,
                               bias=m.cst[:, C_EPS:C_EPS + 1]).then_inc(std_ready, 1)


def bn_linear(nc, m, HT, bns, wname, wide, dinv, dst):
    with nc.cleanup_on_exit():
        w = m.sb("w", [P, 4, wide], F32)
        st = m.sb("st", [P, TU, 4 * B], F32)
        ps = [m.psum(f"ps{i}") for i in range(TU)]
        w_in, staged, product, taken = m.sem("w_in"), m.sem("staged"), m.sem("product"), m.sem("taken")
        with nc.Block() as block:
            @block.sync
            def _(sp):
                sp.dma_start(w[:, :, :], m.a[wname]).then_inc(w_in, 16)
                sp.wait_ge(w_in, 16)

            @block.scalar
            def _(act):
                with act.Fori(0, NBLK // TU) as i:
                    hold(act, product, i * TU + TU)
                    for k in range(TU):
                        for f in range(4):
                            up = act.activation(st[:, k, f * B:(f + 1) * B],
                                                HT[:, ds((i * TU + k) * B + f * NODES, B)], ACT.Relu,
                                                bias=bns[:, 4 + f:5 + f], scale=bns[:, f:f + 1])
                        up.then_inc(staged, 1)

            @block.tensor
            def _(pe):
                pe.sem_inc(product, TU)
                pe.wait_ge(w_in, 16)
                with pe.Fori(0, NBLK // TU) as i:
                    for k in range(TU):
                        pe.wait_ge(staged, i * TU + (k + 1))
                        pe.wait_ge(taken, i * TU + (k + 1))
                        for f in range(4):
                            mm = pe.matmul(ps[k][:B, 0:wide], st[:, k, f * B:(f + 1) * B], w[:, f, :],
                                           start=(f == 0), stop=(f == 3))
                        mm.then_inc(product, 1)

            @block.vector
            def _(v):
                v.sem_inc(taken, TU)
                with v.Fori(0, NBLK // TU) as i:
                    for k in range(TU):
                        t = i * TU + k
                        v.wait_ge(product, i * TU + (k + 1 + TU))
                        v.tensor_scalar(dst[:, ds(t * wide, wide)], ps[k][:B, 0:wide], dinv[:, ds(t, 1)], None,
                                        ALU.mult).then_inc(taken, 1)




def gat(nc, m, l, XN):
    H = 8 if l == 2 else 4
    C = D // H
    W = D + H
    HB = m.bufa[:B, 0:NBLK * W]
    hb3 = HB.rearrange("p (t w) -> p t w", w=W)
    acc = m.bufb[:B, NT * 8:NT * 8 + NBLK * W]
    acc3 = acc.rearrange("p (t w) -> p t w", w=W)
    alpha = m.bufb[:, 0:NT * H]
    M = m.small[:B, 0:NBLK * H]
    asrc = m.small[:B, 200:200 + NBLK * H]
    self_e = m.small[:B, 400:400 + NBLK * H]
    names = {2: ("L2_gnn_a_src", "L2_gnn_a_dst", "L2_gnn_bias"),
             3: ("L3_gnn_att_src", "L3_gnn_att_dst", "L3_gnn_bias")}[l]
    vec = [m.rows[:B, row_at(n):][:, 0:D].unsqueeze(1).broadcast_to([B, NBLK, D]) for n in names]
    t3 = lambda ap: ap.rearrange("p (t h) -> p t h", h=H)
    token_linear(nc, m, XN, m.a[f"L{l}_gnn_W"], D,
                 lambda v, t, ps: v.tensor_scalar(HB[:, ds(t * W, D)], ps, 1.0, None, ALU.mult))
    with nc.cleanup_on_exit():
        steps, tables = m.sem("steps"), m.sem("tables")
        ready = m.sem("ready")
        tmp = m.bufb[:B, 0:XW]
        with nc.Block() as block:
            @block.vector
            def _(v):
                c = Chain(v, steps)
                tv = tmp.rearrange("p (t w) -> p t w", w=D)
                c.link(v.tensor_tensor(tv, hb3[:, :, 0:D], vec[0], ALU.mult))
                v.tensor_reduce(asrc, tmp.rearrange("p (q c) -> p q c", c=C), AX.X, ALU.add).then_inc(ready, 1)
                v.wait_ge(ready, 1)
                c.link(v.tensor_tensor(tv, hb3[:, :, 0:D], vec[1], ALU.mult))
                c.link(v.tensor_reduce(self_e, tmp.rearrange("p (q c) -> p q c", c=C), AX.X, ALU.add))
                c.link(v.tensor_scalar(hb3[:, :, D:W], t3(self_e), 1.0, None, ALU.mult))
                if l == 2:
                    v.memset(M, -BIG)
                else:
                    c.link(v.tensor_tensor(self_e, self_e, asrc, ALU.add))
                    c.link(v.scalar_tensor_tensor(self_e, self_e, 0.2, self_e, ALU.mult, ALU.max))
                    v.tensor_copy(M, self_e)

            @block.sync
            def _(sp):
                sp.dma_start(m.table.rearrange("(t p) w -> p t w", p=B), hb3[:, :, 0:D]).then_inc(tables, 16)
                sp.wait_ge(ready, 1)
                sp.dma_start(m.tablea[H].rearrange("(t p) w -> p t w", p=B), t3(asrc)).then_inc(tables, 16)
                sp.wait_ge(tables, 32)
    if l == 2:
        edge_scores(nc, m, H, HB, W, alpha)
        edge_maxima(nc, m, H, alpha, M, Arena(m.bufa[:, NBLK * W:]))
    else:
        scores_and_maxima(nc, m, H, HB, W, alpha, M)
    if l == 2:
        with nc.cleanup_on_exit():
            with nc.Block() as block:
                @block.vector
                def _(v):
                    v.memset(acc, 0.0)
    else:
        with nc.cleanup_on_exit():
            steps, shifted, exped = m.sem("steps"), m.sem("shifted"), m.sem("exped")
            with nc.Block() as block:
                @block.vector
                def _(v):
                    v.tensor_tensor(self_e, self_e, M, ALU.subtract).then_inc(shifted, 1)
                    v.wait_ge(exped, 1)
                    v.tensor_scalar(acc3[:, :, D:W], t3(self_e), 1.0, None, ALU.mult)
                    v.tensor_tensor(acc3[:, :, 0:D].rearrange("p t (h c) -> p t h c", c=C),
                                    hb3[:, :, 0:D].rearrange("p t (h c) -> p t h c", c=C),
                                    t3(self_e).unsqueeze(3).broadcast_to([B, NBLK, H, C]), ALU.mult)

                @block.scalar
                def _(act):
                    act.wait_ge(shifted, 1)
                    act.activation(self_e, self_e, ACT.Exp).then_inc(exped, 1)
    edge_messages(nc, m, H, alpha, M, acc, W)
    with nc.cleanup_on_exit():
        steps, squared, rooted = m.sem("steps"), m.sem("squared"), m.sem("rooted")
        inv = M
        o = m.bufa[:B, 0:XW]
        ov = o.rearrange("p (t w) -> p t w", w=D)
        ss = m.small[:B, 700:700 + NBLK]
        with nc.Block() as block:
            @block.vector
            def _(v):
                c = Chain(v, steps)
                c.link(v.tensor_scalar(t3(inv), acc3[:, :, D:W], 1e-10, None, ALU.max))
                c.link(v.reciprocal(inv, inv))
                c.link(v.tensor_tensor(ov.rearrange("p t (h c) -> p t h c", c=C),
                                       acc3[:, :, 0:D].rearrange("p t (h c) -> p t h c", c=C),
                                       t3(inv).unsqueeze(3).broadcast_to([B, NBLK, H, C]), ALU.mult))
                c.link(v.tensor_tensor(ov, ov, vec[2], ALU.add))
                if l == 3:
                    sq = acc[:, 0:XW]
                    c.link(v.tensor_scalar(o, o, 0.0, None, ALU.max))
                    c.link(v.tensor_tensor(sq, o, o, ALU.mult))
                    v.tensor_reduce(ss, sq.rearrange("p (t w) -> p t w", w=D), AX.X, ALU.add).then_inc(squared, 1)
                    v.wait_ge(rooted, 1)
                    c.link(v.tensor_scalar(ss, ss, 1e-12, None, ALU.max))
                    c.link(v.reciprocal(ss, ss))
                    with v.Fori(0, NBLK) as t:
                        x = m.X[:, ds(t * D, D)]
                        v.scalar_tensor_tensor(x, o[:, ds(t * D, D)], ss[:, ds(t, 1)], x, ALU.mult, ALU.add)
                else:
                    v.tensor_tensor(m.X[:, :], m.X[:, :], o, ALU.add)

            @block.scalar
            def _(act):
                if l == 3:
                    act.wait_ge(squared, 1)
                    act.activation(ss, ss, ACT.Sqrt).then_inc(rooted, 1)


def edge_scores(nc, m, H, HB, W, alpha):
    lst = fields(m, "dst")
    C = D // H
    with nc.cleanup_on_exit():
        sb, sem, psum = m.sb, m.sem, m.psum
        space = Arena(m.bufb[:, NT * 8:])
        idx = sb("idx", [P, RT], I32)
        sums, part, asg = (space.take(P, [RT, H]) for _ in range(3))
        onehot, onehotT = space.take(P, [RT, B], BF16), space.take(B, [RT, P])
        identb = space.take(P, [P], BF16)
        rec, recT = space.take(P, [RT, PF]), space.take(EG * PF, [2, P])
        enc = space.take(P, [2 * EG, D])
        ew = space.take(EG * PF, [EG * D])
        pr, pw, pe_ = ([psum(f"{n}{i}") for i in range(2)] for n in ("pr", "pw", "pe"))
        pt = [nc.alloc_psum_tensor(m.name(f"pt{i}"), [P, 1024], BF16) for i in range(2)]
        picked, hot_ready, turned, lifted = sem("picked"), sem("hot_ready"), sem("turned"), sem("lifted")
        spread_done, combined = sem("spread_done"), sem("combined")
        enc_sums, enc_done = sem("enc_sums"), sem("enc_done")
        w_in, made, steps, scored = sem("w_in"), sem("made"), sem("steps"), sem("scored")
        gathered = [sem(f"gathered{g}") for g in range(RING)]
        with nc.Block() as block:
            @block.sync
            def _(sp):
                sp.dma_start(ew, m.a["edge_w"]).then_inc(w_in, 16)
                sp.wait_ge(w_in, 16)

            @block.gpsimd
            def _(pool):
                pool_gathers(pool, m, "dst", idx, picked, scored, 1, m.tablea[H], lambda k: asg[:, k, :], gathered)

            @block.vector
            def _(v):
                v.tensor_scalar(identb, m.cst[:, C_ID:C_ID + P], 1.0, None, ALU.mult).then_inc(made, 1)
                v.sem_inc(combined, 2)
                v.sem_inc(scored, RING)

                def one_hots(i, g):
                    v.wait_ge(turned, i * RING + (g + 1))
                    v.tensor_scalar(rec[:, ring(g), :].rearrange("p c f -> p (c f)").bitcast(I32),
                                    lst[:, ds(i * RT + g * EG, EG), :].rearrange("p c f -> p (c f)").bitcast(I32),
                                    0, None, ALU.bitwise_or)
                    vector_onehots(v, m, lst, i, g, onehot, hot_ready)

                def combine(i, g):
                    s3 = sums[:, ring(g), :]
                    q0 = (g % 2) * EG
                    v.wait_ge(gathered[g], i * (16 * EG) + 16 * EG)
                    for j in range(g * EG, (g + 1) * EG):
                        q = j % (2 * EG)
                        tgt = pw[j % 2]
                        v.wait_ge(spread_done, i * RT + (j + 1))
                        if j % 2 == 0:
                            v.wait_ge(enc_done, i * (RT // 2) + (j // 2 + 3))
                        v.tensor_tensor(enc[:, q, :], enc[:, q, :], tgt[:, 0:D], ALU.mult)
                        v.scalar_tensor_tensor(sums[:, j, :], asg[:, j, :], lst[:, ds(i * RT + j, 1), 6],
                                               tgt[:, D:W], ALU.add, ALU.add).then_inc(combined, 1)
                    v.wait_ge(combined, i * RT + (g * EG + EG + 2))
                    v.tensor_reduce(part[:, ring(g), :], enc[:, q0:q0 + EG, :].rearrange("p k (h c) -> p k h c", c=C),
                                    AX.X, ALU.add).then_inc(steps, 1)
                    v.wait_ge(steps, i * (2 * RING) + (2 * g + 1))
                    v.tensor_tensor(s3, s3, part[:, ring(g), :], ALU.add).then_inc(steps, 1)
                    v.wait_ge(steps, i * (2 * RING) + (2 * g + 2))
                    sv = s3.rearrange("p c h -> p (c h)")
                    v.scalar_tensor_tensor(alpha[:, ds(i * (RT * H) + g * EG * H, EG * H)], sv, 0.2, sv, ALU.mult,
                                           ALU.max).then_inc(scored, 1)

                over_groups(v, (one_hots, 3), (combine, 0))

            @block.tensor
            def _(pe):
                pe.sem_inc(turned, RING)
                pe.sem_inc(enc_sums, 4)
                pe.wait_ge(w_in, 16)
                pe.wait_ge(made, 1)

                def transposes(i, g):
                    pe.wait_ge(hot_ready, i * RING + (g + 1))
                    pe.wait_ge(lifted, i * RING + (g + 1))
                    for q in range(EG):
                        pe.transpose(pt[g % 2][:B, q * P:(q + 1) * P], onehot[:, g * EG + q, :], identb)
                    pe.transpose(pr[g % 2][:EG * PF, 0:P], rec[:, ring(g), :].rearrange("p c f -> p (c f)"),
                                 m.cst[:, C_ID:C_ID + P]).then_inc(turned, 1)

                def encodings(i, g):
                    pe.wait_ge(lifted, i * RING + (g + 3))
                    for j in range(g * EG, (g + 1) * EG, 2):
                        pe.wait_ge(enc_done, i * (RT // 2) + (j // 2 + 1))
                        q = j % EG
                        pe.matmul(pe_[(j // 2) % 2][:, :], recT[:, g % 2, :], ew[:, q * D:(q + 2) * D],
                                  start=True, stop=True).then_inc(enc_sums, 1)

                def get_blocks(i, g):
                    blocks[:] = blocks_of(pe, m, "dst", i, g)

                def spreads(i, g):
                    pe.wait_ge(lifted, i * RING + (g + 3))
                    for j in range(g * EG, (g + 1) * EG):
                        hold(pe, combined, i * RT + (j + 1))
                        pe.matmul(pw[j % 2][:, 0:W], onehotT[:, j, :], HB[:, ds(blocks[j % EG] * W, W)], start=True,
                                  stop=True).then_inc(spread_done, 1)

                blocks = []
                over_groups(pe, (get_blocks, 0), (transposes, 2), (encodings, 1), (spreads, 0))

            @block.scalar
            def _(act):
                act.sem_inc(lifted, 2)
                act.sem_inc(enc_done, 2)

                def lift(i, g):
                    act.wait_ge(turned, i * RING + (g + 1 + RING))
                    act.wait_ge(enc_sums, i * (RT // 2) + (g * 2 + 2))
                    act.activation(recT[:, g % 2, :], pr[g % 2][:EG * PF, 0:P], ACT.Copy)
                    act.activation(onehotT[:, ring(g), :].rearrange("p c e -> p (c e)"), pt[g % 2][:B, 0:EG * P],
                                   ACT.Copy).then_inc(lifted, 1)

                def encode(i, g):
                    for h in range(EG // 2):
                        q = (g % 2) * EG + 2 * h
                        act.wait_ge(enc_sums, i * (RT // 2) + (g * 2 + h + 5))
                        act.wait_ge(scored, i * RING + (g + 3))
                        act.activation(enc[:, q:q + 2, :].rearrange("p c e -> p (c e)"), pe_[h % 2][:, :],
                                       ACT.Relu).then_inc(enc_done, 1)

                over_groups(act, (lift, 1), (encode, 0))


class Maxima:

    def __init__(self, m, H, alpha, M, space, tiles):
        self.m, self.H, self.alpha, self.M, self.NB = m, H, alpha, M, tiles
        self.HG, self.K = H // 4, 2 * H + 1
        K = self.K
        self.dist, self.onehot = space.take(P, [2 * EG, B], BF16), space.take(P, [RT, B], BF16)
        self.al, self.alT = space.take(P, [RT, K + 1], BF16), space.take(K, [RT, P], BF16)
        self.identb, self.bigi = space.take(P, [P], BF16), space.take(P, [4, P], BF16)
        self.sel, self.top = space.take(K, [H, B], BF16), space.take(B, [RT, H])
        self.pt = [m.nc.alloc_psum_tensor(m.name(f"pal{i}"), [P, 1024], BF16) for i in range(2)]
        self.pm = [[m.psum(f"pm{i}{g}") for g in range(self.HG)] for i in range(tiles)]
        self.made, self.steps = m.sem("made"), m.sem("steps")
        self.split, self.al_ready = m.sem("split"), m.sem("al_ready")
        self.al_turned, self.al_lifted = m.sem("al_turned"), m.sem("al_lifted")
        self.measured, self.hot_ready = m.sem("measured"), m.sem("hot_ready")
        self.masked, self.reduced, self.raised = m.sem("masked"), m.sem("reduced"), m.sem("raised")

    def vector_start(self, v):
        m, H, K = self.m, self.H, self.K
        c = Chain(v, self.steps)
        v.tensor_scalar(self.bigi, m.cst[:, C_ID:C_ID + P].unsqueeze(1).broadcast_to([P, 4, P]), BIG, None, ALU.mult)
        v.tensor_scalar(self.identb, m.cst[:, C_ID:C_ID + P], 1.0, None, ALU.mult)
        v.memset(self.al, -BIG)
        s = m.small[:K, 1100:1100 + H]
        c.link(v.tensor_tensor(s, m.cst[:K, C_ID:C_ID + H], m.cst[:K, C_ID + H:C_ID + 2 * H], ALU.add))
        c.link(v.tensor_tensor(s, s, m.cst[:K, C_ID + 2 * H:C_ID + K].broadcast_to([K, H]), ALU.add))
        c.link(v.tensor_scalar(self.sel, s.unsqueeze(2).broadcast_to([K, H, B]), 1.0, None, ALU.mult))
        v.sem_inc(self.made, 1)
        v.sem_inc(self.reduced, self.NB)
        v.sem_inc(self.raised, 1)

    def parts(self, v, i, g):
        H = self.H
        a = self.alpha[:, ds(i * (RT * H) + g * EG * H, EG * H)].rearrange("p (c h) -> p c h", h=H)
        v.wait_ge(self.al_turned, i * RING + (g + 1))
        v.tensor_scalar(self.al[:, ring(g), 0:H], a, 1.0, None, ALU.mult).then_inc(self.split, 1)
        v.wait_ge(self.split, i * RING + (g + 1))
        v.tensor_tensor(self.al[:, ring(g), H:2 * H], a, self.al[:, ring(g), 0:H],
                        ALU.subtract).then_inc(self.al_ready, 1)

    def reduce(self, v, i, g, tiles=range(EG)):
        if tiles[0] == 0:
            self.blocks = blocks_of(v, self.m, "dst", i, g)
        for q in tiles:
            j = g * EG + q
            v.wait_ge(self.masked, i * RT + (j + 1 + RT))
            for h in range(self.HG):
                r = v.tensor_reduce(self.top[:, j, 4 * h:4 * h + 4],
                                    self.pm[j % self.NB][h][:B, :].rearrange("p (h e) -> p h e", e=P), AX.X, ALU.max)
            r.then_inc(self.reduced, 1)
            if q > 0:
                self.raise_max(v, i, j - 1)
            if q == EG - 1:
                self.raise_max(v, i, j)

    def raise_max(self, v, i, j):
        part = self.M[:, ds(self.blocks[j % EG] * self.H, self.H)]
        v.wait_ge(self.reduced, i * RT + (j + 1 + self.NB))
        v.wait_ge(self.raised, i * RT + (j + 1))
        v.tensor_tensor(part, part, self.top[:, j, :], ALU.max).then_inc(self.raised, 1)

    def tensor_start(self, pe):
        pe.sem_inc(self.masked, RT)
        pe.sem_inc(self.al_turned, RING)
        pe.wait_ge(self.made, 1)

    def al_transposes(self, pe, i, g):
        pe.wait_ge(self.al_ready, i * RING + (g + 1))
        pe.wait_ge(self.al_lifted, i * RING + (g + 1))
        for q in range(EG):
            tr = pe.transpose(self.pt[g % 2][:self.K, q * P:(q + 1) * P], self.al[:, g * EG + q, 0:self.K],
                              self.identb)
        tr.then_inc(self.al_turned, 1)

    def masks(self, pe, i, g, tiles=range(EG)):
        pe.wait_ge(self.hot_ready, i * RING + (g + 3))
        pe.wait_ge(self.al_lifted, i * RING + (g + 3))
        for j in (g * EG + q for q in tiles):
            pe.wait_ge(self.reduced, i * RT + (j + 1))
            for h in range(self.HG):
                o = self.pm[j % self.NB][h][:B, :]
                pe.matmul(o, self.onehot[:, j, :], self.bigi.rearrange("p a b -> p (a b)"), start=True,
                          stop=False, skip_group_check=True)
                for q in range(4):
                    mm = pe.matmul(o[:, q * P:(q + 1) * P], self.sel[:, 4 * h + q, :], self.alT[:, j, :],
                                   start=False, stop=(q == 3), skip_group_check=True)
            mm.then_inc(self.masked, 1)

    def scalar_start(self, act):
        act.sem_inc(self.al_lifted, 2)
        act.sem_inc(self.hot_ready, 2)

    def one_hots(self, act, i, g):
        hold(act, self.masked, i * RT + (g * EG + EG))
        act_onehots(act, self.m, fields(self.m, "dst"), i, g, self.dist, self.onehot, self.measured, self.hot_ready)

    def lift_al(self, act, i, g):
        act.wait_ge(self.al_turned, i * RING + (g + 1 + RING))
        act.wait_ge(self.masked, i * RT + (g * EG + EG))
        act.activation(self.alT[:, ring(g), :].rearrange("p c e -> p (c e)"), self.pt[g % 2][:self.K, 0:EG * P],
                       ACT.Copy).then_inc(self.al_lifted, 1)


def edge_maxima(nc, m, H, alpha, M, space):
    with nc.cleanup_on_exit():
        x = Maxima(m, H, alpha, M, space, 4 // (H // 4))
        with nc.Block() as block:
            @block.vector
            def _(v):
                x.vector_start(v)
                over_groups(v, (lambda i, g: x.parts(v, i, g), 2), (lambda i, g: x.reduce(v, i, g), 0))

            @block.tensor
            def _(pe):
                x.tensor_start(pe)
                over_groups(pe, (lambda i, g: x.al_transposes(pe, i, g), 1), (lambda i, g: x.masks(pe, i, g), 0))

            @block.scalar
            def _(act):
                x.scalar_start(act)
                over_groups(act, (lambda i, g: x.one_hots(act, i, g), 1), (lambda i, g: x.lift_al(act, i, g), 0))


def scores_and_maxima(nc, m, H, HB, W, alpha, M):
    lst = fields(m, "dst")
    with nc.cleanup_on_exit():
        sem = m.sem
        space = Arena(m.bufb[:, NT * 8:])
        x = Maxima(m, H, alpha, M, Arena(m.bufa[:, NBLK * W:]), 2)
        idx = m.sb("idx", [P, RT], I32)
        sums, asg = space.take(P, [RT, H]), space.take(P, [RT, H])
        onehotT = space.take(B, [RT, P])
        pt = [nc.alloc_psum_tensor(m.name(f"pt{i}"), [P, 1024], BF16) for i in range(2)]
        pw = [m.psum(f"pw{i}") for i in range(2)]
        picked, turned, lifted, spread_done, combined, padded, scored = (
            sem(n) for n in ("picked", "turned", "lifted", "spread_done", "combined", "padded", "scored"))
        gathered = [sem(f"gathered{g}") for g in range(RING)]
        with nc.Block() as block:
            @block.gpsimd
            def _(pool):
                pool_gathers(pool, m, "dst", idx, picked, scored, 1, m.tablea[H], lambda k: asg[:, k, :], gathered)

            @block.vector
            def _(v):
                x.vector_start(v)
                v.sem_inc(combined, 2)
                v.sem_inc(scored, RING)

                def add_parts(i, g):
                    v.wait_ge(gathered[g], i * (16 * EG) + 16 * EG)
                    v.wait_ge(spread_done, i * RING + (g + 1 + RING))
                    v.tensor_tensor(sums[:, ring(g), :], asg[:, ring(g), :],
                                    pw[g % 2][:, 0:EG * H].rearrange("p (k h) -> p k h", h=H),
                                    ALU.add).then_inc(combined, 1)

                def pad(i, g):
                    v.wait_ge(combined, i * RING + (g + 3))
                    for j in range(g * EG, (g + 1) * EG):
                        o = v.tensor_scalar(sums[:, j, :], sums[:, j, :], lst[:, ds(i * RT + j, 1), 6], None, ALU.add)
                    o.then_inc(padded, 1)

                def leaky(i, g):
                    v.wait_ge(padded, i * RING + (g + 1))
                    sv = sums[:, ring(g), :].rearrange("p c h -> p (c h)")
                    v.scalar_tensor_tensor(alpha[:, ds(i * (RT * H) + g * EG * H, EG * H)], sv, 0.2, sv, ALU.mult,
                                           ALU.max).then_inc(scored, 1)

                def split(i, g):
                    v.wait_ge(scored, i * RING + (g + 1 + RING))
                    x.parts(v, i, g)

                def reduce(q):
                    return lambda i, g: x.reduce(v, i, g, [q])

                over_groups(v, (reduce(0), 0), (add_parts, 2), (reduce(1), 0), (pad, 2),
                            (reduce(2), 0), (leaky, 2), (reduce(3), 0), (split, 2))

            @block.tensor
            def _(pe):
                x.tensor_start(pe)
                pe.sem_inc(spread_done, RING)

                def transposes(i, g):
                    pe.wait_ge(x.hot_ready, i * RING + (g + 3))
                    pe.wait_ge(lifted, i * RING + (g + 1))
                    for q in range(EG):
                        tr = pe.transpose(pt[g % 2][:B, q * P:(q + 1) * P], x.onehot[:, g * EG + q, :], x.identb)
                    tr.then_inc(turned, 1)

                def spreads(i, g):
                    blocks = blocks_of(pe, m, "dst", i, g)
                    pe.wait_ge(lifted, i * RING + (g + 3))
                    hold(pe, combined, i * RING + (g + 1))
                    for q in range(EG):
                        mm = pe.matmul(pw[g % 2][:, q * H:(q + 1) * H], onehotT[:, g * EG + q, :],
                                       HB[:, ds(blocks[q] * W + D, H)], start=True, stop=True)
                    mm.then_inc(spread_done, 1)

                over_groups(pe, (spreads, 2), (lambda i, g: x.al_transposes(pe, i, g), 1),
                            (lambda i, g: x.masks(pe, i, g, range(0, 2)), 0), (transposes, 3),
                            (lambda i, g: x.masks(pe, i, g, range(2, EG)), 0))

            @block.scalar
            def _(act):
                x.scalar_start(act)
                act.sem_inc(lifted, 2)

                def lift(i, g):
                    act.wait_ge(turned, i * RING + (g + 1))
                    act.wait_ge(spread_done, i * RING + (g + 1))
                    act.activation(onehotT[:, ring(g), :].rearrange("p c e -> p (c e)"), pt[g % 2][:B, 0:EG * P],
                                   ACT.Copy).then_inc(lifted, 1)

                over_groups(act, (lambda i, g: x.lift_al(act, i, g), 1), (lift, 3),
                            (lambda i, g: x.one_hots(act, i, g), 4))


def edge_messages(nc, m, H, alpha, M, acc, W):
    lst = fields(m, "dst")
    C = D // H
    with nc.cleanup_on_exit():
        sem, psum = m.sem, m.psum
        space = Arena(m.bufa)
        idx = m.sb("idx", [P, RT], I32)
        rows, onehot, onehotT = space.take(P, [RT, D]), space.take(P, [RT, B]), space.take(B, [RT, P])
        wt, msg = space.take(P, [RT, H]), space.take(P, [2 * EG, W])
        pt, pm = ([psum(f"{n}{i}") for i in range(2)] for n in ("pt", "pm"))
        pa = [psum(f"pa{i}") for i in range(EG)]
        picked, hot_ready, turned, lifted = sem("picked"), sem("hot_ready"), sem("turned"), sem("lifted")
        spread_done, shifted, exped = sem("spread_done"), sem("shifted"), sem("exped")
        msg_ready = sem("msg_ready")
        summed, added = sem("summed"), sem("added")
        gathered = [sem(f"gathered{g}") for g in range(RING)]
        with nc.Block() as block:
            @block.gpsimd
            def _(pool):
                pool_gathers(pool, m, "dst", idx, picked, msg_ready, 1, m.table, lambda k: rows[:, k, :], gathered)

            @block.vector
            def _(v):
                v.sem_inc(added, EG)
                v.sem_inc(shifted, 2)
                v.sem_inc(msg_ready, RING)

                def one_hots(i, g):
                    v.wait_ge(summed, i * RT + (g * EG + EG))
                    vector_onehots(v, m, lst, i, g, onehot, hot_ready)

                def shift(i, g):
                    v.wait_ge(spread_done, i * RING + (g + 1 + RING))
                    v.tensor_tensor(wt[:, ring(g), :].rearrange("p c h -> p (c h)"),
                                    alpha[:, ds(i * (RT * H) + g * EG * H, EG * H)], pm[g % 2][:, 0:EG * H],
                                    ALU.subtract).then_inc(shifted, 1)

                def messages(i, g):
                    q0 = (g % 2) * EG
                    v.wait_ge(exped, i * RING + (g + 1))
                    v.wait_ge(gathered[g], i * (16 * EG) + 16 * EG)
                    v.wait_ge(summed, i * RT + (g * EG + EG + RT // 2))
                    v.tensor_scalar(msg[:, q0:q0 + EG, D:W], wt[:, ring(g), :], 1.0, None, ALU.mult)
                    v.tensor_tensor(msg[:, q0:q0 + EG, 0:D].rearrange("p k (h c) -> p k h c", c=C),
                                    rows[:, ring(g), :].rearrange("p k (h c) -> p k h c", c=C),
                                    wt[:, ring(g), :].unsqueeze(3).broadcast_to([P, EG, H, C]),
                                    ALU.mult).then_inc(msg_ready, 1)

                def add(i, g):
                    blocks = blocks_of(v, m, "dst", i, g)
                    for j in range(g * EG, (g + 1) * EG):
                        part = acc[:, ds(blocks[j % EG] * W, W)]
                        v.wait_ge(summed, i * RT + (j + 1 + RT))
                        v.wait_ge(added, i * RT + (j + EG))
                        v.tensor_tensor(part, part, pa[j % EG][:B, 0:W], ALU.add).then_inc(added, 1)

                over_groups(v, (one_hots, 3), (messages, 1), (add, 0), (shift, 2))

            @block.tensor
            def _(pe):
                pe.sem_inc(spread_done, RING)
                pe.sem_inc(summed, RT)

                def transposes(i, g):
                    pe.wait_ge(hot_ready, i * RING + (g + 1))
                    pe.wait_ge(lifted, i * RING + (g + 1))
                    for q in range(EG):
                        tr = pe.transpose(pt[g % 2][:B, q * P:(q + 1) * P], onehot[:, g * EG + q, :],
                                          m.cst[:, C_ID:C_ID + P])
                    tr.then_inc(turned, 1)

                def spreads(i, g):
                    blocks = blocks_of(pe, m, "dst", i, g)
                    pe.wait_ge(lifted, i * RING + (g + 3))
                    hold(pe, shifted, i * RING + (g + 1))
                    for q in range(EG):
                        mm = pe.matmul(pm[g % 2][:, q * H:(q + 1) * H], onehotT[:, g * EG + q, :],
                                       M[:, ds(blocks[q] * H, H)], start=True, stop=True)
                    mm.then_inc(spread_done, 1)

                def sums(i, g):
                    pe.wait_ge(msg_ready, i * RING + (g + 1 + RING))
                    for j in range(g * EG, (g + 1) * EG):
                        pe.wait_ge(added, i * RT + (j + 1))
                        pe.matmul(pa[j % EG][:B, 0:W], onehot[:, j, :], msg[:, j % (2 * EG), :], start=True,
                                  stop=True).then_inc(summed, 1)

                over_groups(pe, (sums, 0), (spreads, 2), (transposes, 3))

            @block.scalar
            def _(act):
                act.sem_inc(lifted, 2)

                def lift(i, g):
                    act.wait_ge(turned, i * RING + (g + 1))
                    act.wait_ge(spread_done, i * RING + (g + 1))
                    act.activation(onehotT[:, ring(g), :].rearrange("p c e -> p (c e)"), pt[g % 2][:B, :],
                                   ACT.Copy).then_inc(lifted, 1)

                def exps(i, g):
                    act.wait_ge(shifted, i * RING + (g + 3))
                    w = wt[:, ring(g), :]
                    act.activation(w, w, ACT.Exp).then_inc(exped, 1)

                over_groups(act, (exps, 0), (lift, 1))


def spread_cols(v, fc):
    v = np.asarray(v).reshape(-1, fc, P)
    return np.ascontiguousarray(v.transpose(2, 0, 1).reshape(P, -1))


def consts():
    c = np.zeros((P, C_END), np.float32)
    c[:, C_ID:C_ID + P] = np.eye(P)
    c[:, C_IOTA:C_IOTA + P] = np.arange(P)
    r = np.arange(B)
    c[:B, C_STRICT:C_STRICT + B] = r[:, None] < r[None]
    c[:B, C_UPTO:C_UPTO + B] = r[:, None] <= r[None]
    c[:, C_ONE:C_ONE + P] = 1
    c[:, C_TILE:C_TILE + NT] = np.arange(NT)
    c[:B, C_SPARE:C_SPARE + NBLK] = SPARE + np.arange(NBLK)[None] * B + r[:, None]
    c[:, C_STEP:C_STEP + 7] = UR * np.arange(7)
    c[:, C_EPS] = LN_EPS
    c[:, C_EPS + 1] = FBN_EPS
    return c


def kernel(**inp):
    import concourse.bacc as bacc
    from concourse.bass_utils import run_bass_kernel_spmd

    v = {k: np.asarray(x) for k, x in inp.items()}
    arr = {"consts": consts(), "x": v["x"]}
    arr["src"] = v["src"].reshape(B, EC)
    arr["dst"] = v["dst"].reshape(B, EC)
    arr["attr"] = v["edge_attr_3"].reshape(B, EC * 3)
    flat = np.concatenate([v[n].reshape(-1) for n in ROWS + GATEB])
    arr["rows"] = np.broadcast_to(flat, (P, ROWN))
    fc = {64: 8, 32: 4, 16: 2, 4: 4}
    arr["cols"] = np.concatenate([spread_cols(v[n], fc[w]) for n, w in COLS], axis=1)

    def kmajor(w):
        w = w.reshape(w.shape[:-2] + (w.shape[-2] // P, P, w.shape[-1]))
        return np.swapaxes(w, -3, -2)

    for l in range(2):
        arr[f"L0_gnn_W{l}"] = kmajor(v[f"L0_gnn_W{l}"].T)
    for n in ("L1_gnn_W1", "L1_gnn_W2", "L1_gnn_W3"):
        arr[n] = kmajor(v[n])
    arr["L2_gnn_W"] = kmajor(v["L2_gnn_W"].T)
    arr["L3_gnn_W"] = kmajor(v["L3_gnn_W"])
    ew = np.zeros((EG, PF, EG, D), np.float32)
    for q in range(EG):
        ew[q, 2:5, q] = v["L2_gnn_edge_W"].T
        ew[q, 5, q] = v["L2_gnn_edge_b"]
    arr["edge_w"] = ew.reshape(EG * PF, EG * D)
    for n in GATES:
        arr[n] = kmajor(v[n])
    for n in B2S:
        arr[n] = v[n]
    arr["L0_ffn_W1"], arr["L0_ffn_W2"] = kmajor(v["L0_ffn_w1"]), kmajor(v["L0_ffn_w2"])
    for l in (1, 3):
        arr[f"L{l}_ffn_W1"], arr[f"L{l}_ffn_W2"] = kmajor(v[f"L{l}_ffn_W1"]), kmajor(v[f"L{l}_ffn_W2"])
    arr["L2_ffn_W1"], arr["L2_ffn_Wm"], arr["L2_ffn_W2"] = (kmajor(v[f"L2_ffn_{n}"]) for n in ("W1", "W2", "Wo"))

    nc = bacc.Bacc("TRN2", target_bir_lowering=False, num_devices=1)
    arr = {k: np.ascontiguousarray(x) for k, x in arr.items()}
    a = {k: nc.dram_tensor(f"in_{k}", x.shape, mybir.dt.from_np(x.dtype), kind="ExternalInput").ap()
         for k, x in arr.items()}
    out = nc.dram_tensor("out", (NODES, D), F32, kind="ExternalOutput").ap()
    build(nc, a, out)
    r = run_bass_kernel_spmd(nc, [{f"in_{k}": x for k, x in arr.items()}], core_ids=[0])
    return r.results[0]["out"]
```
